# Optimizing a Trainium2 kernel written in Bass

```python
import numpy as np
import jax
import jax.numpy as jnp

def _softmax(x, axis=-1):
    return jax.nn.softmax(x, axis=axis)

def _gelu(x):
    return jax.nn.gelu(x, approximate=True)

def _silu(x):
    return jax.nn.silu(x)

def _sigmoid(x):
    return jax.nn.sigmoid(x)

def _layernorm(x, axis=-1, eps=1e-05):
    m = jnp.mean(x, axis=axis, keepdims=True)
    v = jnp.var(x, axis=axis, keepdims=True)
    return (x - m) / jnp.sqrt(v + eps)

def _scatter_add(tgt, idx, src, axis=0):
    return tgt.at[idx].add(src)

def _segment_sum(src, seg, n):
    return jax.ops.segment_sum(src, seg, n)
kernel_name = 'mk_xattn_ffn_d2_seqx_r4_fed4ad'

def setup_inputs(seed: int=0):
    np.random.seed(seed)
    _w = jnp.asarray

    def _rec_inputs():
        import jax
        import jax.numpy as jnp
        _rk = jax.random.key(seed)
        x = 7.22e-05 + 1 * jax.random.normal(jax.random.fold_in(_rk, 1), (8, 112, 256), jnp.float32)
        _lenS = 112 - jax.random.randint(jax.random.fold_in(_rk, 7), (8,), 0, max(1, 112 // 4) + 1, jnp.int32)
        _lenS2 = 375 - jax.random.randint(jax.random.fold_in(_rk, 8), (8,), 0, max(1, 375 // 4) + 1, jnp.int32)
        _ctx_1024P = jax.random.normal(jax.random.fold_in(_rk, 11), (8, 16, 256), jnp.float32)
        _ctx_1024c = jax.random.dirichlet(jax.random.fold_in(_rk, 511), 0.3 * jnp.ones((16,), jnp.float32), (8, 375))
        _ctx_1024t = jnp.einsum('bsk,bkd->bsd', _ctx_1024c, _ctx_1024P)
        _ctx_1024t = _ctx_1024t * jax.lax.rsqrt(jnp.mean(jnp.square(_ctx_1024t)) + 1e-12) * 0.953939
        ctx_1024 = 4.13588e-05 + 0.999923 * (_ctx_1024t + 0.3 * jax.random.normal(jax.random.fold_in(_rk, 611), (8, 375, 256), jnp.float32))
        _validS = jnp.arange(112)[None, :] < _lenS[:, None]
        _validS2 = jnp.arange(375)[None, :] < _lenS2[:, None]
        _causal = jnp.tril(jnp.ones((112, 112), dtype=bool))
        mask_BxS2_ff1 = jnp.where(jnp.ones((8, 375), dtype=bool), 1.0, 0.0).astype(jnp.float32)
        return (x, ctx_1024, mask_BxS2_ff1)
    x, ctx_1024, mask_BxS2_ff1 = _rec_inputs()

    def _L0_xattn_setup():
        import jax, jax.numpy as jnp
        import numpy as np
        HEADS = 16
        D_MODEL = 256
        D_K = D_MODEL // HEADS
        key = jax.random.key(seed)
        ks = jax.random.split(key, 11)
        B, S, D = (4, 512, D_MODEL)
        q = jax.random.normal(ks[0], (B, S, D), dtype=jnp.float32)
        k = jax.random.normal(ks[1], (B, S, D), dtype=jnp.float32)
        v = jax.random.normal(ks[2], (B, S, D), dtype=jnp.float32)
        s = 1.0 / np.sqrt(D)
        Wq = jax.random.normal(ks[3], (D, D), dtype=jnp.float32) * s
        bq = jax.random.normal(ks[4], (D,), dtype=jnp.float32) * 0.01
        Wk = jax.random.normal(ks[5], (D, D), dtype=jnp.float32) * s
        bk = jax.random.normal(ks[6], (D,), dtype=jnp.float32) * 0.01
        Wv = jax.random.normal(ks[7], (D, D), dtype=jnp.float32) * s
        bv = jax.random.normal(ks[8], (D,), dtype=jnp.float32) * 0.01
        Wo = jax.random.normal(ks[9], (D, D), dtype=jnp.float32) * s
        bo = jax.random.normal(ks[10], (D,), dtype=jnp.float32) * 0.01
        return {'q': q, 'k': k, 'v': v, 'Wq': Wq, 'bq': bq, 'Wk': Wk, 'bk': bk, 'Wv': Wv, 'bv': bv, 'Wo': Wo, 'bo': bo}
    _L0_xattn_all = _L0_xattn_setup()
    _L0_xattn_in = {k: v for k, v in _L0_xattn_all.items() if k in ('Wq', 'bq', 'Wk', 'bk', 'Wv', 'bv', 'Wo', 'bo')}
    del _L0_xattn_all

    def _L0_ffn_setup():
        import jax, jax.numpy as jnp
        import numpy as np

        def _moe_forward(x, Wg, W1, b1, W2, b2):
            B, S, H = x.shape
            E = Wg.shape[1]
            tokens = x.reshape(-1, H)
            T = tokens.shape[0]
            C = -(-T // E)
            logits = tokens @ Wg
            gates = jax.nn.softmax(logits, axis=-1)
            idx = jnp.argmax(gates, axis=1)
            mask1 = jax.nn.one_hot(idx, E, dtype=gates.dtype)
            locations1 = jnp.cumsum(mask1, axis=0) - 1.0
            mask1 = mask1 * (locations1 < C).astype(gates.dtype)
            loc_s = jnp.sum(locations1 * mask1, axis=1).astype(jnp.int32)
            gates1 = jnp.sum(gates * mask1, axis=1)
            loc_oh = jax.nn.one_hot(loc_s, C, dtype=gates.dtype)
            dispatch = mask1[:, :, None] * loc_oh[:, None, :]
            combine = gates1[:, None, None] * dispatch
            expert_in = jnp.einsum('tec,th->ech', dispatch, tokens)
            hidden = jax.nn.relu(jnp.einsum('ech,ehf->ecf', expert_in, W1) + b1[:, None, :])
            expert_out = jnp.einsum('ecf,efh->ech', hidden, W2) + b2[:, None, :]
            out = jnp.einsum('tec,ech->th', combine, expert_out)
            return out.reshape(B, S, H)
        key = jax.random.key(seed)
        ks = jax.random.split(key, 6)
        B, S, H, F, E = (4, 512, 256, 1024, 8)
        x = jax.random.normal(ks[0], (B, S, H), dtype=jnp.float32)
        Wg = jax.random.normal(ks[1], (H, E), dtype=jnp.float32) * (1.0 / np.sqrt(H))
        W1 = jax.random.normal(ks[2], (E, H, F), dtype=jnp.float32) * (1.0 / np.sqrt(H))
        b1 = jnp.zeros((E, F), dtype=jnp.float32)
        W2 = jax.random.normal(ks[3], (E, F, H), dtype=jnp.float32) * (1.0 / np.sqrt(F))
        b2 = jnp.zeros((E, H), dtype=jnp.float32)
        return {'x': x, 'Wg': Wg, 'W1': W1, 'b1': b1, 'W2': W2, 'b2': b2}
    _L0_ffn_all = _L0_ffn_setup()
    _L0_ffn_in = {k: v for k, v in _L0_ffn_all.items() if k in ('Wg', 'W1', 'b1', 'W2', 'b2')}
    del _L0_ffn_all

    def _L1_xattn_setup():
        import jax, jax.numpy as jnp
        import numpy as np
        import math
        B, L, D, NUM_HEADS = (4, 512, 256, 16)
        HEAD_SIZE = D // NUM_HEADS
        key = jax.random.key(seed)
        ks = jax.random.split(key, 9)
        s = 1.0 / math.sqrt(D)
        return {'query_states': jax.random.normal(ks[0], (B, L, D), jnp.float32), 'key_states': jax.random.normal(ks[1], (B, L, D), jnp.float32), 'value_states': jax.random.normal(ks[2], (B, L, D), jnp.float32), 'attention_mask': jnp.ones((B, L), jnp.float32), 'Wq': jax.random.normal(ks[3], (D, D), jnp.float32) * s, 'bq': jnp.zeros((D,), jnp.float32), 'Wk': jax.random.normal(ks[4], (D, D), jnp.float32) * s, 'bk': jnp.zeros((D,), jnp.float32), 'Wv': jax.random.normal(ks[5], (D, D), jnp.float32) * s, 'bv': jnp.zeros((D,), jnp.float32)}
    _L1_xattn_all = _L1_xattn_setup()
    _L1_xattn_in = {k: v for k, v in _L1_xattn_all.items() if k in ('Wq', 'bq', 'Wk', 'bk', 'Wv', 'bv')}
    del _L1_xattn_all

    def _L1_ffn_setup():
        import jax, jax.numpy as jnp
        import numpy as np
        LORA_DIM = 16
        LORA_TOKEN_INDEX = 1
        B, S, D, H = (4, 512, 256, 1024)
        key = jax.random.key(seed)
        ks = jax.random.split(key, 6)
        x = jax.random.normal(ks[0], (B, S, D), dtype=jnp.float32)
        W1 = jax.random.normal(ks[1], (H, D), dtype=jnp.float32) * 0.02
        b1 = jnp.zeros((H,), dtype=jnp.float32)
        W2 = jax.random.normal(ks[2], (D, H), dtype=jnp.float32) * 0.02
        b2 = jnp.zeros((D,), dtype=jnp.float32)
        scale = jnp.asarray(0.001, dtype=jnp.float32)
        return {'x': x, 'W1': W1, 'b1': b1, 'W2': W2, 'b2': b2, 'scale': scale}
    _L1_ffn_all = _L1_ffn_setup()
    _L1_ffn_in = {k: v for k, v in _L1_ffn_all.items() if k in ('W1', 'b1', 'W2', 'b2', 'scale')}
    del _L1_ffn_all
    return {'x': x, 'ctx_1024': ctx_1024, 'mask_BxS2_ff1': mask_BxS2_ff1, 'L0_xattn_Wq': _L0_xattn_in['Wq'], 'L0_xattn_bq': _L0_xattn_in['bq'], 'L0_xattn_Wk': _L0_xattn_in['Wk'], 'L0_xattn_bk': _L0_xattn_in['bk'], 'L0_xattn_Wv': _L0_xattn_in['Wv'], 'L0_xattn_bv': _L0_xattn_in['bv'], 'L0_xattn_Wo': _L0_xattn_in['Wo'], 'L0_xattn_bo': _L0_xattn_in['bo'], 'L0_ffn_Wg': _L0_ffn_in['Wg'], 'L0_ffn_W1': _L0_ffn_in['W1'], 'L0_ffn_b1': _L0_ffn_in['b1'], 'L0_ffn_W2': _L0_ffn_in['W2'], 'L0_ffn_b2': _L0_ffn_in['b2'], 'L1_xattn_Wq': _L1_xattn_in['Wq'], 'L1_xattn_bq': _L1_xattn_in['bq'], 'L1_xattn_Wk': _L1_xattn_in['Wk'], 'L1_xattn_bk': _L1_xattn_in['bk'], 'L1_xattn_Wv': _L1_xattn_in['Wv'], 'L1_xattn_bv': _L1_xattn_in['bv'], 'L1_ffn_W1': _L1_ffn_in['W1'], 'L1_ffn_b1': _L1_ffn_in['b1'], 'L1_ffn_W2': _L1_ffn_in['W2'], 'L1_ffn_b2': _L1_ffn_in['b2'], 'L1_ffn_scale': _L1_ffn_in['scale']}

def reference(x, ctx_1024, mask_BxS2_ff1, L0_xattn_Wq, L0_xattn_bq, L0_xattn_Wk, L0_xattn_bk, L0_xattn_Wv, L0_xattn_bv, L0_xattn_Wo, L0_xattn_bo, L0_ffn_Wg, L0_ffn_W1, L0_ffn_b1, L0_ffn_W2, L0_ffn_b2, L1_xattn_Wq, L1_xattn_bq, L1_xattn_Wk, L1_xattn_bk, L1_xattn_Wv, L1_xattn_bv, L1_ffn_W1, L1_ffn_b1, L1_ffn_W2, L1_ffn_b2, L1_ffn_scale):
    import jax
    import jax.numpy as jnp

    def _L0_xattn_ref(q, k, v, Wq, bq, Wk, bk, Wv, bv, Wo, bo):
        import jax, jax.numpy as jnp
        import numpy as np
        HEADS = 16
        D_MODEL = 256
        D_K = D_MODEL // HEADS
        B, Sq, D = q.shape
        Sk = k.shape[1]
        q_ = (q @ Wq.T + bq).reshape(B, Sq, HEADS, D_K).transpose(0, 2, 1, 3)
        k_ = (k @ Wk.T + bk).reshape(B, Sk, HEADS, D_K).transpose(0, 2, 1, 3)
        v_ = (v @ Wv.T + bv).reshape(B, Sk, HEADS, D_K).transpose(0, 2, 1, 3)
        scores = jnp.einsum('bhqd,bhkd->bhqk', q_, k_) / jnp.sqrt(jnp.float32(D_K))
        attn = jax.nn.softmax(scores, axis=-1)
        ctx = jnp.einsum('bhqk,bhkd->bhqd', attn, v_)
        concat = ctx.transpose(0, 2, 1, 3).reshape(B, Sq, D)
        return concat @ Wo.T + bo

    def _L0_ffn_ref(x, Wg, W1, b1, W2, b2):
        import jax, jax.numpy as jnp
        import numpy as np

        def _moe_forward(x, Wg, W1, b1, W2, b2):
            B, S, H = x.shape
            E = Wg.shape[1]
            tokens = x.reshape(-1, H)
            T = tokens.shape[0]
            C = -(-T // E)
            logits = tokens @ Wg
            gates = jax.nn.softmax(logits, axis=-1)
            idx = jnp.argmax(gates, axis=1)
            mask1 = jax.nn.one_hot(idx, E, dtype=gates.dtype)
            locations1 = jnp.cumsum(mask1, axis=0) - 1.0
            mask1 = mask1 * (locations1 < C).astype(gates.dtype)
            loc_s = jnp.sum(locations1 * mask1, axis=1).astype(jnp.int32)
            gates1 = jnp.sum(gates * mask1, axis=1)
            loc_oh = jax.nn.one_hot(loc_s, C, dtype=gates.dtype)
            dispatch = mask1[:, :, None] * loc_oh[:, None, :]
            combine = gates1[:, None, None] * dispatch
            expert_in = jnp.einsum('tec,th->ech', dispatch, tokens)
            hidden = jax.nn.relu(jnp.einsum('ech,ehf->ecf', expert_in, W1) + b1[:, None, :])
            expert_out = jnp.einsum('ecf,efh->ech', hidden, W2) + b2[:, None, :]
            out = jnp.einsum('tec,ech->th', combine, expert_out)
            return out.reshape(B, S, H)
        return _moe_forward(x, Wg, W1, b1, W2, b2)

    def _L1_xattn_ref(query_states, key_states, value_states, attention_mask, Wq, bq, Wk, bk, Wv, bv):
        import jax, jax.numpy as jnp
        import numpy as np
        import math
        B, L, D, NUM_HEADS = (4, 512, 256, 16)
        HEAD_SIZE = D // NUM_HEADS
        q = jnp.einsum('bld,de->ble', query_states, Wq) + bq
        k = jnp.einsum('bld,de->ble', key_states, Wk) + bk
        v = jnp.einsum('bld,de->ble', value_states, Wv) + bv
        scores = jnp.einsum('bqd,bkd->bqk', q, k) / math.sqrt(HEAD_SIZE)
        scores = scores + (1.0 - attention_mask)[:, None, :] * -10000.0
        probs = jax.nn.softmax(scores, axis=-1)
        context = jnp.einsum('bqk,bkd->bqd', probs, v)
        return context

    def _L1_ffn_ref(x, W1, b1, W2, b2, scale):
        import jax, jax.numpy as jnp
        import numpy as np
        LORA_DIM = 16
        LORA_TOKEN_INDEX = 1
        B, S, D, H = (4, 512, 256, 1024)
        Bx, Sx, Dx = x.shape
        Hx = W1.shape[0]
        lt = jax.lax.dynamic_slice_in_dim(x, LORA_TOKEN_INDEX, LORA_DIM, axis=1)
        even = lt[:, ::2, :]
        odd = lt[:, 1::2, :]
        m1 = (even[:, :4, :, None] * odd[:, :4, None, :]).reshape(Bx, Hx, Dx)
        m2 = (even[:, 4:, :, None] * odd[:, 4:, None, :]).reshape(Bx, Dx, Hx)
        h = jnp.einsum('bsd,hd->bsh', x, W1) + scale * jnp.einsum('bsd,bhd->bsh', x, m1) + b1
        h = jax.nn.gelu(h, approximate=False)
        out = jnp.einsum('bsh,oh->bso', h, W2) + scale * jnp.einsum('bsh,boh->bso', h, m2) + b2
        return out
    x = x + _L0_xattn_ref(_layernorm(x, axis=-1), ctx_1024, ctx_1024, L0_xattn_Wq, L0_xattn_bq, L0_xattn_Wk, L0_xattn_bk, L0_xattn_Wv, L0_xattn_bv, L0_xattn_Wo, L0_xattn_bo)
    x = x + _L0_ffn_ref(_layernorm(x, axis=-1), L0_ffn_Wg, L0_ffn_W1, L0_ffn_b1, L0_ffn_W2, L0_ffn_b2)
    x = x + _L1_xattn_ref(_layernorm(x, axis=-1), ctx_1024, ctx_1024, mask_BxS2_ff1, L1_xattn_Wq, L1_xattn_bq, L1_xattn_Wk, L1_xattn_bk, L1_xattn_Wv, L1_xattn_bv)
    x = x + _L1_ffn_ref(_layernorm(x, axis=-1), L1_ffn_W1, L1_ffn_b1, L1_ffn_W2, L1_ffn_b2, L1_ffn_scale)
    return x

_drawn_inputs = setup_inputs


def setup_inputs(seed=0):
    import zlib

    import numpy as np

    out = dict(_drawn_inputs(seed))
    spreads = {'L0_ffn_b1': (0.0, 0.314),
     'L0_ffn_b2': (0.0, 0.1),
     'L1_xattn_bq': (0.0, 0.1),
     'L1_xattn_bk': (0.0, 0.8),
     'L1_xattn_bv': (0.0, 0.1),
     'L1_ffn_b1': (0.0, 0.36),
     'L1_ffn_b2': (0.0, 0.1)}
    factors = {'L0_xattn_bq': 4.812, 'L0_xattn_bk': 8.0}
    for name, (base, spread) in spreads.items():
        noise = np.random.default_rng([zlib.crc32(name.encode()), seed]).standard_normal(out[name].shape)
        drawn = base * np.exp(spread * noise) if base else spread * noise
        out[name] = jnp.asarray(drawn.astype(out[name].dtype))
    for name, factor in factors.items():
        out[name] = (out[name] * factor).astype(out[name].dtype)
    return out
```

```python
from contextlib import ExitStack

import numpy as np
import concourse.bass as bass
from concourse import mybir

ALU = mybir.AluOpType
ACT = mybir.ActivationFunctionType
F32 = mybir.dt.float32
BF16 = mybir.dt.bfloat16
I32 = mybir.dt.int32
AX = mybir.AxisListType

P = 128
NB, S, D = 8, 112, 256
S2, KC = 375, 125
NKC = S2 // KC
DT = D // P
H, DK = 16, 16
E, F = 8, 1024
FT = F // P
CAP = NB * S // E
T = NB * S
EPS = 1e-5
HG = 4
UNITS = NKC * (H // HG)
VW = DK + 1
ROWS = 6 * DK
Q_PIECES = (0, 1, 2, 0, 1, 0)
K_PIECES = (0, 1, 0, 1, 0, 2)
RING = 4

PIPE = {
    0: [("V0", -1), ("C6", 2)],
    1: [],
    2: [("U", 1)],
    3: [("C1", 1), ("V1", -1)],
    4: [],
    5: [("C2", 1)],
    6: [("C3", 1), ("V2", -1)],
    7: [],
    8: [("NM", -1), ("L2", 1)],
    9: [("C4", 1)],
    10: [("C5", 1)],
    11: [],
}


def steps():
    for i in range(-1, NB + 2):
        for u in range(UNITS):
            yield i, u


def extras(i, u):
    for stage, behind in PIPE[u]:
        if 0 <= i - behind < NB:
            yield stage, i - behind


def norm_orders():
    moments = [(n, b) for n in (1, 2) for b in range(NB)] + [(3, 0)]
    rows = [(n, b) for n in (1, 2) for b in range(NB)]
    for i in range(NB + 7):
        moments += [(3, i + 1)] * (i + 1 < NB)
        rows += [(4, i - 7)] * (i >= 7)
        rows += [(3, i)] * (i < NB)
        moments += [(4, i - 6)] * (0 <= i - 6 < NB)
    return ({k: n + 1 for n, k in enumerate(moments)}, {k: n + 1 for n, k in enumerate(rows)})


MOMENTS, ROWS_DONE = norm_orders()


def build(nc, A):
    out = A["out"]
    with ExitStack() as ctx:
        def sb(name, shape, dt=F32):
            return ctx.enter_context(nc.sbuf_tensor(name, shape, dt))

        def sem(name):
            return ctx.enter_context(nc.semaphore(name))

        k_dram = nc.dram_tensor("k_pieces_dram", (NB, 3, DT * P, S2), BF16).ap()
        q_dram = nc.dram_tensor("q_pieces_dram", (3, DT * P, T), BF16).ap()
        xg_dram = nc.dram_tensor("expert_in_dram", (2 * T, D), F32).ap()
        eo_dram = nc.dram_tensor("expert_out_dram", (T, D), F32).ap()

        ctxT = sb("ctxT", [P, DT, NB * S2])
        xres = sb("xres", [S, NB, D])
        xn = sb("xn", [S, NB, D])
        xT = sb("xT", [P, DT, T])
        w_in = sb("w_in", [P, 4, DT, D])
        ident = sb("ident", [P, P])
        identb = sb("identb", [P, P], BF16)
        wg = sb("wg", [P, DT, E])
        bcol = sb("bcol", [P, 4, DT])
        b1col = sb("b1col", [P, E, FT])
        fb1col = sb("fb1col", [P, FT])
        browL0 = sb("browL0", [P, 2, D])
        browL1 = sb("browL1", [S, 2, D])
        mv = sb("mv", [S, NB, 2])
        stats = sb("stats", [S, NB, 6])
        veps = sb("veps", [S, NB])
        rstd = sb("rstd", [S, NB])
        neghalf = sb("neghalf", [S, NB])
        stackf = sb("stackf", [P, (3 * H * S2 + H * T) // 2])
        kstack = [stackf[:, n * H * S2 // 2:(n + 1) * H * S2 // 2].bitcast(BF16)
                  .rearrange("p (h k) -> p h k", h=H) for n in range(3)]
        qstack = stackf[:, 3 * H * S2 // 2:].bitcast(BF16).rearrange("p (h q) -> p h q", h=H)
        at = [0]

        def cut(region, n):
            a = at[0]
            at[0] += n
            assert at[0] <= region.shape[1], (at[0], region.shape)
            return region[:, a:a + n]

        ctxN = cut(stackf, NB * NKC * D).rearrange("p (c d) -> p c d", d=D)
        w_at1 = cut(stackf, 3 * DT * D).rearrange("p (w k e) -> p w k e", w=3, k=DT)
        w1f = cut(stackf, DT * F).rearrange("p (k f) -> p k f", k=DT)
        W2W = D + 16
        w2f = [cut(stackf, FT * W2W).rearrange("p (f o) -> p f o", f=FT) for _ in range(2)]
        hid = [cut(stackf, FT * S).rearrange("p (f s) -> p f s", f=FT) for _ in range(2)]
        vones = [sb(f"vones{n}", [P, NKC, H, VW]) for n in range(2)]
        pT = [sb(f"pT{n}", [P, HG * S]) for n in range(3)]
        ctxU = sb("ctxU", [P, 4 * S])
        cc = sb("cc", [S, D])
        ccT = sb("ccT", [P, DT, S])
        mneg = sb("mneg", [S, H])
        mpieces = sb("mpieces", [S, 2 * H], BF16)
        mT = sb("mT", [2 * H, S], BF16)
        rden = sb("rden", [S, H])
        tri = sb("tri", [S, S], BF16)
        onesb = sb("onesb", [S, S], BF16)
        em8 = sb("em8", [S, E])
        slot0 = sb("slot0", [S, E])
        spill = sb("spill", [S, NB])
        onehot = sb("onehot", [S, E], BF16)
        seen = sb("seen", [S, 2, E], BF16)
        lg = sb("lg", [S, E])
        ex = sb("ex", [S, E])
        small = sb("small", [S, 16])
        tmp8 = sb("tmp8", [S, 4, E])
        gate = sb("gate", [S, NB])
        idx_put = sb("idx_put", [S, NB], I32)
        idx_get = sb("idx_get", [S, NB], I32)
        ring = sb("ring", [P, RING, 2 * DT * F])
        w1e = [ring[:, n, 0:DT * F].rearrange("p (k f) -> p k f", k=DT) for n in range(RING)]
        w2e = [ring[:, n, DT * F:].rearrange("p (f o) -> p f o", f=FT) for n in range(RING)]
        stage = ring[:, 2:4, :].rearrange("p a n -> p (a n)")
        at[0] = 0
        kt = [cut(stage, DT * S2).rearrange("p (m k) -> p m k", m=DT) for _ in range(2)]
        kr = cut(stage, DT * S2).rearrange("p (m k) -> p m k", m=DT)
        kp = [cut(stage, 3 * DT * S2 // 2).bitcast(BF16).rearrange("p (c m k) -> p c m k", c=3, m=DT)
              for _ in range(2)]
        qt = cut(stage, DT * T // 2).rearrange("p (m k) -> p m k", m=DT)
        qr = cut(stage, DT * T // 2).rearrange("p (m k) -> p m k", m=DT)
        qp = cut(stage, 3 * DT * T // 4).bitcast(BF16).rearrange("p (c m k) -> p c m k", c=3, m=DT)
        eo = [sb("eo0", [S, D]), cc]
        b2row = [sb(f"b2row{n}", [S, D]) for n in range(2)]
        late = ring[:, :, :].rearrange("p a n -> p (a n)")
        at[0] = 0
        q1T = [cut(late, DT * S).rearrange("p (k s) -> p k s", k=DT) for _ in range(2)]
        qkT = [cut(late, DT * S).rearrange("p (k s) -> p k s", k=DT) for _ in range(2)]
        tq = [cut(late, 1) for _ in range(2)]
        maskr = cut(late, NB * S2).rearrange("p (b k) -> p b k", b=NB)
        sc = [cut(late, S2) for _ in range(2)]
        pr = [cut(late, S2) for _ in range(2)]
        pT1 = [cut(late, NKC * S).rearrange("p (c s) -> p c s", c=NKC) for _ in range(2)]
        uT = [cut(late, DT * S).rearrange("p (k s) -> p k s", k=DT) for _ in range(2)]
        sm1 = cut(late, 4 * NB).rearrange("p (b j) -> p b j", j=4)
        gT = [cut(late, FT * S).rearrange("p (f s) -> p f s", f=FT) for _ in range(2)]
        R = [cut(late, 4 * S).rearrange("p (j s) -> p j s", j=4) for _ in range(2)]
        Bm = [cut(late, D).rearrange("p (o r) -> p o r", r=4) for _ in range(2)]
        Bs = [cut(late, D // 4) for _ in range(2)]
        B2 = [cut(late, D).rearrange("p (j o) -> p j o", j=4) for _ in range(4)]
        G2 = [cut(late, 64) for _ in range(2)]
        G2T = [cut(late, S) for _ in range(2)]
        outs = [cut(late, D) for _ in range(2)]
        m1mask = sb("m1mask", [16, 4])
        sel2 = sb("sel2", [S, 64])
        maskR = sb("maskR", [64, 4])
        maskJ = sb("maskJ", [64, 4])
        scale_t = sb("scale_t", [64, 1])

        ps = ctx.enter_context(nc.psum_tensor("ps", [P, 8, 512], F32))

        def bank(n):
            return ps[:, n, :]

        filled = [sem(f"bank{n}_filled") for n in range(8)]
        drained = [sem(f"bank{n}_drained") for n in range(8)]
        fills, drains = [0] * 8, [0] * 8
        place = {}

        def filled_at(key):
            n, c, _ = place[key]
            return filled[n], c

        def drained_at(key):
            n, _, c = place[key]
            return drained[n], c

        ld = {n: sem(f"loaded_{n}") for n in
              ("x", "wq", "wk", "wv", "wo", "bias", "wg", "b1", "rows", "qstack0", "qstack1",
               "at1w", "at1rows", "ffnw", "mask", "ffnb1", "scale")}
        ld_ctx = [sem(f"loaded_ctx{b}") for b in range(NB)]
        ld_ctxN = [sem(f"loaded_ctxN{n}") for n in range(2)]
        ld_ring = [sem(f"loaded_expert{n}") for n in range(RING)]
        ld_kstack = [sem(f"loaded_kstack{n}") for n in range(3)]
        ld_b2 = [sem(f"loaded_b2row{n}") for n in range(2)]
        k_written = [sem(f"k_pieces_written{n}") for n in range(2)]
        q_written = sem("q_pieces_written")
        max_placed = sem("max_rows_placed")
        consts = sem("constants_ready")
        scaled = sem("masks_scaled")
        ones_ready = sem("ones_and_zeros_ready")
        var_ready = sem("variance_ready")
        rstd_ready = sem("rstd_ready")
        xn_ready = sem("normalised_ready")
        xbo_ready = sem("x_plus_bo_ready")
        k_high = sem("k_high_piece_ready")
        k_split = sem("k_pieces_ready")
        q_high = sem("q_high_piece_ready")
        q_split = sem("q_pieces_ready")
        pv_units = sem("pv_units_done")
        max_ready = sem("max_pieces_ready")
        lg_ready = sem("logit_max_ready")
        esum_ready = sem("gate_sum_ready")
        onehot_ready = sem("onehot_ready")
        slots_ready = sem("slots_ready")
        zeroed = sem("expert_in_zeroed")
        put = sem("rows_put")
        xe_loaded = [sem(f"expert_rows_loaded{n}") for n in range(2)]
        eo_stored = [sem(f"expert_out_stored{n}") for n in range(2)]
        got_rows = [sem(f"rows_got{b}") for b in range(NB)]
        at_ready = sem("second_scores_ready")
        exp_ready = sem("second_probs_ready")
        xbv_ready = sem("x_plus_bv_ready")
        xb2_ready = sem("x_plus_b2_ready")
        bm_ready = sem("ffn_rank_rows_ready")
        w2_ready = sem("ffn_w2_columns_ready")
        gelu_ready = sem("gelu_ready")
        stored = [sem(f"out_stored{n}") for n in range(2)]
        dve = sem("dve_step")
        acts = sem("act_step")
        pools = sem("pool_step")

        block = ctx.enter_context(nc.Block())

        @block.tensor
        def _(pe):
            def open_bank(key, n, fill=1):
                if drains[n]:
                    pe.wait_ge(drained[n], drains[n])
                fills[n] += fill
                drains[n] += 1
                place[key] = (n, fills[n], drains[n])
                return bank(n)

            def read(key):
                pe.wait_ge(*drained_at(key))

            ring_bank = [0]

            def next_bank(banks):
                ring_bank[0] += 1
                return banks[ring_bank[0] % len(banks)]

            def transpose_x(key, b, n):
                o = open_bank((key, b), n)[:, 0:DT * S].rearrange("p (k s) -> p k s", k=DT)
                for k in range(DT):
                    mm = pe.transpose(o[:, k, :], xn[:, b, k * P:(k + 1) * P], ident[0:S, 0:S])
                mm.then_inc(filled[n], 1)

            def project_k(b):
                pe.wait_ge(ld_ctx[b], 16)
                for m in range(DT):
                    n = next_bank(range(0, 5))
                    o = open_bank(("K", b, m), n)
                    for k in range(DT):
                        mm = pe.matmul(o[:, 0:S2], w_in[:, 1, k, m * P:(m + 1) * P],
                                       ctxT[:, k, b * S2:(b + 1) * S2], start=k == 0, stop=k == DT - 1)
                    mm.then_inc(filled[n], 1)

            def project_q(h):
                W = T // 2
                for b in range(4 * h, 4 * h + 4):
                    read(("XT1", b))
                for m in range(DT):
                    n = next_bank(range(0, 5))
                    o = open_bank(("Q", h, m), n)
                    for k in range(DT):
                        mm = pe.matmul(o[:, 0:W], w_in[:, 0, k, m * P:(m + 1) * P],
                                       xT[:, k, h * W:(h + 1) * W], start=k == 0, stop=k == DT - 1)
                    mm.then_inc(filled[n], 1)

            pe.wait_ge(consts, 1)
            pe.wait_ge(ld["wk"], 16)
            project_k(0)
            pe.wait_ge(ld["wq"], 16)
            for h in range(2):
                pe.wait_ge(xn_ready, 4 * (h + 1))
                for b in range(4 * h, 4 * h + 4):
                    transpose_x("XT1", b, 6 + b % 2)
                project_q(h)
                project_k(h + 1)
            for b in range(3, NB):
                project_k(b)

            def row_max(b, h):
                n = 3 + h % 2
                o = open_bank(("MX", b, h), n)
                pe.matmul(o[0:S, 0:S2], qstack[0:ROWS, h, b * S:(b + 1) * S], kstack[b % 3][0:ROWS, h, :],
                          start=True, stop=True).then_inc(filled[n], 1)

            def scores(b, u):
                c, g = divmod(u, H // HG)
                n = (UNITS * b + u) % 3
                o = open_bank(("ST", b, u), n)
                if u == 0:
                    pe.wait_ge(max_placed, 32 * (b + 1))
                for j in range(HG):
                    h = HG * g + j
                    mm = pe.matmul(o[0:KC, j * S:(j + 1) * S], kstack[b % 3][0:ROWS + 2, h, c * KC:(c + 1) * KC],
                                   qstack[0:ROWS + 2, h, b * S:(b + 1) * S], start=True, stop=True)
                mm.then_inc(filled[n], 1)

            def weighted(b, u):
                c, g = divmod(u, H // HG)
                if u == 0:
                    open_bank(("PV", b), 5, fill=0)
                    for chunk in range(NKC):
                        read(("V", b, chunk))
                read(("ST", b, u))
                for j in range(HG):
                    h = HG * g + j
                    mm = pe.matmul(bank(5)[32 * j:32 * j + VW, g * S:(g + 1) * S],
                                   vones[b % 2][0:KC, c, h, :], pT[(UNITS * b + u) % 3][0:KC, j * S:(j + 1) * S],
                                   start=u == 0, stop=c == NKC - 1, skip_group_check=True)
                mm.then_inc(pv_units, 1)

            def values(b, c):
                n = next_bank((6, 7))
                o = open_bank(("V", b, c), n)
                for k in range(DT):
                    mm = pe.matmul(o[0:KC, 0:D], ctxT[:, k, b * S2 + c * KC:b * S2 + (c + 1) * KC],
                                   w_in[:, 2, k, :], start=k == 0, stop=k == DT - 1)
                mm.then_inc(filled[n], 1)

            def post(stage, b):
                if stage in ("V0", "V1", "V2"):
                    values(b, int(stage[1]))
                elif stage == "NM":
                    pe.wait_ge(max_ready, b + 1)
                    n = next_bank((6, 7))
                    o = open_bank(("NM", b), n).bitcast(BF16)
                    pe.transpose(o[0:2 * H, 0:S], mpieces[:, :], identb[0:S, 0:S]).then_inc(filled[n], 1)
                elif stage == "C1":
                    read(("PV", b))
                    n = next_bank((6, 7))
                    o = open_bank(("C1", b), n)
                    for g in range(4):
                        mm = pe.transpose(o[0:S, g * P:(g + 1) * P], ctxU[:, g * S:(g + 1) * S], ident[:, :])
                    mm.then_inc(filled[n], 1)
                elif stage == "C2":
                    read(("C1", b))
                    n = next_bank((6, 7))
                    o = open_bank(("C2", b), n)[:, 0:DT * S].rearrange("p (k s) -> p k s", k=DT)
                    for k in range(DT):
                        mm = pe.transpose(o[:, k, :], cc[:, k * P:(k + 1) * P], ident[0:S, 0:S])
                    mm.then_inc(filled[n], 1)
                elif stage == "C3":
                    read(("C2", b))
                    n = next_bank((6, 7))
                    o = open_bank(("C3", b), n)
                    for k in range(DT):
                        mm = pe.matmul(o[0:S, 0:D], ccT[:, k, :], w_in[:, 3, k, :], start=k == 0, stop=k == DT - 1)
                    mm.then_inc(filled[n], 1)
                elif stage == "C4":
                    pe.wait_ge(xn_ready, NB + b + 1)
                    transpose_x("XT2", b, next_bank((6, 7)))
                elif stage == "C5":
                    read(("XT2", b))
                    n = next_bank((6, 7))
                    o = open_bank(("LG", b), n)
                    for k in range(DT):
                        mm = pe.matmul(o[0:S, 0:E], xT[:, k, b * S:(b + 1) * S], wg[:, k, :],
                                       start=k == 0, stop=k == DT - 1)
                    mm.then_inc(filled[n], 1)
                elif stage == "C6":
                    pe.wait_ge(onehot_ready, b + 1)
                    n = next_bank((6, 7))
                    o = open_bank(("CUM", b), n)
                    pe.matmul(o[0:S, 0:E], tri[:, :], onehot[:, :], start=True, stop=False)
                    pe.matmul(o[0:S, 0:E], onesb[:, :], seen[:, b % 2, :], start=False, stop=True)\
                      .then_inc(filled[n], 1)

            pe.wait_ge(ld["wv"], 16)
            pe.wait_ge(ld["wo"], 16)
            pe.wait_ge(ld["wg"], 16)
            pe.wait_ge(consts, 2)
            pe.wait_ge(ones_ready, 6)
            for i, u in steps():
                if i < NB and i >= 0:
                    scores(i, u)
                before = UNITS * i + u - 2
                if 0 <= before < UNITS * NB:
                    weighted(*divmod(before, UNITS))
                if i + 1 < NB and u < H // 2:
                    if u == 0:
                        pe.wait_ge(ld_kstack[(i + 1) % 3], 96 * ((i + 1) // 3 + 1))
                        if i + 1 in (0, 4):
                            pe.wait_ge(ld[f"qstack{(i + 1) // 4}"], 96)
                    row_max(i + 1, 2 * u)
                    row_max(i + 1, 2 * u + 1)
                for stage, b in extras(i, u):
                    if stage not in ("U", "L2"):
                        post(stage, b)

            def expert_rows(e):
                n = 6 + e % 2
                pe.wait_ge(xe_loaded[e // 4], 16)
                transpose_x("XE", e, n)

            def expert_up(e):
                read(("XE", e))
                pe.wait_ge(ld_ring[e % RING], 32 * (e // RING + 1))
                for half in range(2):
                    n = 2 * (e % 2) + half
                    o = open_bank(("UP", e, half), n)
                    for f in range(4):
                        ft = 4 * half + f
                        for k in range(DT):
                            mm = pe.matmul(o[:, f * S:(f + 1) * S], w1e[e % RING][:, k, ft * P:(ft + 1) * P],
                                           xT[:, k, e * S:(e + 1) * S], start=k == 0, stop=k == DT - 1)
                    mm.then_inc(filled[n], 1)

            def expert_down(e):
                n = 4 + e % 2
                read(("UP", e, 0))
                read(("UP", e, 1))
                o = open_bank(("DN", e), n)
                for ft in range(FT):
                    mm = pe.matmul(o[0:S, 0:D], hid[e % 2][:, ft, :], w2e[e % RING][:, ft, :],
                                   start=ft == 0, stop=ft == FT - 1)
                mm.then_inc(filled[n], 1)

            for e in range(E + 1):
                if e == 0:
                    expert_rows(0)
                if e + 1 < E:
                    expert_rows(e + 1)
                if e < E:
                    expert_up(e)
                if e >= 1:
                    expert_down(e - 1)

            def attend(stage, b):
                s = b % 2
                if stage == 0:
                    pe.wait_ge(xn_ready, ROWS_DONE[3, b])
                    transpose_x("XT3", b, 0)
                elif stage == 1:
                    if b == 0:
                        pe.wait_ge(ld["at1w"], 48)
                    read(("XT3", b))
                    o = open_bank(("Q1", b), 1)
                    for m in range(DT):
                        for k in range(DT):
                            mm = pe.matmul(o[:, m * S:(m + 1) * S], w_at1[:, 0, k, m * P:(m + 1) * P],
                                           xT[:, k, b * S:(b + 1) * S], start=k == 0, stop=k == DT - 1)
                    mm.then_inc(filled[1], 1)
                elif stage == 2:
                    read(("Q1", b))
                    o = open_bank(("QK", b), 2)
                    for m in range(DT):
                        for k in range(DT):
                            mm = pe.matmul(o[:, m * S:(m + 1) * S], w_at1[:, 1, k, m * P:(m + 1) * P],
                                           q1T[s][:, k, :], start=k == 0, stop=k == DT - 1)
                    for k in range(DT):
                        mm = pe.matmul(o[0:S, 2 * S:2 * S + 1], q1T[s][:, k, :], bcol[:, 3, k:k + 1],
                                       start=k == 0, stop=k == DT - 1)
                    mm.then_inc(filled[2], 1)
                elif stage == 3:
                    read(("QK", b))
                    o = open_bank(("S1", b), 3)
                    for k in range(DT):
                        mm = pe.matmul(o[0:S, 0:S2], qkT[s][:, k, :], ctxT[:, k, b * S2:(b + 1) * S2],
                                       start=k == 0, stop=k == DT - 1)
                    mm.then_inc(filled[3], 1)
                elif stage == 4:
                    pe.wait_ge(exp_ready, b + 1)
                    o = open_bank(("PT", b), 4)
                    for c in range(NKC):
                        mm = pe.transpose(o[0:KC, c * S:(c + 1) * S], pr[s][0:S, c * KC:(c + 1) * KC],
                                          ident[0:S, 0:S])
                    mm.then_inc(filled[4], 1)
                elif stage == 5:
                    read(("PT", b))
                    if b % 4 == 0:
                        pe.wait_ge(ld_ctxN[b // 4], 16)
                    o = open_bank(("UT", b), 5)
                    for m in range(DT):
                        for c in range(NKC):
                            mm = pe.matmul(o[:, m * S:(m + 1) * S], ctxN[0:KC, NKC * b + c, m * P:(m + 1) * P],
                                           pT1[s][0:KC, c, :], start=c == 0, stop=c == NKC - 1)
                    mm.then_inc(filled[5], 1)
                elif stage == 6:
                    read(("UT", b))
                    o = open_bank(("O1", b), 6)
                    for k in range(DT):
                        mm = pe.matmul(o[0:S, 0:D], uT[s][:, k, :], w_at1[:, 2, k, :],
                                       start=k == 0, stop=k == DT - 1)
                    mm.then_inc(filled[6], 1)
                elif stage == 7:
                    pe.wait_ge(xn_ready, ROWS_DONE[4, b])
                    transpose_x("XT4", b, 7)

            for i in range(NB + 7):
                for stage in range(7, -1, -1):
                    if 0 <= i - stage < NB:
                        attend(stage, i - stage)

            def ffn(stage, b):
                s = b % 2
                if stage == 0:
                    read(("XT4", b))
                    o = open_bank(("GR", b), 6)
                    for k in range(DT):
                        mm = pe.matmul(o[0:16, 0:S], xT[:, k, b * S + 1:b * S + 17], xT[:, k, b * S:(b + 1) * S],
                                       start=k == 0, stop=k == DT - 1)
                    mm.then_inc(filled[6], 1)
                    o = open_bank(("BS", b), 7)
                    pe.matmul(o[0:64, 0:D], sel2[:, :], xn[:, b, :], start=True, stop=True).then_inc(filled[7], 1)
                elif stage == 1:
                    if b == 0:
                        pe.wait_ge(ld["ffnw"], 48)
                    read(("GR", b))
                    for half in range(2):
                        n = 2 * s + half
                        o = open_bank(("F1", b, half), n)
                        for f in range(4):
                            ft = 4 * half + f
                            for k in range(DT):
                                pe.matmul(o[:, f * S:(f + 1) * S], w1f[:, k, ft * P:(ft + 1) * P],
                                          xT[:, k, b * S:(b + 1) * S], start=k == 0, stop=False)
                            j, m = divmod(ft, 2)
                            mm = pe.matmul(o[:, f * S:(f + 1) * S], xn[0:64, b, m * P:(m + 1) * P],
                                           R[s][0:64, j, :], start=False, stop=True)
                        mm.then_inc(filled[n], 1)
                elif stage == 2:
                    pe.wait_ge(gelu_ready, FT * (b + 1))
                    pe.wait_ge(w2_ready, 2 * (b + 1))
                    n = 4 + s
                    o = open_bank(("F2", b), n)
                    for ft in range(FT):
                        mm = pe.matmul(o[0:S, 0:W2W], gT[s][:, ft, :], w2f[s][:, ft, :],
                                       start=ft == 0, stop=ft == FT - 1)
                    mm.then_inc(filled[n], 1)
                elif stage == 3:
                    read(("F2", b))
                    o = open_bank(("GT", b), 7)
                    pe.transpose(o[0:64, 0:S], G2[s][0:S, :], ident[0:S, 0:S]).then_inc(filled[7], 1)
                elif stage == 4:
                    read(("GT", b))
                    pe.wait_ge(bm_ready, b + 1)
                    n = place["F2", b][0]
                    fills[n] += 1
                    drains[n] += 1
                    place["F3", b] = (n, fills[n], drains[n])
                    pe.matmul(bank(n)[0:S, 0:D], G2T[s][0:64, :], B2[b % 4][0:64, :, :].rearrange("p j o -> p (j o)"),
                              start=False, stop=True, skip_group_check=True).then_inc(filled[n], 1)

            for i in range(NB + 4):
                for stage in range(4, -1, -1):
                    if 0 <= i - stage < NB:
                        ffn(stage, i - stage)

        @block.scalar
        def _(act):
            n_act = [0]

            def step(ins):
                n_act[0] += 1
                ins.then_inc(acts, 1)
                act.wait_ge(acts, n_act[0])

            def full(key):
                act.wait_ge(*filled_at(key))
                return bank(place[key][0]), drained[place[key][0]]

            act.dma_start(w_in[:, 1, :, :], A["L0_xattn_Wk"].rearrange("(k p) n -> p k n", p=P)).then_inc(ld["wk"], 16)
            for r, name in enumerate(("L0_xattn_bq", "L0_xattn_bk", "L1_xattn_bq", "L1_xattn_bk")):
                act.dma_start(bcol[:, r, :], A[name]).then_inc(ld["bias"], 16)
            act.dma_start(w_in[:, 2, :, :], A["L0_xattn_Wv"].rearrange("(k p) n -> p k n", p=P)).then_inc(ld["wv"], 16)
            act.dma_start(w_in[:, 3, :, :], A["L0_xattn_Wo"].rearrange("(k p) n -> p k n", p=P)).then_inc(ld["wo"], 16)
            act.dma_start(wg[:, :, :], A["L0_ffn_Wg"].rearrange("(k p) n -> p k n", p=P)).then_inc(ld["wg"], 16)
            for r, name in enumerate(("L0_xattn_bv", "L0_xattn_bo")):
                act.dma_start(browL0[:, r, :], A[name].partition_broadcast(P)).then_inc(ld["rows"], 16)
            act.dma_start(b1col[:, :, :], A["L0_ffn_b1"]).then_inc(ld["b1"], 16)
            act.dma_start(fb1col[:, :], A["L1_ffn_b1"]).then_inc(ld["ffnb1"], 16)

            def copy_xT(key, b):
                o, free = full((key, b))
                act.activation(xT[:, :, b * S:(b + 1) * S], o[:, 0:DT * S].rearrange("p (k s) -> p k s", k=DT),
                               ACT.Copy).then_inc(free, 1)

            def split_k(b):
                if b >= 2:
                    act.wait_ge(k_split, b - 1)
                for m in range(DT):
                    o, free = full(("K", b, m))
                    act.activation(kt[b % 2][:, m, :], o[:, 0:S2], ACT.Identity, bias=bcol[:, 1, m:m + 1])\
                       .then_inc(free, 1)
                if b >= 2:
                    act.wait_ge(k_written[b % 2], 16 * (b // 2))
                for m in range(DT):
                    act.wait_ge(*drained_at(("K", b, m)))
                act.activation(kp[b % 2][:, 0, :, :], kt[b % 2][:, :, :], ACT.Copy).then_inc(k_high, 1)

            def split_q(h):
                W = T // 2
                if h:
                    act.wait_ge(q_split, h)
                    act.wait_ge(q_written, 16 * h)
                for m in range(DT):
                    o, free = full(("Q", h, m))
                    act.activation(qt[:, m, :], o[:, 0:W], ACT.Identity, bias=bcol[:, 0, m:m + 1])\
                       .then_inc(free, 1)
                for m in range(DT):
                    act.wait_ge(*drained_at(("Q", h, m)))
                act.activation(qp[:, 0, :, :], qt[:, :, :], ACT.Copy).then_inc(q_high, 1)

            act.wait_ge(ld["bias"], 64)
            split_k(0)
            for h in range(2):
                for b in range(4 * h, 4 * h + 4):
                    copy_xT("XT1", b)
                split_q(h)
                split_k(h + 1)
            for b in range(3, NB):
                split_k(b)

            def exps(b, u):
                w = UNITS * b + u
                o, free = full(("ST", b, u))
                if w >= 3:
                    act.wait_ge(pv_units, w - 2)
                act.activation(pT[w % 3][0:KC, :], o[0:KC, 0:HG * S], ACT.Exp, scale=DK ** -0.5).then_inc(free, 1)

            def post(stage, b):
                if stage == "U":
                    act.wait_ge(pv_units, UNITS * (b + 1))
                    if b:
                        act.wait_ge(*filled_at(("C1", b - 1)))
                    act.activation(ctxU[:, :], bank(5)[:, 0:4 * S], ACT.Copy).then_inc(drained[5], 1)
                elif stage == "C2":
                    o, free = full(("C2", b))
                    act.activation(ccT[:, :, :], o[:, 0:DT * S].rearrange("p (k s) -> p k s", k=DT), ACT.Copy)\
                       .then_inc(free, 1)
                elif stage == "NM":
                    o, free = full(("NM", b))
                    if b:
                        act.wait_ge(max_placed, 32 * b)
                    act.activation(mT[:, :], o.bitcast(BF16)[0:2 * H, 0:S], ACT.Copy).then_inc(free, 1)
                elif stage == "C4":
                    copy_xT("XT2", b)
                elif stage == "C5":
                    act.wait_ge(lg_ready, b + 1)
                    act.activation(ex[:, :], lg[:, :], ACT.Exp, bias=small[:, 0:1], accum_out=small[:, 1:2])\
                       .then_inc(esum_ready, 1)

            for i, u in steps():
                if 0 <= i < NB:
                    exps(i, u)
                for stage, b in extras(i, u):
                    if stage in ("U", "C2", "NM", "C4", "C5"):
                        post(stage, b)

            def hidden(e):
                if e >= 2:
                    act.wait_ge(*filled_at(("DN", e - 2)))
                o, free = full(("UP", e, 0))
                for f in range(4):
                    ins = act.activation(hid[e % 2][:, f, :], o[:, f * S:(f + 1) * S], ACT.Relu,
                                         bias=b1col[:, e, f:f + 1])
                ins.then_inc(free, 1)

            act.wait_ge(ld["b1"], 16)
            for e in range(E):
                if e == 0:
                    copy_xT("XE", 0)
                if e + 1 < E:
                    copy_xT("XE", e + 1)
                hidden(e)

            def attend(stage, b):
                s = b % 2
                if stage == 0:
                    copy_xT("XT3", b)
                elif stage == 1:
                    if b >= 2:
                        act.wait_ge(*filled_at(("QK", b - 2)))
                    o, free = full(("Q1", b))
                    for m in range(DT):
                        ins = act.activation(q1T[s][:, m, :], o[:, m * S:(m + 1) * S], ACT.Identity,
                                             bias=bcol[:, 2, m:m + 1])
                    ins.then_inc(free, 1)
                elif stage == 3:
                    act.wait_ge(at_ready, b + 1)
                    if b >= 2:
                        act.wait_ge(*filled_at(("PT", b - 2)))
                    act.activation(pr[s][0:S, :], sc[s][0:S, :], ACT.Exp, bias=sm1[0:S, b, 1:2],
                                   scale=DK ** -0.5, accum_out=sm1[0:S, b, 2:3]).then_inc(exp_ready, 1)
                elif stage == 4:
                    o, free = full(("PT", b))
                    if b >= 2:
                        act.wait_ge(*filled_at(("UT", b - 2)))
                    act.activation(pT1[s][0:KC, :, :], o[0:KC, 0:NKC * S].rearrange("p (c s) -> p c s", c=NKC),
                                   ACT.Copy).then_inc(free, 1)
                elif stage == 7:
                    copy_xT("XT4", b)

            for i in range(NB + 7):
                for stage in range(7, -1, -1):
                    if 0 <= i - stage < NB:
                        attend(stage, i - stage)

            act.wait_ge(ld["ffnb1"], 16)
            for b in range(NB):
                if b >= 2:
                    act.wait_ge(*filled_at(("F2", b - 2)))
                for half in range(2):
                    o, free = full(("F1", b, half))
                    for f in range(4):
                        ft = 4 * half + f
                        act.activation(gT[b % 2][:, ft, :], o[:, f * S:(f + 1) * S], ACT.Gelu,
                                       bias=fb1col[:, ft:ft + 1]).then_inc(gelu_ready, 1)
                    act.wait_ge(gelu_ready, FT * b + 4 * half + 4)
                    act.sem_inc(free, 1)

        @block.vector
        def _(v):
            n_dve = [0]

            def step(ins):
                n_dve[0] += 1
                ins.then_inc(dve, 1)
                v.wait_ge(dve, n_dve[0])

            def full(key):
                v.wait_ge(*filled_at(key))
                return bank(place[key][0]), drained[place[key][0]]

            def drained_by_me(key):
                v.wait_ge(*drained_at(key))

            def moments(b):
                step(v.bn_stats(stats[:, b, :], xres[:, b, :]))
                step(v.bn_aggr(mv[:, b, :], stats[:, b, :]))
                v.tensor_scalar(veps[:, b:b + 1], mv[:, b, 1:2], EPS, None, ALU.add).then_inc(var_ready, 1)

            def normalise(norm, b):
                v.wait_ge(rstd_ready, MOMENTS[norm, b])
                v.tensor_scalar(xn[:, b, :], xres[:, b, :], mv[:, b, 0:1], rstd[:, b:b + 1],
                                ALU.subtract, ALU.mult).then_inc(xn_ready, 1)

            def split_k(b):
                v.wait_ge(k_high, b + 1)
                step(v.tensor_tensor(kr[:, :, :], kt[b % 2][:, :, :], kp[b % 2][:, 0, :, :], ALU.subtract))
                step(v.tensor_copy(kp[b % 2][:, 1, :, :], kr[:, :, :]))
                v.tensor_tensor(kp[b % 2][:, 2, :, :], kr[:, :, :], kp[b % 2][:, 1, :, :], ALU.subtract)\
                 .then_inc(k_split, 1)
                v.wait_ge(k_split, b + 1)

            def split_q(h):
                v.wait_ge(q_high, h + 1)
                step(v.tensor_tensor(qr[:, :, :], qt[:, :, :], qp[:, 0, :, :], ALU.subtract))
                step(v.tensor_copy(qp[:, 1, :, :], qr[:, :, :]))
                v.tensor_tensor(qp[:, 2, :, :], qr[:, :, :], qp[:, 1, :, :], ALU.subtract).then_inc(q_split, 1)
                v.wait_ge(q_split, h + 1)

            v.memset(neghalf[:, :], -0.5).then_inc(ones_ready, 1)
            v.memset(eo[0][:, :], 0.0).then_inc(ones_ready, 1)
            v.wait_ge(ld["x"], 16)
            for b in range(4):
                moments(b)
            for b in range(4):
                normalise(1, b)
            for b in range(4, NB):
                moments(b)
            split_k(0)
            for b in range(4, NB):
                normalise(1, b)
            v.memset(vones[0][:, :, :, DK:VW], 1.0).then_inc(ones_ready, 1)
            v.memset(vones[1][:, :, :, DK:VW], 1.0).then_inc(ones_ready, 1)
            v.memset(bank(5)[:, :], 0.0).then_inc(ones_ready, 1)
            split_q(0)
            split_k(1)
            split_q(1)
            for b in range(2, NB):
                split_k(b)
            v.memset(seen[:, :, :], 0.0).then_inc(ones_ready, 1)
            v.wait_ge(ld["rows"], 32)
            v.wait_ge(ones_ready, 6)

            def row_max(b, h):
                o, free = full(("MX", b, h))
                v.tensor_reduce(mneg[:, h:h + 1], o[0:S, 0:S2], AX.X, ALU.max, negate=True).then_inc(free, 1)

            def post(stage, b):
                if stage in ("V0", "V1", "V2"):
                    c = int(stage[1])
                    o, free = full(("V", b, c))
                    if c == 0 and b >= 2:
                        v.wait_ge(pv_units, UNITS * (b - 1))
                    v.tensor_tensor(vones[b % 2][0:KC, c, :, 0:DK],
                                    o[0:KC, 0:D].rearrange("p (h w) -> p h w", h=H),
                                    browL0[0:KC, 0, :].rearrange("p (h w) -> p h w", h=H), ALU.add)\
                     .then_inc(free, 1)
                elif stage == "NM":
                    for h in (H - 2, H - 1):
                        drained_by_me(("MX", b, h))
                    if b:
                        v.wait_ge(*filled_at(("NM", b - 1)))
                    step(v.tensor_copy(mpieces[:, 0:H], mneg[:, :]))
                    v.tensor_tensor(mpieces[:, H:2 * H], mneg[:, :], mpieces[:, 0:H], ALU.subtract)\
                     .then_inc(max_ready, 1)
                    v.wait_ge(max_ready, b + 1)
                elif stage == "C1":
                    o, free = full(("C1", b))
                    o = o[0:S, :].rearrange("p (h w) -> p h w", h=H)
                    step(v.reciprocal(rden[:, :], o[:, :, DK]))
                    if b:
                        v.wait_ge(*filled_at(("C2", b - 1)))
                    v.tensor_tensor(cc[:, :].rearrange("p (h w) -> p h w", h=H), o[:, :, 0:DK],
                                    rden[:, :].unsqueeze(2).broadcast_to([S, H, DK]), ALU.mult)\
                     .then_inc(free, 1)
                elif stage == "C3":
                    o, free = full(("C3", b))
                    v.wait_ge(xbo_ready, NB)
                    v.tensor_tensor(xres[:, b, :], o[0:S, 0:D], xres[:, b, :], ALU.add).then_inc(free, 1)
                    drained_by_me(("C3", b))
                    moments(b)
                elif stage == "L2":
                    normalise(2, b)
                elif stage == "C5":
                    o, free = full(("LG", b))
                    v.wait_ge(esum_ready, b) if b else None
                    v.tensor_copy(lg[:, :], o[0:S, 0:E]).then_inc(free, 1)
                    drained_by_me(("LG", b))
                    v.tensor_reduce(small[:, 0:1], lg[:, :], AX.X, ALU.max, negate=True).then_inc(lg_ready, 1)
                    v.wait_ge(lg_ready, b + 1)
                    step(v.tensor_scalar(tmp8[:, 0, :], lg[:, :], small[:, 0:1], 0.0, ALU.add, ALU.is_equal))
                    step(v.tensor_tensor(tmp8[:, 1, :], tmp8[:, 0, :], em8[:, :], ALU.mult))
                    step(v.tensor_reduce(small[:, 2:3], tmp8[:, 1, :], AX.X, ALU.min))
                    v.tensor_scalar(onehot[:, :], tmp8[:, 1, :], small[:, 2:3], None, ALU.is_equal)\
                     .then_inc(onehot_ready, 1)
                    v.wait_ge(onehot_ready, b + 1)
                    step(v.tensor_tensor(seen[:, (b + 1) % 2, :], seen[:, b % 2, :], onehot[:, :], ALU.add))
                elif stage == "C6":
                    o, free = full(("CUM", b))
                    v.tensor_copy(tmp8[:, 2, :], o[0:S, 0:E]).then_inc(free, 1)
                    drained_by_me(("CUM", b))
                    step(v.scalar_tensor_tensor(tmp8[:, 0, :], tmp8[:, 2, :], float(CAP), onehot[:, :],
                                                ALU.is_le, ALU.mult))
                    step(v.tensor_tensor(tmp8[:, 3, :], tmp8[:, 2, :], slot0[:, :], ALU.add))
                    step(v.tensor_tensor(tmp8[:, 1, :], tmp8[:, 3, :], onehot[:, :], ALU.mult))
                    step(v.tensor_reduce(small[:, 3:5], tmp8[:, 0:2, :], AX.X, ALU.add))
                    v.tensor_scalar(idx_get[:, b:b + 1], small[:, 4:5], small[:, 3:4], None, ALU.mult)
                    step(v.tensor_scalar(small[:, 5:6], small[:, 4:5], spill[:, b:b + 1], small[:, 3:4],
                                         ALU.subtract, ALU.mult))
                    v.tensor_scalar(idx_put[:, b:b + 1], small[:, 5:6], spill[:, b:b + 1], None, ALU.add)\
                     .then_inc(slots_ready, 1)
                    v.wait_ge(esum_ready, b + 1)
                    step(v.reciprocal(small[:, 6:7], small[:, 1:2]))
                    step(v.tensor_scalar(gate[:, b:b + 1], small[:, 6:7], small[:, 3:4], None, ALU.mult))

            for i, u in steps():
                if i + 1 < NB and u < H // 2:
                    row_max(i + 1, 2 * u)
                    row_max(i + 1, 2 * u + 1)
                for stage, b in extras(i, u):
                    if stage not in ("U", "C2", "C4"):
                        post(stage, b)

            v.wait_ge(ld["b1"], 16)

            def finish(e):
                o, free = full(("DN", e))
                v.wait_ge(ld_b2[e % 2], 16 * (e // 2 + 1))
                if e >= 2:
                    v.wait_ge(eo_stored[e % 2], 16 * (e // 2))
                v.tensor_tensor(eo[e % 2][:, :], o[0:S, 0:D], b2row[e % 2][:, :], ALU.add).then_inc(free, 1)

            for e in range(E):
                if e >= 2:
                    v.wait_ge(*filled_at(("DN", e - 2)))
                o, free = full(("UP", e, 1))
                for f in range(4):
                    ins = v.tensor_scalar(hid[e % 2][:, 4 + f, :], o[:, f * S:(f + 1) * S],
                                          b1col[:, e, 4 + f:5 + f], 0.0, ALU.add, ALU.max)
                ins.then_inc(free, 1)
                if e:
                    finish(e - 1)
            finish(E - 1)

            def combine(b):
                v.wait_ge(got_rows[b], 16)
                step(v.scalar_tensor_tensor(xres[:, b, :], xn[:, b, :], gate[:, b:b + 1], xres[:, b, :],
                                            ALU.mult, ALU.add))
                moments(b)

            def attend(stage, b):
                s = b % 2
                if stage == 2:
                    if b >= 2:
                        v.wait_ge(*filled_at(("S1", b - 2)))
                    o, free = full(("QK", b))
                    step(v.tensor_copy(tq[s][0:S, :], o[0:S, 2 * S:2 * S + 1]))
                    v.tensor_copy(qkT[s][:, :, :], o[:, 0:DT * S].rearrange("p (k s) -> p k s", k=DT))\
                     .then_inc(free, 1)
                elif stage == 3:
                    o, free = full(("S1", b))
                    if b == 0:
                        v.wait_ge(ld["mask"], 16)
                    if b >= 2:
                        v.wait_ge(exp_ready, b - 1)
                    step(v.tensor_scalar(maskr[0:S, b, :], maskr[0:S, b, :], 40000.0, -40000.0, ALU.mult, ALU.add))
                    v.scalar_tensor_tensor(sc[s][0:S, :], o[0:S, 0:S2], tq[s][0:S, :], maskr[0:S, b, :],
                                           ALU.add, ALU.add).then_inc(free, 1)
                    drained_by_me(("S1", b))
                    step(v.tensor_reduce(sm1[0:S, b, 0:1], sc[s][0:S, :], AX.X, ALU.max, negate=True))
                    v.tensor_scalar(sm1[0:S, b, 1:2], sm1[0:S, b, 0:1], DK ** -0.5, None, ALU.mult)\
                     .then_inc(at_ready, 1)
                elif stage == 5:
                    if b >= 2:
                        v.wait_ge(*filled_at(("O1", b - 2)))
                    o, free = full(("UT", b))
                    v.tensor_copy(uT[s][:, :, :], o[:, 0:DT * S].rearrange("p (k s) -> p k s", k=DT))\
                     .then_inc(free, 1)
                elif stage == 6:
                    v.wait_ge(exp_ready, b + 1)
                    step(v.reciprocal(sm1[0:S, b, 3:4], sm1[0:S, b, 2:3]))
                    o, free = full(("O1", b))
                    v.wait_ge(xbv_ready, b + 1)
                    v.scalar_tensor_tensor(xres[:, b, :], o[0:S, 0:D], sm1[0:S, b, 3:4], xres[:, b, :],
                                           ALU.mult, ALU.add).then_inc(free, 1)
                    drained_by_me(("O1", b))
                    moments(b)

            combine(0)
            for i in range(NB + 7):
                if i + 1 < NB:
                    combine(i + 1)
                if 0 <= i - 7:
                    normalise(4, i - 7)
                if i < NB:
                    normalise(3, i)
                for stage in (6, 5, 3, 2):
                    if 0 <= i - stage < NB:
                        attend(stage, i - stage)

            v.wait_ge(scaled, 2)
            v.wait_ge(ld["ffnw"], 48)
            for s in range(2):
                step(v.memset(R[s][0:64, :, :], 0.0))
                step(v.memset(G2[s][0:S, :], 0.0))
                step(v.memset(w2f[s][:, :, D:W2W], 0.0))

            def ffn(stage, b):
                s = b % 2
                if stage == 0:
                    if b >= 2:
                        for half in range(2):
                            v.wait_ge(*filled_at(("F1", b - 2, half)))
                    o, free = full(("GR", b))
                    v.tensor_tensor(R[s][0:16, :, :], o[0:16, 0:S].unsqueeze(1).broadcast_to([16, 4, S]),
                                    m1mask[:, :].unsqueeze(2).broadcast_to([16, 4, S]), ALU.mult).then_inc(free, 1)
                    o, free = full(("BS", b))
                    v.tensor_tensor(Bm[s][0:64, :, :], o[0:64, 0:D].rearrange("p (o r) -> p o r", r=4),
                                    maskR[:, :].unsqueeze(1).broadcast_to([64, D // 4, 4]), ALU.mult)\
                     .then_inc(free, 1)
                    drained_by_me(("BS", b))
                    step(v.tensor_reduce(Bs[s][0:64, :], Bm[s][0:64, :, :], AX.X, ALU.add))
                    if b >= 4:
                        v.wait_ge(*filled_at(("F3", b - 4)))
                    v.tensor_tensor(B2[b % 4][0:64, :, :], Bs[s][0:64, :].unsqueeze(1).broadcast_to([64, 4, D // 4]),
                                    maskJ[:, :].unsqueeze(2).broadcast_to([64, 4, D // 4]), ALU.mult)\
                     .then_inc(bm_ready, 1)
                    if b >= 2:
                        v.wait_ge(*filled_at(("F2", b - 2)))
                    for m in range(DT):
                        cols = w2f[s][:, :, D:W2W].rearrange("p (r m) (a j) -> p m r a j", m=DT, a=4)[:, m]
                        for r in range(4):
                            ins = v.tensor_copy(cols[:, r, r, :], xT[:, m, b * S + 10:b * S + 17:2])
                        ins.then_inc(w2_ready, 1)
                elif stage == 3:
                    if b >= 2:
                        v.wait_ge(*filled_at(("GT", b - 2)))
                    o, free = full(("F2", b))
                    v.tensor_copy(G2[s][0:S, 0:16], o[0:S, D:W2W]).then_inc(free, 1)
                elif stage == 5:
                    o, free = full(("GT", b))
                    v.tensor_copy(G2T[s][0:64, :], o[0:64, 0:S]).then_inc(free, 1)
                elif stage == 4:
                    o, free = full(("F3", b))
                    v.wait_ge(xb2_ready, b + 1)
                    if b >= 2:
                        v.wait_ge(stored[s], 16 * (b // 2))
                    v.tensor_tensor(outs[s][0:S, :], o[0:S, 0:D], xres[:, b, :], ALU.add).then_inc(free, 1)

            for i in range(NB + 4):
                if 0 <= i - 4 < NB:
                    ffn(4, i - 4)
                if 0 <= i - 3 < NB:
                    ffn(5, i - 3)
                if 0 <= i - 2 < NB:
                    ffn(3, i - 2)
                if 0 <= i < NB:
                    ffn(0, i)

        @block.gpsimd
        def _(g):
            n_pool = [0]

            def step(ins):
                n_pool[0] += 1
                ins.then_inc(pools, 1)
                g.wait_ge(pools, n_pool[0])

            def root(norm, b):
                g.wait_ge(var_ready, MOMENTS[norm, b])
                g.tensor_tensor(rstd[:, b:b + 1], veps[:, b:b + 1], neghalf[:, b:b + 1], ALU.pow)\
                 .then_inc(rstd_ready, 1)

            def diagonal(ap, base, pattern, cm):
                step(g.affine_select(out=ap, in_=ap, compare_op=ALU.not_equal, fill=1.0, base=base,
                                     pattern=pattern, channel_multiplier=cm))

            step(g.memset(ident[:, :], 0.0))
            diagonal(ident[:, :], 0, [[-1, P]], 1)
            g.tensor_copy(identb[:, :], ident[:, :]).then_inc(consts, 1)
            g.wait_ge(ones_ready, 1)
            for b in range(NB):
                root(1, b)
            g.wait_ge(rstd_ready, NB)
            for n in range(3):
                step(g.memset(kstack[n][96:98, :, :], 1.0))
            step(g.memset(onesb[:, :], 1.0))
            step(g.affine_select(out=tri[:, :], in_=onesb[:, :], compare_op=ALU.is_ge, fill=0.0, base=0,
                                 pattern=[[1, S]], channel_multiplier=-1))
            step(g.iota(em8[:, :], pattern=[[1, E]], base=-E, channel_multiplier=0,
                        allow_small_or_imprecise_dtypes=True))
            step(g.iota(slot0[:, :], pattern=[[CAP, E]], base=-1, channel_multiplier=0,
                        allow_small_or_imprecise_dtypes=True))
            g.iota(spill[:, :], pattern=[[S, NB]], base=T, channel_multiplier=1,
                   allow_small_or_imprecise_dtypes=True).then_inc(consts, 1)
            g.wait_ge(xn_ready, NB)
            g.wait_ge(ld["rows"], 32)
            for b in range(NB):
                g.tensor_tensor(xres[:, b, :], xres[:, b, :], browL0[0:S, 1, :], ALU.add).then_inc(xbo_ready, 1)
            g.wait_ge(xbo_ready, NB)
            step(g.memset(m1mask[:, :], 0.0))
            diagonal(m1mask[:, :], -1, [[-2, 4]], 1)
            step(g.memset(sel2[:, :], 0.0))
            diagonal(sel2[:, 0:16].rearrange("p (r j) -> p r j", r=4), -9, [[0, 4], [-2, 4]], 1)
            step(g.memset(maskJ[:, :], 0.0))
            for r in range(4):
                diagonal(maskJ[:, :], -4 * r, [[-1, 4]], 1)
            step(g.memset(maskR[:, :], 1.0))
            step(g.affine_select(out=maskR[:, :], in_=maskR[:, :], compare_op=ALU.is_ge, fill=0.0, base=0,
                                 pattern=[[-4, 4]], channel_multiplier=1))
            step(g.affine_select(out=maskR[:, :], in_=maskR[:, :], compare_op=ALU.is_ge, fill=0.0, base=3,
                                 pattern=[[4, 4]], channel_multiplier=-1))
            g.wait_ge(ld["scale"], 16)
            g.tensor_scalar(m1mask[:, :], m1mask[:, :], scale_t[0:16, :], None, ALU.mult).then_inc(scaled, 1)
            g.tensor_scalar(maskJ[:, :], maskJ[:, :], scale_t[:, :], None, ALU.mult).then_inc(scaled, 1)

            g.wait_ge(zeroed, 16)
            for i, u in steps():
                for stage, b in extras(i, u):
                    if stage == "C3":
                        root(2, b)
                    elif stage == "C6":
                        g.wait_ge(slots_ready, b + 1)
                        g.indirect_dma_start(out=xg_dram, out_offset=bass.IndirectOffsetOnAxis(
                            ap=idx_put[:, b:b + 1], axis=0), in_=xn[:, b, :], in_offset=None).then_inc(put, 16)

            for n in range(2):
                g.wait_ge(eo_stored[n], 16 * E // 2)
            for b in range(NB):
                g.indirect_dma_start(out=xn[:, b, :], out_offset=None, in_=eo_dram,
                                     in_offset=bass.IndirectOffsetOnAxis(ap=idx_get[:, b:b + 1], axis=0))\
                 .then_inc(got_rows[b], 16)

            g.wait_ge(ld["at1rows"], 32)
            def plus(b, r, s):
                g.tensor_tensor(xres[:, b, :], xres[:, b, :], browL1[:, r, :], ALU.add).then_inc(s, 1)

            root(3, 0)
            for i in range(NB + 7):
                if i + 1 < NB:
                    root(3, i + 1)
                if i < NB:
                    g.wait_ge(xn_ready, ROWS_DONE[3, i])
                    plus(i, 0, xbv_ready)
                if 0 <= i - 6 < NB:
                    root(4, i - 6)
                if 0 <= i - 7 < NB:
                    g.wait_ge(xn_ready, ROWS_DONE[4, i - 7])
                    plus(i - 7, 1, xb2_ready)

        @block.sync
        def _(sp):
            def wait_filled(key):
                sp.wait_ge(*filled_at(key))

            def kp_of(name, **kw):
                return A[name].rearrange("(k p) n -> p k n", p=P)

            def load_ctx(b):
                sp.dma_start(ctxT[:, :, b * S2:(b + 1) * S2],
                             A["ctxT"].rearrange("(k p) t -> p k t", p=P)[:, :, b * S2:(b + 1) * S2])\
                  .then_inc(ld_ctx[b], 16)

            def load_expert(e):
                n = e % RING
                sp.dma_start(w1e[n], A["L0_ffn_W1"][e].rearrange("(k p) f -> p k f", p=P)).then_inc(ld_ring[n], 16)
                sp.dma_start(w2e[n], A["L0_ffn_W2"][e].rearrange("(f p) o -> p f o", p=P)).then_inc(ld_ring[n], 16)

            def load_b2(e):
                sp.dma_start(b2row[e % 2][:, :], A["L0_ffn_b2"][e].partition_broadcast(S)).then_inc(ld_b2[e % 2], 16)

            sp.dma_start(xres[:, :, :], A["x"].rearrange("b s d -> s b d")).then_inc(ld["x"], 16)
            load_ctx(0)
            sp.dma_start(w_in[:, 0, :, :], kp_of("L0_xattn_Wq")).then_inc(ld["wq"], 16)
            for b in range(1, NB):
                load_ctx(b)

            def write_k(b):
                sp.wait_ge(k_split, b + 1)
                sp.dma_start(k_dram[b].rearrange("c (m p) k -> p c m k", p=P), kp[b % 2][:, :, :, :])\
                  .then_inc(k_written[b % 2], 16)

            def write_q(h):
                W = T // 2
                sp.wait_ge(q_split, h + 1)
                sp.dma_start(q_dram.rearrange("c (m p) t -> p c m t", p=P)[:, :, :, h * W:(h + 1) * W],
                             qp[:, :, :, :]).then_inc(q_written, 16)

            def stack_k(b):
                sp.wait_ge(k_written[b % 2], 16 * (b // 2 + 1))
                if b >= 3:
                    wait_filled(("ST", b - 3, UNITS - 1))
                for j, piece in enumerate(K_PIECES):
                    sp.dma_start(kstack[b % 3][j * DK:(j + 1) * DK, :, :],
                                 k_dram[b, piece].rearrange("(h d) k -> d h k", d=DK)).then_inc(ld_kstack[b % 3], 16)

            def stack_q(h):
                W = T // 2
                sp.wait_ge(q_written, 16 * (h + 1))
                for j, piece in enumerate(Q_PIECES):
                    sp.dma_start(qstack[j * DK:(j + 1) * DK, :, h * W:(h + 1) * W],
                                 q_dram[piece].rearrange("(h d) t -> d h t", d=DK)[:, :, h * W:(h + 1) * W])\
                      .then_inc(ld[f"qstack{h}"], 16)

            write_k(0)
            write_q(0)
            stack_k(0)
            stack_q(0)
            write_k(1)
            write_q(1)
            stack_k(1)
            stack_q(1)
            write_k(2)
            stack_k(2)
            for b in range(3, NB):
                write_k(b)
            sp.wait_ge(ones_ready, 2)
            sp.dma_start(xg_dram[0:T].rearrange("(e c) d -> c e d", e=E),
                         eo[0][:, :].unsqueeze(1).broadcast_to([S, E, D])).then_inc(zeroed, 16)
            load_expert(0)
            load_expert(1)
            sp.dma_start(scale_t[:, :], A["L1_ffn_scale"].partition_broadcast(64)).then_inc(ld["scale"], 16)
            load_b2(0)
            load_b2(1)
            for n in range(2):
                sp.wait_ge(k_written[n], 16 * NB // 2)
            load_expert(2)
            load_expert(3)
            for r, name in enumerate(("L1_xattn_bv", "L1_ffn_b2")):
                sp.dma_start(browL1[:, r, :], A[name].partition_broadcast(S)).then_inc(ld["at1rows"], 16)
            for b in range(NB):
                wait_filled(("NM", b))
                sp.wait_ge(*drained_at(("NM", b)))
                for piece in range(2):
                    sp.dma_start(qstack[96 + piece:97 + piece, :, b * S:(b + 1) * S],
                                 mT[piece * H:(piece + 1) * H, :]).then_inc(max_placed, 16)
                if 1 <= b and b + 2 < NB:
                    stack_k(b + 2)

            wait_filled(("ST", NB - 1, UNITS - 1))
            for r, name in enumerate(("L1_xattn_Wq", "L1_xattn_Wk", "L1_xattn_Wv")):
                sp.dma_start(w_at1[:, r, :, :], kp_of(name)).then_inc(ld["at1w"], 16)

            sp.wait_ge(put, 16 * NB)
            for half in range(2):
                sp.dma_start(xn[:, 4 * half:4 * half + 4, :],
                             xg_dram[0:T].rearrange("(e c) d -> c e d", e=E)[:, 4 * half:4 * half + 4, :])\
                  .then_inc(xe_loaded[half], 16)
            for half in range(2):
                sp.dma_start(ctxN[0:KC, 12 * half:12 * half + 12, :],
                             A["ctx"].rearrange("b (c p) d -> p (b c) d", p=KC)[:, 12 * half:12 * half + 12, :])\
                  .then_inc(ld_ctxN[half], 16)
            sp.dma_start(w1f, A["L1_ffn_W1"].rearrange("(k p) f -> p k f", p=P)).then_inc(ld["ffnw"], 16)
            for s in range(2):
                sp.dma_start(w2f[s][:, :, 0:D], A["L1_ffn_W2"].rearrange("(f p) o -> p f o", p=P))\
                  .then_inc(ld["ffnw"], 16)
            for e in range(E):
                wait_filled(("DN", e))
                if e + RING < E:
                    load_expert(e + RING)
                sp.wait_ge(*drained_at(("DN", e)))
                if e + 2 < E:
                    load_b2(e + 2)
                sp.dma_start(eo_dram[e * CAP:(e + 1) * CAP, :], eo[e % 2][:, :]).then_inc(eo_stored[e % 2], 16)
            sp.dma_start(maskr[0:S, :, :].rearrange("p b k -> p (b k)"),
                         A["mask"].partition_broadcast(S)).then_inc(ld["mask"], 16)

            for b in range(NB):
                sp.wait_ge(*drained_at(("F3", b)))
                sp.dma_start(out[b], outs[b % 2][0:S, :]).then_inc(stored[b % 2], 16)
            for n in range(2):
                sp.wait_ge(stored[n], 16 * NB // 2)


_INS = {
    "x": lambda v: v["x"],
    "ctx": lambda v: v["ctx_1024"],
    "ctxT": lambda v: v["ctx_1024"].reshape(NB * S2, D).T,
    "mask": lambda v: v["mask_BxS2_ff1"].reshape(-1),
    "L0_xattn_Wq": lambda v: v["L0_xattn_Wq"].T,
    "L0_xattn_Wk": lambda v: v["L0_xattn_Wk"].T,
    "L0_xattn_Wv": lambda v: v["L0_xattn_Wv"].T,
    "L0_xattn_Wo": lambda v: v["L0_xattn_Wo"].T,
    "L0_xattn_bq": lambda v: v["L0_xattn_bq"].reshape(DT, P).T,
    "L0_xattn_bk": lambda v: v["L0_xattn_bk"].reshape(DT, P).T,
    "L0_xattn_bv": lambda v: v["L0_xattn_bv"],
    "L0_xattn_bo": lambda v: v["L0_xattn_bo"],
    "L0_ffn_Wg": lambda v: v["L0_ffn_Wg"],
    "L0_ffn_W1": lambda v: v["L0_ffn_W1"],
    "L0_ffn_b1": lambda v: v["L0_ffn_b1"].reshape(E, FT, P).transpose(2, 0, 1),
    "L0_ffn_W2": lambda v: v["L0_ffn_W2"],
    "L0_ffn_b2": lambda v: v["L0_ffn_b2"],
    "L1_xattn_Wq": lambda v: v["L1_xattn_Wq"],
    "L1_xattn_Wk": lambda v: v["L1_xattn_Wk"].T,
    "L1_xattn_Wv": lambda v: v["L1_xattn_Wv"],
    "L1_xattn_bq": lambda v: v["L1_xattn_bq"].reshape(DT, P).T,
    "L1_xattn_bk": lambda v: v["L1_xattn_bk"].reshape(DT, P).T,
    "L1_xattn_bv": lambda v: v["L1_xattn_bv"],
    "L1_ffn_W1": lambda v: v["L1_ffn_W1"].T,
    "L1_ffn_b1": lambda v: v["L1_ffn_b1"].reshape(FT, P).T,
    "L1_ffn_W2": lambda v: v["L1_ffn_W2"].T,
    "L1_ffn_b2": lambda v: v["L1_ffn_b2"],
    "L1_ffn_scale": lambda v: v["L1_ffn_scale"].reshape(1),
}


def kernel(**inputs):
    import numpy as _np
    import concourse.bacc as _bacc
    from concourse import mybir as _mybir
    from concourse.bass_utils import run_bass_kernel_spmd as _run

    given = {n: _np.asarray(a) for n, a in inputs.items()}
    nc = _bacc.Bacc("TRN2", target_bir_lowering=False, num_devices=1)
    arrays, aps = {}, {}
    for name, lay in _INS.items():
        a = _np.ascontiguousarray(lay(given))
        arrays[f"in_{name}"] = a
        aps[name] = nc.dram_tensor(f"in_{name}", a.shape, _mybir.dt.from_np(a.dtype), kind="ExternalInput").ap()
    aps["out"] = nc.dram_tensor("out_dram", (NB, S, D), _mybir.dt.float32, kind="ExternalOutput").ap()
    build(nc, aps)
    r = _run(nc, [arrays], core_ids=[0])
    return r.results[0]["out_dram"]
```

```python
from contextlib import ExitStack

import numpy as np
import concourse.bass as bass
from concourse import mybir

ALU = mybir.AluOpType
ACT = mybir.ActivationFunctionType
F32 = mybir.dt.float32
BF16 = mybir.dt.bfloat16
I32 = mybir.dt.int32
AX = mybir.AxisListType

P = 128
NB, S, D = 8, 112, 256
S2, KC = 375, 125
NKC = S2 // KC
DT = D // P
H, DK = 16, 16
E, F = 8, 1024
FT = F // P
CAP = NB * S // E
T = NB * S
EPS = 1e-5
HG = 4
UNITS = NKC * (H // HG)
VW = DK + 1
ROWS = 6 * DK
Q_PIECES = (0, 1, 2, 0, 1, 0)
K_PIECES = (0, 1, 0, 1, 0, 2)
RING = 4

PIPE = {
    0: [("V0", -1), ("C6", 2)],
    1: [("D6", 2), ("K0", -3)],
    2: [("U", 1)],
    3: [("K1", -3), ("V1", -1)],
    4: [("C1", 1), ("SK0", -3)],
    5: [("C2", 1)],
    6: [("ND", -1), ("C3", 1), ("V2", -1)],
    7: [("SK1", -3)],
    8: [("NM", -1), ("L2", 1)],
    9: [("C4", 1), ("SK2", -3)],
    10: [("C5", 1)],
    11: [("D5", 1)],
}
FIRST_K = 3
POOL_K = 2
QW, QCHUNKS, FIRST_Q = 2 * S, NB // 2, 2
Q_UNITS = {7: "QX", 9: "QP", 11: "QS"}
MAX_FROM = 6


AT_STEPS = NB + 6
FFN_AT = 8


def steps():
    for i in range(-2, NB + 2):
        for u in range(UNITS):
            yield i, u


def max_heads(i, u):
    at = UNITS * i + u - MAX_FROM + 2 * UNITS
    for m in range(at * H // UNITS, (at + 1) * H // UNITS):
        if 0 <= m < NB * H:
            yield divmod(m, H)


def extras(i, u):
    for stage, behind in PIPE[u]:
        first = {"K": FIRST_K, "S": POOL_K, "V": 1}.get(stage[0], 0)
        if first <= i - behind < NB:
            yield stage, i - behind
    if u in Q_UNITS and FIRST_Q <= i + 3 < QCHUNKS:
        yield Q_UNITS[u], i + 3


def norm_orders():
    moments = [(n, b) for n in (1, 2) for b in range(NB)] + [(3, 0)]
    rows = [(n, b) for n in (1, 2) for b in range(NB)]
    for i in range(AT_STEPS):
        moments += [(3, i + 1)] * (i + 1 < NB)
        rows += [(4, i - 6)] * (i >= 6)
        rows += [(3, i)] * (i < NB)
        moments += [(4, i - 5)] * (0 <= i - 5 < NB)
    return ({k: n + 1 for n, k in enumerate(moments)}, {k: n + 1 for n, k in enumerate(rows)})


MOMENTS, ROWS_DONE = norm_orders()


def build(nc, A):
    out = A["out"]
    with ExitStack() as ctx:
        def sb(name, shape, dt=F32):
            return ctx.enter_context(nc.sbuf_tensor(name, shape, dt))

        def sem(name):
            return ctx.enter_context(nc.semaphore(name))

        k_dram = nc.dram_tensor("k_pieces_dram", (NB, 3, DT * P, S2), BF16).ap()
        q_dram = nc.dram_tensor("q_pieces_dram", (3, DT * P, T), BF16).ap()
        xg_dram = nc.dram_tensor("expert_in_dram", (2 * T, D), F32).ap()
        eo_dram = nc.dram_tensor("expert_out_dram", (T, D), F32).ap()

        ctxT = sb("ctxT", [P, DT, NB * S2])
        xres = sb("xres", [S, NB, D])
        xn = sb("xn", [S, NB, D])
        xT = sb("xT", [P, DT, T])
        w_in = sb("w_in", [P, 4, DT, D])
        ident = sb("ident", [P, P])
        identb = sb("identb", [P, P], BF16)
        wg = sb("wg", [P, DT, E])
        bcol = sb("bcol", [P, 5, DT])
        b1col = sb("b1col", [P, E, FT])
        fb1col = sb("fb1col", [P, FT])
        browL0 = sb("browL0", [S, D])
        browL1 = sb("browL1", [S, 2, D])
        mv = sb("mv", [S, NB, 2])
        stats = sb("stats", [S, NB, 6])
        veps = sb("veps", [S, NB])
        rstd = sb("rstd", [S, NB])
        neghalf = sb("neghalf", [S, NB])
        stackf = sb("stackf", [P, (3 * H * S2 + H * T) // 2])
        kstack = [stackf[:, n * H * S2 // 2:(n + 1) * H * S2 // 2].bitcast(BF16)
                  .rearrange("p (h k) -> p h k", h=H) for n in range(3)]
        qstack = stackf[:, 3 * H * S2 // 2:].bitcast(BF16).rearrange("p (h q) -> p h q", h=H)
        at = [0]

        def cut(region, n):
            a = at[0]
            at[0] += n
            assert at[0] <= region.shape[1], (at[0], region.shape)
            return region[:, a:a + n]

        ctxN = cut(stackf, NB * NKC * D).rearrange("p (c d) -> p c d", d=D)
        w_at1 = cut(stackf, 3 * DT * D).rearrange("p (w k e) -> p w k e", w=3, k=DT)
        w1f = cut(stackf, DT * F).rearrange("p (k f) -> p k f", k=DT)
        W2W = D + 16
        w2f = [cut(stackf, FT * W2W).rearrange("p (f o) -> p f o", f=FT) for _ in range(2)]
        hid = [cut(stackf, FT * S).rearrange("p (f s) -> p f s", f=FT) for _ in range(2)]
        bq_wide = cut(stackf, DT * S).rearrange("p (k s) -> p k s", k=DT)
        vones = [sb(f"vones{n}", [P, NKC, H, VW]) for n in range(2)]
        pT = [sb(f"pT{n}", [P, HG * S]) for n in range(3)]
        ctxU = sb("ctxU", [P, 4 * S])
        cc = sb("cc", [S, D])
        ccT = sb("ccT", [P, DT, S])
        mneg = sb("mneg", [S, 2, H])
        mpieces = sb("mpieces", [S, 2 * H], BF16)
        mT = sb("mT", [2 * H, S], BF16)
        rden = sb("rden", [S, H])
        tri = sb("tri", [S, S], BF16)
        onesb = sb("onesb", [S, S], BF16)
        em8 = sb("em8", [S, E])
        slot0 = sb("slot0", [S, E])
        spill = sb("spill", [S, NB])
        onehot = sb("onehot", [S, E], BF16)
        seen = sb("seen", [S, 2, E], BF16)
        lg = sb("lg", [S, E])
        ex = sb("ex", [S, E])
        small = sb("small", [S, 16])
        tmp8 = sb("tmp8", [S, 4, E])
        gate = sb("gate", [S, NB])
        idx_put = sb("idx_put", [S, NB], I32)
        idx_get = sb("idx_get", [S, NB], I32)
        ring = sb("ring", [P, RING, 2 * DT * F])
        w1e = [ring[:, n, 0:DT * F].rearrange("p (k f) -> p k f", k=DT) for n in range(RING)]
        w2e = [ring[:, n, DT * F:].rearrange("p (f o) -> p f o", f=FT) for n in range(RING)]
        stage = ring[:, 2:4, :].rearrange("p a n -> p (a n)")
        at[0] = 0
        kt = [cut(stage, DT * S2).rearrange("p (m k) -> p m k", m=DT) for _ in range(2)]
        kr = cut(stage, DT * S2).rearrange("p (m k) -> p m k", m=DT)
        kp = [cut(stage, 3 * DT * S2 // 2).bitcast(BF16).rearrange("p (c m k) -> p c m k", c=3, m=DT)
              for _ in range(2)]
        qt = [cut(stage, DT * QW).rearrange("p (m k) -> p m k", m=DT) for _ in range(2)]
        qr = cut(stage, DT * QW).rearrange("p (m k) -> p m k", m=DT)
        qp = [cut(stage, 3 * DT * QW // 2).bitcast(BF16).rearrange("p (c m k) -> p c m k", c=3, m=DT)
              for _ in range(2)]
        eo = [sb("eo0", [S, D]), cc]
        b2row = [sb(f"b2row{n}", [S, D]) for n in range(2)]
        late = ring[:, :, :].rearrange("p a n -> p (a n)")
        at[0] = 0
        wqk = cut(late, DT * D).rearrange("p (k e) -> p k e", k=DT)
        qk_bias = cut(late, 2 * DT)
        bqbk = cut(late, 1)
        qkT = [cut(late, DT * S).rearrange("p (k s) -> p k s", k=DT) for _ in range(2)]
        tq = [cut(late, 1) for _ in range(2)]
        maskr = cut(late, NB * S2).rearrange("p (b k) -> p b k", b=NB)
        sc = [cut(late, S2) for _ in range(2)]
        pr = [cut(late, S2) for _ in range(2)]
        pT1 = [cut(late, NKC * S).rearrange("p (c s) -> p c s", c=NKC) for _ in range(2)]
        uT = [cut(late, DT * S).rearrange("p (k s) -> p k s", k=DT) for _ in range(2)]
        sm1 = cut(late, 4 * NB).rearrange("p (b j) -> p b j", j=4)
        gT = [cut(late, FT * S).rearrange("p (f s) -> p f s", f=FT) for _ in range(2)]
        R = [cut(late, 4 * S).rearrange("p (j s) -> p j s", j=4) for _ in range(2)]
        Bm = [cut(late, D).rearrange("p (o r) -> p o r", r=4) for _ in range(2)]
        Bs = [cut(late, D // 4) for _ in range(2)]
        B2 = [cut(late, D).rearrange("p (j o) -> p j o", j=4) for _ in range(4)]
        G2 = [cut(late, 64) for _ in range(2)]
        G2T = [cut(late, S) for _ in range(2)]
        outs = [cut(late, D) for _ in range(2)]
        m1mask = sb("m1mask", [16, 4])
        sel2 = sb("sel2", [S, 64])
        maskR = sb("maskR", [64, 4])
        maskJ = sb("maskJ", [64, 4])
        scale_t = sb("scale_t", [64, 1])

        ps = ctx.enter_context(nc.psum_tensor("ps", [P, 8, 512], F32))

        def bank(n):
            return ps[:, n, :]

        filled = [sem(f"bank{n}_filled") for n in range(8)]
        drained = [sem(f"bank{n}_drained") for n in range(8)]
        fills, drains = [0] * 8, [0] * 8
        place = {}

        def filled_at(key):
            n, c, _ = place[key]
            return filled[n], c

        def drained_at(key):
            n, _, c = place[key]
            return drained[n], c

        ld = {n: sem(f"loaded_{n}") for n in
              ("wq", "wk", "wv", "wo", "bias", "wg", "b1", "rows",
               "at1w", "at1rows", "ffnw", "mask", "ffnb1", "scale")}
        ld_ctx = [sem(f"loaded_ctx{b}") for b in range(NB)]
        ld_ctxN = [sem(f"loaded_ctxN{n}") for n in range(2)]
        ld_ring = [sem(f"loaded_expert{n}") for n in range(RING)]
        ld_kstack = [sem(f"loaded_kstack{n}") for n in range(3)]
        ld_x = [sem(f"loaded_x{n}") for n in range(2)]
        ld_qstack = [sem(f"loaded_qstack{c}") for c in range(QCHUNKS)]
        ld_ones = sem("ones_of_other_stacks_placed")
        ld_b2 = [sem(f"loaded_b2row{n}") for n in range(2)]
        k_written = [sem(f"k_pieces_written{n}") for n in range(2)]
        q_written = [sem(f"q_pieces_written{n}") for n in range(2)]
        max_placed = sem("max_rows_placed")
        consts = sem("constants_ready")
        scaled = sem("masks_scaled")
        ones_ready = sem("ones_and_zeros_ready")
        var_ready = sem("variance_ready")
        rstd_ready = sem("rstd_ready")
        xn_ready = sem("normalised_ready")
        xbo_ready = sem("x_plus_bo_ready")
        k_high = sem("k_high_piece_ready")
        k_rest = sem("k_less_high_piece_ready")
        k_middle = sem("k_middle_piece_ready")
        k_split = sem("k_pieces_ready")
        q_high = sem("q_high_piece_ready")
        q_split = sem("q_pieces_ready")
        pv_units = sem("pv_units_done")
        max_ready = sem("max_pieces_ready")
        lg_ready = sem("logit_max_ready")
        esum_ready = sem("gate_sum_ready")
        onehot_ready = sem("onehot_ready")
        slots_ready = sem("slots_ready")
        zeroed = sem("expert_in_zeroed")
        put = sem("rows_put")
        xe_loaded = [sem(f"expert_rows_loaded{n}") for n in range(2)]
        eo_stored = [sem(f"expert_out_stored{n}") for n in range(2)]
        got_rows = [sem(f"rows_got{b}") for b in range(NB)]
        bq_ready = sem("bq_wide_ready")
        mask_ready = sem("mask_terms_ready")
        at_ready = sem("second_scores_ready")
        exp_ready = sem("second_probs_ready")
        xbv_ready = sem("x_plus_bv_ready")
        xb2_ready = sem("x_plus_b2_ready")
        bm_ready = sem("ffn_rank_rows_ready")
        w2_ready = sem("ffn_w2_columns_ready")
        gelu_ready = sem("gelu_ready")
        stored = [sem(f"out_stored{n}") for n in range(2)]
        dve = sem("dve_step")
        acts = sem("act_step")
        pools = sem("pool_step")

        block = ctx.enter_context(nc.Block())

        @block.tensor
        def _(pe):
            def open_bank(key, n, fill=1):
                if drains[n]:
                    pe.wait_ge(drained[n], drains[n])
                fills[n] += fill
                drains[n] += 1
                place[key] = (n, fills[n], drains[n])
                return bank(n)

            def read(key):
                pe.wait_ge(*drained_at(key))

            ring_bank = [0]

            def next_bank(banks):
                ring_bank[0] += 1
                return banks[ring_bank[0] % len(banks)]

            def transpose_x(key, b, n):
                o = open_bank((key, b), n)[:, 0:DT * S].rearrange("p (k s) -> p k s", k=DT)
                for k in range(DT):
                    mm = pe.transpose(o[:, k, :], xn[:, b, k * P:(k + 1) * P], ident[0:S, 0:S])
                mm.then_inc(filled[n], 1)

            def project_k(b, ms, banks):
                pe.wait_ge(ld_ctx[b], 16)
                for m in ms:
                    n = next_bank(banks)
                    o = open_bank(("K", b, m), n)
                    for k in range(DT):
                        mm = pe.matmul(o[:, 0:S2], w_in[:, 1, k, m * P:(m + 1) * P],
                                       ctxT[:, k, b * S2:(b + 1) * S2], start=k == 0, stop=k == DT - 1)
                    mm.then_inc(filled[n], 1)

            def turn_x(c, banks):
                pe.wait_ge(xn_ready, 2 * (c + 1))
                for b in (2 * c, 2 * c + 1):
                    transpose_x("XT1", b, next_bank(banks))

            def project_q(c, banks):
                for b in (2 * c, 2 * c + 1):
                    read(("XT1", b))
                for m in range(DT):
                    n = next_bank(banks)
                    o = open_bank(("Q", c, m), n)
                    for k in range(DT):
                        mm = pe.matmul(o[:, 0:QW], w_in[:, 0, k, m * P:(m + 1) * P],
                                       xT[:, k, c * QW:(c + 1) * QW], start=k == 0, stop=k == DT - 1)
                    mm.then_inc(filled[n], 1)

            def values(b, c):
                n = next_bank((6, 7))
                o = open_bank(("V", b, c), n)
                for k in range(DT):
                    mm = pe.matmul(o[0:KC, 0:D], ctxT[:, k, b * S2 + c * KC:b * S2 + (c + 1) * KC],
                                   w_in[:, 2, k, :], start=k == 0, stop=k == DT - 1)
                mm.then_inc(filled[n], 1)

            pe.wait_ge(consts, 1)
            for c in range(FIRST_Q):
                if c == 0:
                    pe.wait_ge(ld["wk"], 16)
                project_k(c, range(DT), range(4))
                turn_x(c, (6, 7))
                if c == 0:
                    pe.wait_ge(ld["wq"], 16)
                project_q(c, range(4))
            project_k(FIRST_K - 1, range(DT), range(4))
            pe.wait_ge(ld["wv"], 16)
            for c in range(NKC):
                values(0, c)

            def row_max(b, h):
                n = 2 + h % 2
                o = open_bank(("MX", b, h), n)
                pe.matmul(o[0:S, 0:S2], qstack[0:ROWS, h, b * S:(b + 1) * S], kstack[b % 3][0:ROWS, h, :],
                          start=True, stop=True).then_inc(filled[n], 1)

            def scores(b, u):
                c, g = divmod(u, H // HG)
                n = (UNITS * b + u) % 2
                o = open_bank(("ST", b, u), n)
                if u == 0:
                    pe.wait_ge(max_placed, 32 * (b + 1))
                    if b == 0:
                        pe.wait_ge(consts, 2)
                    if b == 1:
                        pe.wait_ge(ld_ones, 32)
                for j in range(HG):
                    h = HG * g + j
                    mm = pe.matmul(o[0:KC, j * S:(j + 1) * S], kstack[b % 3][0:ROWS + 2, h, c * KC:(c + 1) * KC],
                                   qstack[0:ROWS + 2, h, b * S:(b + 1) * S], start=True, stop=True)
                mm.then_inc(filled[n], 1)

            def weighted(b, u):
                c, g = divmod(u, H // HG)
                if u == 0:
                    open_bank(("PV", b), 4 + b % 2, fill=0)
                    if b == 0:
                        pe.wait_ge(ones_ready, 7)
                    for chunk in range(NKC):
                        read(("V", b, chunk))
                read(("ST", b, u))
                for j in range(HG):
                    h = HG * g + j
                    mm = pe.matmul(bank(4 + b % 2)[32 * j:32 * j + VW, g * S:(g + 1) * S],
                                   vones[b % 2][0:KC, c, h, :], pT[(UNITS * b + u) % 3][0:KC, j * S:(j + 1) * S],
                                   start=u == 0, stop=c == NKC - 1, skip_group_check=True)
                mm.then_inc(pv_units, 1)

            def post(stage, b):
                if stage in ("V0", "V1", "V2"):
                    values(b, int(stage[1]))
                elif stage == "QX":
                    turn_x(b, (6, 7))
                elif stage == "QP":
                    project_q(b, (6, 7))
                elif stage in ("K0", "K1"):
                    project_k(b, [int(stage[1])], (6, 7))
                elif stage == "NM":
                    pe.wait_ge(max_ready, b + 1)
                    n = next_bank((6, 7))
                    o = open_bank(("NM", b), n).bitcast(BF16)
                    pe.transpose(o[0:2 * H, 0:S], mpieces[:, :], identb[0:S, 0:S]).then_inc(filled[n], 1)
                elif stage == "C1":
                    read(("PV", b))
                    n = next_bank((6, 7))
                    o = open_bank(("C1", b), n)
                    for g in range(4):
                        mm = pe.transpose(o[0:S, g * P:(g + 1) * P], ctxU[:, g * S:(g + 1) * S], ident[:, :])
                    mm.then_inc(filled[n], 1)
                elif stage == "C2":
                    read(("C1", b))
                    n = next_bank((6, 7))
                    o = open_bank(("C2", b), n)[:, 0:DT * S].rearrange("p (k s) -> p k s", k=DT)
                    for k in range(DT):
                        mm = pe.transpose(o[:, k, :], cc[:, k * P:(k + 1) * P], ident[0:S, 0:S])
                    mm.then_inc(filled[n], 1)
                elif stage == "C3":
                    read(("C2", b))
                    n = next_bank((6, 7))
                    o = open_bank(("C3", b), n)
                    for k in range(DT):
                        mm = pe.matmul(o[0:S, 0:D], ccT[:, k, :], w_in[:, 3, k, :], start=k == 0, stop=k == DT - 1)
                    mm.then_inc(filled[n], 1)
                elif stage == "C4":
                    pe.wait_ge(xn_ready, NB + b + 1)
                    transpose_x("XT2", b, next_bank((6, 7)))
                elif stage == "C5":
                    read(("XT2", b))
                    n = next_bank((6, 7))
                    o = open_bank(("LG", b), n)
                    for k in range(DT):
                        mm = pe.matmul(o[0:S, 0:E], xT[:, k, b * S:(b + 1) * S], wg[:, k, :],
                                       start=k == 0, stop=k == DT - 1)
                    mm.then_inc(filled[n], 1)
                elif stage == "C6":
                    if b == 0:
                        pe.wait_ge(consts, 3)
                    pe.wait_ge(onehot_ready, b + 1)
                    n = next_bank((6, 7))
                    o = open_bank(("CUM", b), n)
                    pe.matmul(o[0:S, 0:E], tri[:, :], onehot[:, :], start=True, stop=False)
                    pe.matmul(o[0:S, 0:E], onesb[:, :], seen[:, b % 2, :], start=False, stop=True)\
                      .then_inc(filled[n], 1)

            pe.wait_ge(ld["wo"], 16)
            pe.wait_ge(ld["wg"], 16)
            for i, u in steps():
                if i < NB and i >= 0:
                    scores(i, u)
                before = UNITS * i + u - 2
                if 0 <= before < UNITS * NB:
                    weighted(*divmod(before, UNITS))
                for b, h in max_heads(i, u):
                    if h == 0:
                        pe.wait_ge(ld_kstack[b % 3], 96 * (b // 3 + 1))
                        if b % 2 == 0:
                            pe.wait_ge(ld_qstack[b // 2], 96)
                    row_max(b, h)
                for stage, b in extras(i, u):
                    if stage not in ("U", "L2", "ND", "SK0", "SK1", "SK2", "QS", "D5", "D6"):
                        post(stage, b)

            def expert_rows(e):
                n = 6 + e % 2
                pe.wait_ge(xe_loaded[e // 4], 16)
                transpose_x("XE", e, n)

            def expert_up(e):
                read(("XE", e))
                pe.wait_ge(ld_ring[e % RING], 32 * (e // RING + 1))
                for half in range(2):
                    n = 2 * (e % 2) + half
                    o = open_bank(("UP", e, half), n)
                    for f in range(4):
                        ft = 4 * half + f
                        for k in range(DT):
                            mm = pe.matmul(o[:, f * S:(f + 1) * S], w1e[e % RING][:, k, ft * P:(ft + 1) * P],
                                           xT[:, k, e * S:(e + 1) * S], start=k == 0, stop=k == DT - 1)
                    mm.then_inc(filled[n], 1)

            def expert_down(e):
                n = 4 + e % 2
                read(("UP", e, 0))
                read(("UP", e, 1))
                o = open_bank(("DN", e), n)
                for ft in range(FT):
                    mm = pe.matmul(o[0:S, 0:D], hid[e % 2][:, ft, :], w2e[e % RING][:, ft, :],
                                   start=ft == 0, stop=ft == FT - 1)
                mm.then_inc(filled[n], 1)

            for e in range(E + 1):
                if e == 0:
                    expert_rows(0)
                if e + 1 < E:
                    expert_rows(e + 1)
                if e < E:
                    expert_up(e)
                if e >= 1:
                    expert_down(e - 1)

            pe.wait_ge(ld["at1w"], 48)
            o = open_bank("WQK", 0)
            for m in range(DT):
                for k in range(DT):
                    mm = pe.matmul(o[:, m * D:(m + 1) * D], w_at1[:, 0, k, m * P:(m + 1) * P], w_at1[:, 1, k, :],
                                   start=k == 0, stop=k == DT - 1)
            mm.then_inc(filled[0], 1)
            pe.wait_ge(bq_ready, 1)
            o = open_bank("WQKB", 1)
            for side in range(2):
                for m in range(DT):
                    for k in range(DT):
                        pe.matmul(o[:, DT * side + m:DT * side + m + 1], w_at1[:, 1 - side, k, m * P:(m + 1) * P],
                                  bcol[:, 2 + side, k:k + 1], start=k == 0, stop=k == DT - 1)
            for k in range(DT):
                mm = pe.matmul(o[0:S, 2 * DT:2 * DT + 1], bq_wide[:, k, :], bcol[:, 3, k:k + 1],
                               start=k == 0, stop=k == DT - 1)
            mm.then_inc(filled[1], 1)

            def attend(stage, b):
                s = b % 2
                if stage == 0:
                    pe.wait_ge(xn_ready, ROWS_DONE[3, b])
                    transpose_x("XT3", b, 0)
                elif stage == 1:
                    if b == 0:
                        read("WQK")
                        read("WQKB")
                    read(("XT3", b))
                    o = open_bank(("QK", b), 1)
                    for m in range(DT):
                        for k in range(DT):
                            pe.matmul(o[:, m * S:(m + 1) * S], wqk[:, k, m * P:(m + 1) * P],
                                      xT[:, k, b * S:(b + 1) * S], start=k == 0, stop=k == DT - 1)
                    for k in range(DT):
                        mm = pe.matmul(o[0:S, 2 * S:2 * S + 1], xT[:, k, b * S:(b + 1) * S],
                                       qk_bias[:, DT + k:DT + k + 1], start=k == 0, stop=k == DT - 1)
                    mm.then_inc(filled[1], 1)
                elif stage == 2:
                    read(("QK", b))
                    o = open_bank(("S1", b), 2 + s)
                    for k in range(DT):
                        mm = pe.matmul(o[0:S, 0:S2], qkT[s][:, k, :], ctxT[:, k, b * S2:(b + 1) * S2],
                                       start=k == 0, stop=k == DT - 1)
                    mm.then_inc(filled[2 + s], 1)
                elif stage == 3:
                    pe.wait_ge(exp_ready, b + 1)
                    o = open_bank(("PT", b), 4)
                    for c in range(NKC):
                        mm = pe.transpose(o[0:KC, c * S:(c + 1) * S], pr[s][0:S, c * KC:(c + 1) * KC],
                                          ident[0:S, 0:S])
                    mm.then_inc(filled[4], 1)
                elif stage == 4:
                    read(("PT", b))
                    if b % 4 == 0:
                        pe.wait_ge(ld_ctxN[b // 4], 16)
                    o = open_bank(("UT", b), 5)
                    for m in range(DT):
                        for c in range(NKC):
                            mm = pe.matmul(o[:, m * S:(m + 1) * S], ctxN[0:KC, NKC * b + c, m * P:(m + 1) * P],
                                           pT1[s][0:KC, c, :], start=c == 0, stop=c == NKC - 1)
                    mm.then_inc(filled[5], 1)
                elif stage == 5:
                    read(("UT", b))
                    o = open_bank(("O1", b), 6)
                    for k in range(DT):
                        mm = pe.matmul(o[0:S, 0:D], uT[s][:, k, :], w_at1[:, 2, k, :],
                                       start=k == 0, stop=k == DT - 1)
                    mm.then_inc(filled[6], 1)
                elif stage == 6:
                    pe.wait_ge(xn_ready, ROWS_DONE[4, b])
                    transpose_x("XT4", b, 7)

            def ffn(stage, b):
                s = b % 2
                if stage == 0:
                    read(("XT4", b))
                    o = open_bank(("GR", b), 6)
                    for k in range(DT):
                        mm = pe.matmul(o[0:16, 0:S], xT[:, k, b * S + 1:b * S + 17], xT[:, k, b * S:(b + 1) * S],
                                       start=k == 0, stop=k == DT - 1)
                    mm.then_inc(filled[6], 1)
                    o = open_bank(("BS", b), 7)
                    pe.matmul(o[0:64, 0:D], sel2[:, :], xn[:, b, :], start=True, stop=True).then_inc(filled[7], 1)
                elif stage == 1:
                    if b == 0:
                        pe.wait_ge(ld["ffnw"], 48)
                    read(("GR", b))
                    for m in range(DT):
                        n = 2 * s + m
                        o = open_bank(("F1", b, m), n)
                        pe.matmul(o[:, 0:4 * S], xn[0:64, b, m * P:(m + 1) * P],
                                  R[s][0:64, :, :].rearrange("p j s -> p (j s)"),
                                  start=True, stop=False, skip_group_check=True)
                        for j in range(4):
                            ft = 2 * j + m
                            for k in range(DT):
                                mm = pe.matmul(o[:, j * S:(j + 1) * S], w1f[:, k, ft * P:(ft + 1) * P],
                                               xT[:, k, b * S:(b + 1) * S], start=False, stop=k == DT - 1,
                                               skip_group_check=True)
                        mm.then_inc(filled[n], 1)
                elif stage == 2:
                    pe.wait_ge(gelu_ready, FT * (b + 1))
                    pe.wait_ge(w2_ready, 2 * (b + 1))
                    n = 4 + s
                    o = open_bank(("F2", b), n)
                    for ft in range(FT):
                        mm = pe.matmul(o[0:S, 0:W2W], gT[s][:, ft, :], w2f[s][:, ft, :],
                                       start=ft == 0, stop=ft == FT - 1)
                    mm.then_inc(filled[n], 1)
                elif stage == 3:
                    read(("F2", b))
                    o = open_bank(("GT", b), 7)
                    pe.transpose(o[0:64, 0:S], G2[s][0:S, :], ident[0:S, 0:S]).then_inc(filled[7], 1)
                elif stage == 4:
                    read(("GT", b))
                    pe.wait_ge(bm_ready, b + 1)
                    n = place["F2", b][0]
                    fills[n] += 1
                    drains[n] += 1
                    place["F3", b] = (n, fills[n], drains[n])
                    pe.matmul(bank(n)[0:S, 0:D], G2T[s][0:64, :], B2[b % 4][0:64, :, :].rearrange("p j o -> p (j o)"),
                              start=False, stop=True, skip_group_check=True).then_inc(filled[n], 1)

            for i in range(FFN_AT + NB + 3):
                for stage in (5, 4, 6, 3, 2, 1, 0):
                    if 0 <= i - stage < NB:
                        attend(stage, i - stage)
                for stage, behind in ((1, 1), (3, 3), (0, 0), (2, 2), (4, 3)):
                    if 0 <= i - FFN_AT - behind < NB:
                        ffn(stage, i - FFN_AT - behind)

        @block.scalar
        def _(act):
            n_act = [0]

            def step(ins):
                n_act[0] += 1
                ins.then_inc(acts, 1)
                act.wait_ge(acts, n_act[0])

            def full(key):
                act.wait_ge(*filled_at(key))
                return bank(place[key][0]), drained[place[key][0]]

            act.dma_start(w_in[:, 1, :, :], A["L0_xattn_Wk"].rearrange("(k p) n -> p k n", p=P)).then_inc(ld["wk"], 16)
            act.dma_start(w_in[:, 0, :, :], A["L0_xattn_Wq"].rearrange("(k p) n -> p k n", p=P)).then_inc(ld["wq"], 16)
            act.dma_start(bcol[:, :, :], A["bias_columns"]).then_inc(ld["bias"], 16)
            act.dma_start(w_in[:, 2, :, :], A["L0_xattn_Wv"].rearrange("(k p) n -> p k n", p=P)).then_inc(ld["wv"], 16)
            act.dma_start(w_in[:, 3, :, :], A["L0_xattn_Wo"].rearrange("(k p) n -> p k n", p=P)).then_inc(ld["wo"], 16)
            act.dma_start(wg[:, :, :], A["L0_ffn_Wg"].rearrange("(k p) n -> p k n", p=P)).then_inc(ld["wg"], 16)
            act.dma_start(browL0[:, :], A["L0_xattn_bo"].partition_broadcast(S)).then_inc(ld["rows"], 16)
            act.dma_start(b1col[:, :, :], A["L0_ffn_b1"]).then_inc(ld["b1"], 16)
            act.dma_start(fb1col[:, :], A["L1_ffn_b1"]).then_inc(ld["ffnb1"], 16)

            def copy_xT(key, b):
                o, free = full((key, b))
                act.activation(xT[:, :, b * S:(b + 1) * S], o[:, 0:DT * S].rearrange("p (k s) -> p k s", k=DT),
                               ACT.Copy).then_inc(free, 1)

            def split_k(b, ms):
                if b >= 2:
                    act.wait_ge(k_split, b - 1)
                for m in ms:
                    o, free = full(("K", b, m))
                    act.activation(kt[b % 2][:, m, :], o[:, 0:S2], ACT.Identity, bias=bcol[:, 1, m:m + 1])\
                       .then_inc(free, 1)
                if DT - 1 not in ms:
                    return
                if b >= 2:
                    act.wait_ge(k_written[b % 2], 16 * (b // 2))
                for m in range(DT):
                    act.wait_ge(*drained_at(("K", b, m)))
                act.activation(kp[b % 2][:, 0, :, :], kt[b % 2][:, :, :], ACT.Copy).then_inc(k_high, 1)

            def split_q(c):
                if c >= 2:
                    act.wait_ge(q_split, c - 1)
                for m in range(DT):
                    o, free = full(("Q", c, m))
                    act.activation(qt[c % 2][:, m, :], o[:, 0:QW], ACT.Identity, bias=bcol[:, 0, m:m + 1])\
                       .then_inc(free, 1)
                if c >= 2:
                    act.wait_ge(q_written[c % 2], 16 * (c // 2))
                for m in range(DT):
                    act.wait_ge(*drained_at(("Q", c, m)))
                act.activation(qp[c % 2][:, 0, :, :], qt[c % 2][:, :, :], ACT.Copy).then_inc(q_high, 1)

            def copy_chunk(c):
                for b in (2 * c, 2 * c + 1):
                    copy_xT("XT1", b)

            def copy_v(b, c):
                if c == 0 and b >= 2:
                    act.wait_ge(pv_units, UNITS * (b - 1))
                o, free = full(("V", b, c))
                act.activation(vones[b % 2][0:KC, c, :, 0:DK],
                               o[0:KC, 0:D].rearrange("p (h w) -> p h w", h=H), ACT.Copy).then_inc(free, 1)

            act.wait_ge(ld["bias"], 16)
            for c in range(FIRST_Q):
                split_k(c, range(DT))
                copy_chunk(c)
                split_q(c)
            split_k(FIRST_K - 1, range(DT))
            for c in range(NKC):
                copy_v(0, c)

            def exps(b, u):
                w = UNITS * b + u
                o, free = full(("ST", b, u))
                if w >= 3:
                    act.wait_ge(pv_units, w - 2)
                act.activation(pT[w % 3][0:KC, :], o[0:KC, 0:HG * S], ACT.Exp, scale=DK ** -0.5).then_inc(free, 1)

            def post(stage, b):
                if stage == "U":
                    act.wait_ge(pv_units, UNITS * (b + 1))
                    if b:
                        act.wait_ge(*filled_at(("C1", b - 1)))
                    act.activation(ctxU[:, :], bank(4 + b % 2)[:, 0:4 * S], ACT.Copy)\
                       .then_inc(drained[4 + b % 2], 1)
                elif stage in ("V0", "V1", "V2"):
                    copy_v(b, int(stage[1]))
                elif stage in ("K0", "K1"):
                    split_k(b, [int(stage[1])])
                elif stage == "QX":
                    copy_chunk(b)
                elif stage == "QP":
                    split_q(b)
                elif stage == "SK1":
                    act.wait_ge(k_rest, b - POOL_K + 1)
                    act.activation(kp[b % 2][:, 1, :, :], kr[:, :, :], ACT.Copy).then_inc(k_middle, 1)
                elif stage == "C2":
                    o, free = full(("C2", b))
                    for k in range(DT):
                        ins = act.activation(ccT[:, k, :], o[:, k * S:(k + 1) * S], ACT.Identity,
                                             bias=bcol[:, 4, k:k + 1])
                    ins.then_inc(free, 1)
                elif stage == "NM":
                    o, free = full(("NM", b))
                    if b:
                        act.wait_ge(max_placed, 32 * b)
                    act.activation(mT[:, :], o.bitcast(BF16)[0:2 * H, 0:S], ACT.Copy).then_inc(free, 1)
                elif stage == "C4":
                    copy_xT("XT2", b)
                elif stage == "C5":
                    act.wait_ge(lg_ready, b + 1)
                    act.activation(ex[:, :], lg[:, :], ACT.Exp, bias=small[:, 0:1], accum_out=small[:, 1:2])\
                       .then_inc(esum_ready, 1)

            for i, u in steps():
                if 0 <= i < NB:
                    exps(i, u)
                for stage, b in extras(i, u):
                    if stage in ("V0", "V1", "V2", "K0", "K1", "SK1", "QX", "QP", "U", "C2", "NM", "C4", "C5"):
                        post(stage, b)

            def hidden(e):
                if e >= 2:
                    act.wait_ge(*filled_at(("DN", e - 2)))
                o, free = full(("UP", e, 0))
                for f in range(4):
                    ins = act.activation(hid[e % 2][:, f, :], o[:, f * S:(f + 1) * S], ACT.Relu,
                                         bias=b1col[:, e, f:f + 1])
                ins.then_inc(free, 1)

            act.wait_ge(ld["b1"], 16)
            for e in range(E):
                if e == 0:
                    copy_xT("XE", 0)
                if e + 1 < E:
                    copy_xT("XE", e + 1)
                hidden(e)

            def attend(stage, b):
                s = b % 2
                if stage == 0:
                    copy_xT("XT3", b)
                elif stage == 1:
                    if b == 0:
                        act.wait_ge(*drained_at("WQKB"))
                    if b >= 2:
                        act.wait_ge(*drained_at(("S1", b - 2)))
                    o, free = full(("QK", b))
                    act.activation(tq[s][0:S, :], o[0:S, 2 * S:2 * S + 1], ACT.Identity, bias=bqbk[0:S, :])
                    for m in range(DT):
                        ins = act.activation(qkT[s][:, m, :], o[:, m * S:(m + 1) * S], ACT.Identity,
                                             bias=qk_bias[:, m:m + 1])
                    ins.then_inc(free, 1)
                elif stage == 2:
                    act.wait_ge(at_ready, b + 1)
                    if b >= 2:
                        act.wait_ge(*filled_at(("PT", b - 2)))
                    act.activation(pr[s][0:S, :], sc[s][0:S, :], ACT.Exp, bias=sm1[0:S, b, 1:2],
                                   scale=DK ** -0.5, accum_out=sm1[0:S, b, 2:3]).then_inc(exp_ready, 1)
                elif stage == 3:
                    o, free = full(("PT", b))
                    if b >= 2:
                        act.wait_ge(*filled_at(("UT", b - 2)))
                    act.activation(pT1[s][0:KC, :, :], o[0:KC, 0:NKC * S].rearrange("p (c s) -> p c s", c=NKC),
                                   ACT.Copy).then_inc(free, 1)
                elif stage == 4:
                    if b >= 2:
                        act.wait_ge(*filled_at(("O1", b - 2)))
                    o, free = full(("UT", b))
                    act.activation(uT[s][:, :, :], o[:, 0:DT * S].rearrange("p (k s) -> p k s", k=DT),
                                   ACT.Copy).then_inc(free, 1)
                elif stage == 6:
                    copy_xT("XT4", b)

            def gelu(b):
                if b == 0:
                    act.wait_ge(ld["ffnb1"], 16)
                if b >= 2:
                    act.wait_ge(*filled_at(("F2", b - 2)))
                for half in range(2):
                    o, free = full(("F1", b, half))
                    for f in range(4):
                        ft = 2 * f + half
                        act.activation(gT[b % 2][:, ft, :], o[:, f * S:(f + 1) * S], ACT.Gelu,
                                       bias=fb1col[:, ft:ft + 1]).then_inc(gelu_ready, 1)
                    act.wait_ge(gelu_ready, FT * b + 4 * half + 4)
                    act.sem_inc(free, 1)

            o, free = full("WQK")
            act.activation(wqk[:, :, :], o[:, 0:DT * D].rearrange("p (k e) -> p k e", k=DT), ACT.Copy)\
               .then_inc(free, 1)
            o, free = full("WQKB")
            act.activation(qk_bias[:, :], o[:, 0:2 * DT], ACT.Copy)
            act.activation(bqbk[0:S, :], o[0:S, 2 * DT:2 * DT + 1], ACT.Copy).then_inc(free, 1)
            for i in range(FFN_AT + NB + 1):
                for stage in (4, 6, 3, 1, 0, 2):
                    if 0 <= i - stage < NB:
                        attend(stage, i - stage)
                if 0 <= i - FFN_AT - 1 < NB:
                    gelu(i - FFN_AT - 1)

        @block.vector
        def _(v):
            n_dve = [0]

            def step(ins):
                n_dve[0] += 1
                ins.then_inc(dve, 1)
                v.wait_ge(dve, n_dve[0])

            def full(key):
                v.wait_ge(*filled_at(key))
                return bank(place[key][0]), drained[place[key][0]]

            def drained_by_me(key):
                v.wait_ge(*drained_at(key))

            def moments(b):
                step(v.bn_stats(stats[:, b, :], xres[:, b, :]))
                step(v.bn_aggr(mv[:, b, :], stats[:, b, :]))
                v.tensor_scalar(veps[:, b:b + 1], mv[:, b, 1:2], EPS, None, ALU.add).then_inc(var_ready, 1)

            def normalise(norm, b):
                v.wait_ge(rstd_ready, MOMENTS[norm, b])
                v.tensor_scalar(xn[:, b, :], xres[:, b, :], mv[:, b, 0:1], rstd[:, b:b + 1],
                                ALU.subtract, ALU.mult).then_inc(xn_ready, 1)

            def split_k(b):
                v.wait_ge(k_high, b + 1)
                step(v.tensor_tensor(kr[:, :, :], kt[b % 2][:, :, :], kp[b % 2][:, 0, :, :], ALU.subtract))
                step(v.tensor_copy(kp[b % 2][:, 1, :, :], kr[:, :, :]))
                v.tensor_tensor(kp[b % 2][:, 2, :, :], kr[:, :, :], kp[b % 2][:, 1, :, :], ALU.subtract)\
                 .then_inc(k_split, 1)
                v.wait_ge(k_split, b + 1)

            def split_q(c):
                v.wait_ge(q_high, c + 1)
                step(v.tensor_tensor(qr[:, :, :], qt[c % 2][:, :, :], qp[c % 2][:, 0, :, :], ALU.subtract))
                step(v.tensor_copy(qp[c % 2][:, 1, :, :], qr[:, :, :]))
                v.tensor_tensor(qp[c % 2][:, 2, :, :], qr[:, :, :], qp[c % 2][:, 1, :, :], ALU.subtract)\
                 .then_inc(q_split, 1)
                v.wait_ge(q_split, c + 1)

            v.memset(neghalf[:, :], -0.5).then_inc(ones_ready, 1)
            v.memset(eo[0][:, :], 0.0).then_inc(ones_ready, 1)
            v.memset(vones[0][:, :, :, DK:VW], 1.0).then_inc(ones_ready, 1)
            v.memset(vones[1][:, :, :, DK:VW], 1.0).then_inc(ones_ready, 1)
            for n in (4, 5):
                v.memset(bank(n)[:, :], 0.0).then_inc(ones_ready, 1)
            v.memset(seen[:, :, :], 0.0).then_inc(ones_ready, 1)
            for n, group in enumerate((range(0, 2), range(2, 4))):
                v.wait_ge(ld_x[n], 16)
                for b in group:
                    moments(b)
                for b in group:
                    normalise(1, b)
            for b in range(4, NB):
                moments(b)
            split_k(0)
            split_q(0)
            for b in range(4, NB):
                normalise(1, b)
            split_k(1)
            split_q(1)
            v.wait_ge(ones_ready, 7)

            def row_max(b, h):
                o, free = full(("MX", b, h))
                v.tensor_reduce(mneg[:, b % 2, h:h + 1], o[0:S, 0:S2], AX.X, ALU.max, negate=True).then_inc(free, 1)

            def post(stage, b):
                if stage == "QS":
                    split_q(b)
                elif stage == "ND":
                    for h in (H - 2, H - 1):
                        drained_by_me(("MX", b, h))
                    if b:
                        v.wait_ge(*filled_at(("NM", b - 1)))
                    step(v.tensor_copy(mpieces[:, 0:H], mneg[:, b % 2, :]))
                    v.tensor_tensor(mpieces[:, H:2 * H], mneg[:, b % 2, :], mpieces[:, 0:H], ALU.subtract)\
                     .then_inc(max_ready, 1)
                    v.wait_ge(max_ready, b + 1)
                elif stage == "C1":
                    o, free = full(("C1", b))
                    o = o[0:S, :].rearrange("p (h w) -> p h w", h=H)
                    step(v.reciprocal(rden[:, :], o[:, :, DK]))
                    if b:
                        v.wait_ge(*filled_at(("C2", b - 1)))
                    v.tensor_tensor(cc[:, :].rearrange("p (h w) -> p h w", h=H), o[:, :, 0:DK],
                                    rden[:, :].unsqueeze(2).broadcast_to([S, H, DK]), ALU.mult)\
                     .then_inc(free, 1)
                elif stage == "C3":
                    o, free = full(("C3", b))
                    v.wait_ge(xbo_ready, NB)
                    v.tensor_tensor(xres[:, b, :], o[0:S, 0:D], xres[:, b, :], ALU.add).then_inc(free, 1)
                    drained_by_me(("C3", b))
                    moments(b)
                elif stage == "L2":
                    normalise(2, b)
                elif stage == "C5":
                    o, free = full(("LG", b))
                    if b:
                        v.wait_ge(esum_ready, b)
                    else:
                        v.wait_ge(consts, 3)
                    v.tensor_copy(lg[:, :], o[0:S, 0:E]).then_inc(free, 1)
                    drained_by_me(("LG", b))
                    v.tensor_reduce(small[:, 0:1], lg[:, :], AX.X, ALU.max, negate=True).then_inc(lg_ready, 1)
                elif stage == "D5":
                    v.wait_ge(lg_ready, b + 1)
                    step(v.tensor_scalar(tmp8[:, 0, :], lg[:, :], small[:, 0:1], 0.0, ALU.add, ALU.is_equal))
                    step(v.tensor_tensor(tmp8[:, 1, :], tmp8[:, 0, :], em8[:, :], ALU.mult))
                    step(v.tensor_reduce(small[:, 2:3], tmp8[:, 1, :], AX.X, ALU.min))
                    v.tensor_scalar(onehot[:, :], tmp8[:, 1, :], small[:, 2:3], None, ALU.is_equal)\
                     .then_inc(onehot_ready, 1)
                    v.wait_ge(onehot_ready, b + 1)
                    step(v.tensor_tensor(seen[:, (b + 1) % 2, :], seen[:, b % 2, :], onehot[:, :], ALU.add))
                elif stage == "C6":
                    o, free = full(("CUM", b))
                    v.tensor_copy(tmp8[:, 2, :], o[0:S, 0:E]).then_inc(free, 1)
                    drained_by_me(("CUM", b))
                    step(v.scalar_tensor_tensor(tmp8[:, 0, :], tmp8[:, 2, :], float(CAP), onehot[:, :],
                                                ALU.is_le, ALU.mult))
                    step(v.tensor_tensor(tmp8[:, 3, :], tmp8[:, 2, :], slot0[:, :], ALU.add))
                elif stage == "D6":
                    step(v.tensor_tensor(tmp8[:, 1, :], tmp8[:, 3, :], onehot[:, :], ALU.mult))
                    step(v.tensor_reduce(small[:, 3:5], tmp8[:, 0:2, :], AX.X, ALU.add))
                    v.tensor_scalar(idx_get[:, b:b + 1], small[:, 4:5], small[:, 3:4], None, ALU.mult)
                    step(v.tensor_scalar(small[:, 5:6], small[:, 4:5], spill[:, b:b + 1], small[:, 3:4],
                                         ALU.subtract, ALU.mult))
                    v.tensor_scalar(idx_put[:, b:b + 1], small[:, 5:6], spill[:, b:b + 1], None, ALU.add)\
                     .then_inc(slots_ready, 1)
                    v.wait_ge(esum_ready, b + 1)
                    step(v.reciprocal(small[:, 6:7], small[:, 1:2]))
                    step(v.tensor_scalar(gate[:, b:b + 1], small[:, 6:7], small[:, 3:4], None, ALU.mult))

            for i, u in steps():
                for b, h in max_heads(i, u):
                    row_max(b, h)
                for stage, b in extras(i, u):
                    if stage in ("QS", "ND", "C1", "C3", "L2", "C5", "D5", "C6", "D6"):
                        post(stage, b)

            v.wait_ge(ld["b1"], 16)
            v.wait_ge(*filled_at(("ST", NB - 1, UNITS - 1)))
            v.tensor_copy(bq_wide[:, :, :], bcol[:, 2, :].unsqueeze(2).broadcast_to([P, DT, S]))\
             .then_inc(bq_ready, 1)

            def finish(e):
                o, free = full(("DN", e))
                v.wait_ge(ld_b2[e % 2], 16 * (e // 2 + 1))
                if e >= 2:
                    v.wait_ge(eo_stored[e % 2], 16 * (e // 2))
                v.tensor_tensor(eo[e % 2][:, :], o[0:S, 0:D], b2row[e % 2][:, :], ALU.add).then_inc(free, 1)

            for e in range(E):
                if e >= 2:
                    v.wait_ge(*filled_at(("DN", e - 2)))
                o, free = full(("UP", e, 1))
                for f in range(4):
                    ins = v.tensor_scalar(hid[e % 2][:, 4 + f, :], o[:, f * S:(f + 1) * S],
                                          b1col[:, e, 4 + f:5 + f], 0.0, ALU.add, ALU.max)
                ins.then_inc(free, 1)
                if e:
                    finish(e - 1)
            finish(E - 1)

            def combine(b):
                v.wait_ge(got_rows[b], 16)
                step(v.scalar_tensor_tensor(xres[:, b, :], xn[:, b, :], gate[:, b:b + 1], xres[:, b, :],
                                            ALU.mult, ALU.add))
                moments(b)

            def attend(stage, b):
                s = b % 2
                if stage == 2:
                    o, free = full(("S1", b))
                    v.wait_ge(mask_ready, b + 1)
                    if b >= 2:
                        v.wait_ge(exp_ready, b - 1)
                    v.scalar_tensor_tensor(sc[s][0:S, :], o[0:S, 0:S2], tq[s][0:S, :], maskr[0:S, b, :],
                                           ALU.add, ALU.add).then_inc(free, 1)
                    drained_by_me(("S1", b))
                    step(v.tensor_reduce(sm1[0:S, b, 0:1], sc[s][0:S, :], AX.X, ALU.max, negate=True))
                    v.tensor_scalar(sm1[0:S, b, 1:2], sm1[0:S, b, 0:1], DK ** -0.5, None, ALU.mult)\
                     .then_inc(at_ready, 1)
                elif stage == 5:
                    v.wait_ge(exp_ready, b + 1)
                    step(v.reciprocal(sm1[0:S, b, 3:4], sm1[0:S, b, 2:3]))
                    o, free = full(("O1", b))
                    v.wait_ge(xbv_ready, b + 1)
                    v.scalar_tensor_tensor(xres[:, b, :], o[0:S, 0:D], sm1[0:S, b, 3:4], xres[:, b, :],
                                           ALU.mult, ALU.add).then_inc(free, 1)
                    drained_by_me(("O1", b))
                    moments(b)

            def clear_ffn():
                v.wait_ge(scaled, 2)
                v.wait_ge(ld["ffnw"], 48)
                for s in range(2):
                    step(v.memset(R[s][0:64, :, :], 0.0))
                    step(v.memset(G2[s][0:S, :], 0.0))
                    step(v.memset(w2f[s][:, :, D:W2W], 0.0))

            def ffn(stage, b):
                s = b % 2
                if stage == 0:
                    if b >= 2:
                        for half in range(2):
                            v.wait_ge(*filled_at(("F1", b - 2, half)))
                    o, free = full(("GR", b))
                    v.tensor_tensor(R[s][0:16, :, :], o[0:16, 0:S].unsqueeze(1).broadcast_to([16, 4, S]),
                                    m1mask[:, :].unsqueeze(2).broadcast_to([16, 4, S]), ALU.mult).then_inc(free, 1)
                    o, free = full(("BS", b))
                    v.tensor_tensor(Bm[s][0:64, :, :], o[0:64, 0:D].rearrange("p (o r) -> p o r", r=4),
                                    maskR[:, :].unsqueeze(1).broadcast_to([64, D // 4, 4]), ALU.mult)\
                     .then_inc(free, 1)
                    drained_by_me(("BS", b))
                    step(v.tensor_reduce(Bs[s][0:64, :], Bm[s][0:64, :, :], AX.X, ALU.add))
                    if b >= 4:
                        v.wait_ge(*filled_at(("F3", b - 4)))
                    v.tensor_tensor(B2[b % 4][0:64, :, :], Bs[s][0:64, :].unsqueeze(1).broadcast_to([64, 4, D // 4]),
                                    maskJ[:, :].unsqueeze(2).broadcast_to([64, 4, D // 4]), ALU.mult)\
                     .then_inc(bm_ready, 1)
                    if b >= 2:
                        v.wait_ge(*filled_at(("F2", b - 2)))
                    for m in range(DT):
                        cols = w2f[s][:, :, D:W2W].rearrange("p (r m) (a j) -> p m r a j", m=DT, a=4)[:, m]
                        for r in range(4):
                            ins = v.tensor_copy(cols[:, r, r, :], xT[:, m, b * S + 10:b * S + 17:2])
                        ins.then_inc(w2_ready, 1)
                elif stage == 3:
                    if b >= 2:
                        v.wait_ge(*filled_at(("GT", b - 2)))
                    o, free = full(("F2", b))
                    v.tensor_copy(G2[s][0:S, 0:16], o[0:S, D:W2W]).then_inc(free, 1)
                elif stage == 5:
                    o, free = full(("GT", b))
                    v.tensor_copy(G2T[s][0:64, :], o[0:64, 0:S]).then_inc(free, 1)
                elif stage == 4:
                    o, free = full(("F3", b))
                    v.wait_ge(xb2_ready, b + 1)
                    if b >= 2:
                        v.wait_ge(stored[s], 16 * (b // 2))
                    v.tensor_tensor(outs[s][0:S, :], o[0:S, 0:D], xres[:, b, :], ALU.add).then_inc(free, 1)

            combine(0)
            for i in range(FFN_AT + NB + 3):
                if i + 1 < NB:
                    combine(i + 1)
                if 0 <= i - 6 < NB:
                    normalise(4, i - 6)
                if i < NB:
                    normalise(3, i)
                for stage in (5, 2):
                    if 0 <= i - stage < NB:
                        attend(stage, i - stage)
                if i == FFN_AT - 1:
                    clear_ffn()
                for stage, behind in ((5, 3), (0, 0), (3, 2), (4, 3)):
                    if 0 <= i - FFN_AT - behind < NB:
                        ffn(stage, i - FFN_AT - behind)

        @block.gpsimd
        def _(g):
            n_pool = [0]

            def step(ins):
                n_pool[0] += 1
                ins.then_inc(pools, 1)
                g.wait_ge(pools, n_pool[0])

            def root(norm, b):
                g.wait_ge(var_ready, MOMENTS[norm, b])
                g.tensor_tensor(rstd[:, b:b + 1], veps[:, b:b + 1], neghalf[:, b:b + 1], ALU.pow)\
                 .then_inc(rstd_ready, 1)

            def diagonal(ap, base, pattern, cm):
                step(g.affine_select(out=ap, in_=ap, compare_op=ALU.not_equal, fill=1.0, base=base,
                                     pattern=pattern, channel_multiplier=cm))

            step(g.memset(ident[:, :], 0.0))
            diagonal(ident[:, :], 0, [[-1, P]], 1)
            g.tensor_copy(identb[:, :], ident[:, :]).then_inc(consts, 1)
            g.wait_ge(ones_ready, 1)
            for b in range(NB):
                root(1, b)
            g.wait_ge(rstd_ready, NB)
            g.memset(kstack[0][96:98, :, :], 1.0).then_inc(consts, 1)
            g.wait_ge(consts, 2)
            for n in range(1, 3):
                g.dma_start(kstack[n][96:98, :, :], kstack[0][96:98, :, :]).then_inc(ld_ones, 16)
            step(g.memset(onesb[:, :], 1.0))
            step(g.affine_select(out=tri[:, :], in_=onesb[:, :], compare_op=ALU.is_ge, fill=0.0, base=0,
                                 pattern=[[1, S]], channel_multiplier=-1))
            step(g.iota(em8[:, :], pattern=[[1, E]], base=-E, channel_multiplier=0,
                        allow_small_or_imprecise_dtypes=True))
            step(g.iota(slot0[:, :], pattern=[[CAP, E]], base=-1, channel_multiplier=0,
                        allow_small_or_imprecise_dtypes=True))
            g.iota(spill[:, :], pattern=[[S, NB]], base=T, channel_multiplier=1,
                   allow_small_or_imprecise_dtypes=True).then_inc(consts, 1)
            g.wait_ge(xn_ready, NB)
            g.wait_ge(ld["rows"], 16)
            for b in range(NB):
                g.tensor_tensor(xres[:, b, :], xres[:, b, :], browL0[:, :], ALU.add).then_inc(xbo_ready, 1)
            g.wait_ge(xbo_ready, NB)
            step(g.memset(m1mask[:, :], 0.0))
            diagonal(m1mask[:, :], -1, [[-2, 4]], 1)
            step(g.memset(sel2[:, :], 0.0))
            diagonal(sel2[:, 0:16].rearrange("p (r j) -> p r j", r=4), -9, [[0, 4], [-2, 4]], 1)
            step(g.memset(maskJ[:, :], 0.0))
            for r in range(4):
                diagonal(maskJ[:, :], -4 * r, [[-1, 4]], 1)
            step(g.memset(maskR[:, :], 1.0))
            step(g.affine_select(out=maskR[:, :], in_=maskR[:, :], compare_op=ALU.is_ge, fill=0.0, base=0,
                                 pattern=[[-4, 4]], channel_multiplier=1))
            step(g.affine_select(out=maskR[:, :], in_=maskR[:, :], compare_op=ALU.is_ge, fill=0.0, base=3,
                                 pattern=[[4, 4]], channel_multiplier=-1))
            g.wait_ge(ld["scale"], 16)
            g.tensor_scalar(m1mask[:, :], m1mask[:, :], scale_t[0:16, :], None, ALU.mult).then_inc(scaled, 1)
            g.tensor_scalar(maskJ[:, :], maskJ[:, :], scale_t[:, :], None, ALU.mult).then_inc(scaled, 1)

            for i, u in steps():
                for stage, b in extras(i, u):
                    if stage == "C3":
                        root(2, b)
                    elif stage == "SK0":
                        g.wait_ge(k_high, b + 1)
                        g.wait_ge(k_split, b)
                        g.tensor_tensor(kr[:, :, :], kt[b % 2][:, :, :], kp[b % 2][:, 0, :, :], ALU.subtract)\
                         .then_inc(k_rest, 1)
                    elif stage == "SK2":
                        g.wait_ge(k_middle, b - POOL_K + 1)
                        g.tensor_tensor(kp[b % 2][:, 2, :, :], kr[:, :, :], kp[b % 2][:, 1, :, :], ALU.subtract)\
                         .then_inc(k_split, 1)
                    elif stage == "D6":
                        if b == 0:
                            g.wait_ge(zeroed, 16)
                        g.wait_ge(slots_ready, b + 1)
                        g.indirect_dma_start(out=xg_dram, out_offset=bass.IndirectOffsetOnAxis(
                            ap=idx_put[:, b:b + 1], axis=0), in_=xn[:, b, :], in_offset=None).then_inc(put, 16)

            for n in range(2):
                g.wait_ge(eo_stored[n], 16 * E // 2)
            for b in range(NB):
                g.indirect_dma_start(out=xn[:, b, :], out_offset=None, in_=eo_dram,
                                     in_offset=bass.IndirectOffsetOnAxis(ap=idx_get[:, b:b + 1], axis=0))\
                 .then_inc(got_rows[b], 16)

            g.wait_ge(ld["at1rows"], 32)
            def plus(b, r, s):
                g.tensor_tensor(xres[:, b, :], xres[:, b, :], browL1[:, r, :], ALU.add).then_inc(s, 1)

            root(3, 0)
            for i in range(AT_STEPS):
                if i + 1 < NB:
                    root(3, i + 1)
                if 0 <= i - 5 < NB:
                    root(4, i - 5)
                if i < NB:
                    g.wait_ge(xn_ready, ROWS_DONE[3, i])
                    plus(i, 0, xbv_ready)
                    if i == 0:
                        g.wait_ge(ld["mask"], 16)
                    g.tensor_scalar(maskr[0:S, i, :], maskr[0:S, i, :], 40000.0, -40000.0, ALU.mult, ALU.add)\
                     .then_inc(mask_ready, 1)
                if 0 <= i - 6 < NB:
                    g.wait_ge(xn_ready, ROWS_DONE[4, i - 6])
                    plus(i - 6, 1, xb2_ready)

        @block.sync
        def _(sp):
            def wait_filled(key):
                sp.wait_ge(*filled_at(key))

            def kp_of(name, **kw):
                return A[name].rearrange("(k p) n -> p k n", p=P)

            def load_ctx(b):
                sp.dma_start(ctxT[:, :, b * S2:(b + 1) * S2],
                             A["ctxT"].rearrange("(k p) t -> p k t", p=P)[:, :, b * S2:(b + 1) * S2])\
                  .then_inc(ld_ctx[b], 16)

            def load_expert(e, parts=(0, 1)):
                n = e % RING
                if 0 in parts:
                    sp.dma_start(w1e[n], A["L0_ffn_W1"][e].rearrange("(k p) f -> p k f", p=P))\
                      .then_inc(ld_ring[n], 16)
                if 1 in parts:
                    sp.dma_start(w2e[n], A["L0_ffn_W2"][e].rearrange("(f p) o -> p f o", p=P))\
                      .then_inc(ld_ring[n], 16)

            def load_b2(e):
                sp.dma_start(b2row[e % 2][:, :], A["L0_ffn_b2"][e].partition_broadcast(S)).then_inc(ld_b2[e % 2], 16)

            for n, (b0, b1) in enumerate(((0, 2), (2, NB))):
                sp.dma_start(xres[:, b0:b1, :], A["x"].rearrange("b s d -> s b d")[:, b0:b1, :]).then_inc(ld_x[n], 16)
                if n == 0:
                    load_ctx(0)
            for b in range(1, 4):
                load_ctx(b)

            def write_k(b):
                sp.wait_ge(k_split, b + 1)
                sp.dma_start(k_dram[b].rearrange("c (m p) k -> p c m k", p=P), kp[b % 2][:, :, :, :])\
                  .then_inc(k_written[b % 2], 16)

            def write_q(c):
                sp.wait_ge(q_split, c + 1)
                sp.dma_start(q_dram.rearrange("c (m p) t -> p c m t", p=P)[:, :, :, c * QW:(c + 1) * QW],
                             qp[c % 2][:, :, :, :]).then_inc(q_written[c % 2], 16)

            def stack_k(b):
                sp.wait_ge(k_written[b % 2], 16 * (b // 2 + 1))
                if b >= 3:
                    wait_filled(("ST", b - 3, UNITS - 1))
                for j, piece in enumerate(K_PIECES):
                    sp.dma_start(kstack[b % 3][j * DK:(j + 1) * DK, :, :],
                                 k_dram[b, piece].rearrange("(h d) k -> d h k", d=DK)).then_inc(ld_kstack[b % 3], 16)

            def stack_q(c):
                sp.wait_ge(q_written[c % 2], 16 * (c // 2 + 1))
                for j, piece in enumerate(Q_PIECES):
                    sp.dma_start(qstack[j * DK:(j + 1) * DK, :, c * QW:(c + 1) * QW],
                                 q_dram[piece].rearrange("(h d) t -> d h t", d=DK)[:, :, c * QW:(c + 1) * QW])\
                      .then_inc(ld_qstack[c], 16)

            write_k(0)
            write_q(0)
            stack_k(0)
            stack_q(0)
            write_k(1)
            write_q(1)
            stack_k(1)
            stack_q(1)
            sp.dma_start(scale_t[:, :], A["L1_ffn_scale"].partition_broadcast(64)).then_inc(ld["scale"], 16)
            for i in range(-1, NB):
                if 3 <= i + 2 < NB:
                    stack_k(i + 2)
                if FIRST_Q <= i + 2 < QCHUNKS:
                    stack_q(i + 2)
                if i + 1 < NB:
                    sp.wait_ge(*drained_at(("NM", i + 1)))
                    for piece in range(2):
                        sp.dma_start(qstack[96 + piece:97 + piece, :, (i + 1) * S:(i + 2) * S],
                                     mT[piece * H:(piece + 1) * H, :]).then_inc(max_placed, 16)
                if POOL_K <= i + 3 < NB:
                    write_k(i + 3)
                if i == -1:
                    stack_k(2)
                if FIRST_Q <= i + 3 < QCHUNKS:
                    write_q(i + 3)
                if i == -1:
                    for b in range(4, NB):
                        load_ctx(b)
                elif i == 1:
                    sp.wait_ge(ones_ready, 2)
                    sp.dma_start(xg_dram[0:T].rearrange("(e c) d -> c e d", e=E),
                                 eo[0][:, :].unsqueeze(1).broadcast_to([S, E, D])).then_inc(zeroed, 16)
                elif i == 3:
                    for b in range(2):
                        load_b2(b)
                    for r, name in enumerate(("L1_xattn_bv", "L1_ffn_b2")):
                        sp.dma_start(browL1[:, r, :], A[name].partition_broadcast(S)).then_inc(ld["at1rows"], 16)
                if 1 <= i < 5:
                    load_expert((i - 1) // 2, [(i - 1) % 2])
                elif i == 5:
                    for n in range(2):
                        sp.wait_ge(k_written[n], 16 * NB // 2)
                    load_expert(2, [0])
                elif i == 6:
                    load_expert(2, [1])
                elif i == 7:
                    load_expert(3)

            wait_filled(("ST", NB - 1, UNITS - 1))
            for r, name in enumerate(("L1_xattn_Wq", "L1_xattn_Wk", "L1_xattn_Wv")):
                sp.dma_start(w_at1[:, r, :, :], kp_of(name)).then_inc(ld["at1w"], 16)

            sp.wait_ge(put, 16 * NB)
            for half in range(2):
                sp.dma_start(xn[:, 4 * half:4 * half + 4, :],
                             xg_dram[0:T].rearrange("(e c) d -> c e d", e=E)[:, 4 * half:4 * half + 4, :])\
                  .then_inc(xe_loaded[half], 16)
            for half in range(2):
                sp.dma_start(ctxN[0:KC, 12 * half:12 * half + 12, :],
                             A["ctx"].rearrange("b (c p) d -> p (b c) d", p=KC)[:, 12 * half:12 * half + 12, :])\
                  .then_inc(ld_ctxN[half], 16)
            sp.dma_start(w1f, A["L1_ffn_W1"].rearrange("(k p) f -> p k f", p=P)).then_inc(ld["ffnw"], 16)
            for s in range(2):
                sp.dma_start(w2f[s][:, :, 0:D], A["L1_ffn_W2"].rearrange("(f p) o -> p f o", p=P))\
                  .then_inc(ld["ffnw"], 16)
            for e in range(E):
                wait_filled(("DN", e))
                if e + RING < E:
                    load_expert(e + RING)
                sp.wait_ge(*drained_at(("DN", e)))
                if e + 2 < E:
                    load_b2(e + 2)
                sp.dma_start(eo_dram[e * CAP:(e + 1) * CAP, :], eo[e % 2][:, :]).then_inc(eo_stored[e % 2], 16)
            sp.dma_start(maskr[0:S, :, :].rearrange("p b k -> p (b k)"),
                         A["mask"].partition_broadcast(S)).then_inc(ld["mask"], 16)

            for b in range(NB):
                sp.wait_ge(*drained_at(("F3", b)))
                sp.dma_start(out[b], outs[b % 2][0:S, :]).then_inc(stored[b % 2], 16)
            for n in range(2):
                sp.wait_ge(stored[n], 16 * NB // 2)


BIAS_COLUMNS = ("L0_xattn_bq", "L0_xattn_bk", "L1_xattn_bq", "L1_xattn_bk", "L0_xattn_bv")

_INS = {
    "x": lambda v: v["x"],
    "ctx": lambda v: v["ctx_1024"],
    "ctxT": lambda v: v["ctx_1024"].reshape(NB * S2, D).T,
    "mask": lambda v: v["mask_BxS2_ff1"].reshape(-1),
    "L0_xattn_Wq": lambda v: v["L0_xattn_Wq"].T,
    "L0_xattn_Wk": lambda v: v["L0_xattn_Wk"].T,
    "L0_xattn_Wv": lambda v: v["L0_xattn_Wv"].T,
    "L0_xattn_Wo": lambda v: v["L0_xattn_Wo"].T,
    "bias_columns": lambda v: np.stack([v[n].reshape(DT, P) for n in BIAS_COLUMNS]).transpose(2, 0, 1),
    "L0_xattn_bo": lambda v: v["L0_xattn_bo"],
    "L0_ffn_Wg": lambda v: v["L0_ffn_Wg"],
    "L0_ffn_W1": lambda v: v["L0_ffn_W1"],
    "L0_ffn_b1": lambda v: v["L0_ffn_b1"].reshape(E, FT, P).transpose(2, 0, 1),
    "L0_ffn_W2": lambda v: v["L0_ffn_W2"],
    "L0_ffn_b2": lambda v: v["L0_ffn_b2"],
    "L1_xattn_Wq": lambda v: v["L1_xattn_Wq"].T,
    "L1_xattn_Wk": lambda v: v["L1_xattn_Wk"].T,
    "L1_xattn_Wv": lambda v: v["L1_xattn_Wv"],
    "L1_xattn_bv": lambda v: v["L1_xattn_bv"],
    "L1_ffn_W1": lambda v: v["L1_ffn_W1"].T,
    "L1_ffn_b1": lambda v: v["L1_ffn_b1"].reshape(FT, P).T,
    "L1_ffn_W2": lambda v: v["L1_ffn_W2"].T,
    "L1_ffn_b2": lambda v: v["L1_ffn_b2"],
    "L1_ffn_scale": lambda v: v["L1_ffn_scale"].reshape(1),
}


def kernel(**inputs):
    import numpy as _np
    import concourse.bacc as _bacc
    from concourse import mybir as _mybir
    from concourse.bass_utils import run_bass_kernel_spmd as _run

    given = {n: _np.asarray(a) for n, a in inputs.items()}
    nc = _bacc.Bacc("TRN2", target_bir_lowering=False, num_devices=1)
    arrays, aps = {}, {}
    for name, lay in _INS.items():
        a = _np.ascontiguousarray(lay(given))
        arrays[f"in_{name}"] = a
        aps[name] = nc.dram_tensor(f"in_{name}", a.shape, _mybir.dt.from_np(a.dtype), kind="ExternalInput").ap()
    aps["out"] = nc.dram_tensor("out_dram", (NB, S, D), _mybir.dt.float32, kind="ExternalOutput").ap()
    build(nc, aps)
    r = _run(nc, [arrays], core_ids=[0])
    return r.results[0]["out_dram"]
```

```python
from contextlib import ExitStack

import numpy as np
import concourse.bass as bass
from concourse import mybir

ALU = mybir.AluOpType
ACT = mybir.ActivationFunctionType
F32 = mybir.dt.float32
BF16 = mybir.dt.bfloat16
I32 = mybir.dt.int32
AX = mybir.AxisListType

P = 128
NB, S, D = 8, 112, 256
S2, KC = 375, 125
NKC = S2 // KC
DT = D // P
H, DK = 16, 16
E, F = 8, 1024
FT = F // P
CAP = NB * S // E
T = NB * S
EPS = 1e-5
HG = 4
UNITS = NKC * (H // HG)
VW = DK + 1
ROWS = 6 * DK
Q_PIECES = (0, 1, 2, 0, 1, 0)
K_PIECES = (0, 1, 0, 1, 0, 2)
RING = 4

PIPE = {
    0: [("D5", 2), ("K0", -3)],
    1: [("C6", 2), ("K1", -3)],
    2: [("U", 1), ("V0", -1), ("SK0", -3)],
    3: [],
    4: [("C1", 1)],
    5: [("C2", 1), ("V1", -1), ("D6", 2)],
    6: [("ND", -1)],
    7: [("C3", 1)],
    8: [("NM", -1), ("L2", 1), ("V2", -1)],
    9: [("SK1", -3)],
    10: [("C4", 1), ("SK2", -3)],
    11: [("C5", 1)],
}
FIRST_K = 3
POOL_K = 2
QW, QCHUNKS, FIRST_Q = 2 * S, NB // 2, 2
Q_UNITS = {7: "QX", 10: "QP", 11: "QS"}
MAX_FROM = 6


POOL_J = 1
GATHER_AHEAD = 3
AT_STEPS = NB + 5
FFN_AT = 8


CTX_FILL = {"C2": 1, "C3": 1, "C4": 4, "C5": 1, "C6": 2}
CTX_BEFORE_EXPERTS = 10


def steps():
    for i in range(-2, NB + 2):
        for u in range(UNITS):
            yield i, u


def max_heads(i, u):
    at = UNITS * i + u - MAX_FROM + 2 * UNITS
    for m in range(at * H // UNITS, (at + 1) * H // UNITS):
        if 0 <= m < NB * H:
            yield divmod(m, H)


def extras(i, u):
    for stage, behind in PIPE[u]:
        first = {"K": FIRST_K, "S": POOL_K, "V": 1}.get(stage[0], 0)
        if first <= i - behind < NB:
            yield stage, i - behind
    if u in Q_UNITS and FIRST_Q <= i + 3 < QCHUNKS:
        yield Q_UNITS[u], i + 3


def combined_in(i):
    return {0: (1, 2), 4: (6, 7)}.get(i, (i + 2,) if i < 4 else ())


def norm_orders():
    moments = [(n, b) for n in (1, 2) for b in range(NB)] + [(3, 0)]
    rows = [(n, b) for n in (1, 2) for b in range(NB)]
    for i in range(AT_STEPS):
        moments += [(3, b) for b in combined_in(i)]
        rows += [(4, i - 5)] * (i >= 5)
        rows += [(3, i)] * (i < NB)
        moments += [(4, i - 4)] * (0 <= i - 4 < NB)
    return ({k: n + 1 for n, k in enumerate(moments)}, {k: n + 1 for n, k in enumerate(rows)})


MOMENTS, ROWS_DONE = norm_orders()


def build(nc, A):
    out = A["out"]
    with ExitStack() as ctx:
        def sb(name, shape, dt=F32):
            return ctx.enter_context(nc.sbuf_tensor(name, shape, dt))

        def sem(name):
            return ctx.enter_context(nc.semaphore(name))

        k_dram = nc.dram_tensor("k_pieces_dram", (NB, 3, DT * P, S2), BF16).ap()
        q_dram = nc.dram_tensor("q_pieces_dram", (3, DT * P, T), BF16).ap()
        xg_dram = nc.dram_tensor("expert_in_dram", (2 * T, D), F32).ap()
        even_dram = nc.dram_tensor("even_rows_dram", (NB, 2, 4, D), F32).ap()
        eo_dram = nc.dram_tensor("expert_out_dram", (T, D), F32).ap()

        ctxT = sb("ctxT", [P, DT, NB * S2])
        xres = sb("xres", [S, NB, D])
        xn = sb("xn", [S, NB, D])
        xT = sb("xT", [P, DT, T])
        w_in = sb("w_in", [P, 4, DT, D])
        ident = sb("ident", [P, P])
        identb = sb("identb", [P, P], BF16)
        wg = sb("wg", [P, DT, E])
        bcol = sb("bcol", [P, 5, DT])
        b1col = sb("b1col", [P, E, FT])
        fb1col = sb("fb1col", [P, FT])
        browL0 = sb("browL0", [S, D])
        browL1 = sb("browL1", [S, 2, D])
        mv = sb("mv", [S, NB, 2])
        stats = sb("stats", [S, NB, 6])
        veps = sb("veps", [S, NB])
        rstd = sb("rstd", [S, NB])
        neghalf = sb("neghalf", [S, NB])
        stackf = sb("stackf", [P, (3 * H * S2 + H * T) // 2])
        kstack = [stackf[:, n * H * S2 // 2:(n + 1) * H * S2 // 2].bitcast(BF16)
                  .rearrange("p (h k) -> p h k", h=H) for n in range(3)]
        qstack = stackf[:, 3 * H * S2 // 2:].bitcast(BF16).rearrange("p (h q) -> p h q", h=H)
        at = [0]

        def cut(region, n):
            a = at[0]
            at[0] += n
            assert at[0] <= region.shape[1], (at[0], region.shape)
            return region[:, a:a + n]

        ctxV = cut(stackf, NB * NKC * D).rearrange("p (c d) -> p c d", d=D)
        w_at1 = cut(stackf, 2 * DT * D).rearrange("p (w k e) -> p w k e", w=2, k=DT)
        wv_at1 = w_in[:, 0]
        w1f = cut(stackf, DT * F).rearrange("p (k f) -> p k f", k=DT)
        w2f = cut(stackf, FT * D).rearrange("p (f o) -> p f o", f=FT)
        w2b0 = cut(stackf, FT * D).rearrange("p (f o) -> p f o", f=FT)
        hid = [cut(stackf, FT * S).rearrange("p (f s) -> p f s", f=FT) for _ in range(2)]
        bq_wide = cut(stackf, DT * S).rearrange("p (k s) -> p k s", k=DT)
        vones = [sb(f"vones{n}", [P, NKC, H, VW]) for n in range(2)]
        pT = [sb(f"pT{n}", [P, HG * S]) for n in range(3)]
        ctxU = sb("ctxU", [P, 4 * S])
        cc = sb("cc", [S, D])
        ccT = sb("ccT", [P, DT, S])
        mneg = sb("mneg", [S, 2, H])
        mpieces = sb("mpieces", [S, 2 * H], BF16)
        mT = sb("mT", [2 * H, S], BF16)
        rden = sb("rden", [S, H])
        tri = sb("tri", [S, S], BF16)
        onesb = sb("onesb", [S, S], BF16)
        em8 = sb("em8", [S, E])
        slot0 = sb("slot0", [S, E])
        spill = sb("spill", [S, NB])
        onehot = sb("onehot", [S, E], BF16)
        seen = sb("seen", [S, 2, E], BF16)
        lg = sb("lg", [S, E])
        ex = sb("ex", [S, E])
        small = sb("small", [S, 16])
        tmp8 = sb("tmp8", [S, 4, E])
        gate = sb("gate", [S, NB])
        idx_put = sb("idx_put", [S, NB], I32)
        idx_get = sb("idx_get", [S, NB], I32)
        ring = sb("ring", [P, RING, 2 * DT * F])
        w1e = [ring[:, n, 0:DT * F].rearrange("p (k f) -> p k f", k=DT) for n in range(RING)]
        w2e = [ring[:, n, DT * F:].rearrange("p (f o) -> p f o", f=FT) for n in range(RING)]
        stage = ring[:, 2:4, :].rearrange("p a n -> p (a n)")
        at[0] = 0
        kt = [cut(stage, DT * S2).rearrange("p (m k) -> p m k", m=DT) for _ in range(2)]
        kr = cut(stage, DT * S2).rearrange("p (m k) -> p m k", m=DT)
        kp = [cut(stage, 3 * DT * S2 // 2).bitcast(BF16).rearrange("p (c m k) -> p c m k", c=3, m=DT)
              for _ in range(2)]
        qt = [cut(stage, DT * QW).rearrange("p (m k) -> p m k", m=DT) for _ in range(2)]
        qr = cut(stage, DT * QW).rearrange("p (m k) -> p m k", m=DT)
        qp = [cut(stage, 3 * DT * QW // 2).bitcast(BF16).rearrange("p (c m k) -> p c m k", c=3, m=DT)
              for _ in range(2)]
        eo = [sb("eo0", [S, D]), cc]
        b2row = [sb(f"b2row{n}", [S, D]) for n in range(2)]
        late = ring[:, :, :].rearrange("p a n -> p (a n)")
        at[0] = 0
        wqk = cut(late, DT * D).rearrange("p (k e) -> p k e", k=DT)
        qk_bias = cut(late, 2 * DT)
        bqbk = cut(late, 1)
        qkT = [cut(late, DT * S).rearrange("p (k s) -> p k s", k=DT) for _ in range(2)]
        tq = [cut(late, 1) for _ in range(2)]
        maskr = cut(late, NB * S2).rearrange("p (b k) -> p b k", b=NB)
        assert at[0] <= ring.shape[2]
        sc = [cut(late, S2) for _ in range(2)]
        pr = [cut(late, S2) for _ in range(2)]
        pT1 = [cut(late, NKC * S).rearrange("p (c s) -> p c s", c=NKC) for _ in range(2)]
        sm1 = cut(late, 4 * NB).rearrange("p (b j) -> p b j", j=4)
        gT = [cut(late, FT * S).rearrange("p (f s) -> p f s", f=FT) for _ in range(2)]
        at_late = at[0]
        at[0] = 0
        ctx_flat = ctxT[:, :, :].rearrange("p k t -> p (k t)")
        w1b1 = cut(ctx_flat, DT * F).rearrange("p (k f) -> p k f", k=DT)
        w2b1 = cut(ctx_flat, FT * D).rearrange("p (f o) -> p f o", f=FT)
        at[0] = at_late
        def w2_part(w, m, j):
            return w.rearrange("p (r m) (j o) -> p m j r o", m=DT, j=4)[:, m, j]

        w1b = [cut(late, DT * F).rearrange("p (k f) -> p k f", k=DT), w1b1]
        w2b = [w2b0, w2b1]
        even1 = [cut(late, 4 * D).rearrange("p (j d) -> p j d", j=4) for _ in range(2)]
        even2 = [cut(late, 4 * D).rearrange("p (j d) -> p j d", j=4) for _ in range(2)]
        odd = [cut(late, DT * 8).rearrange("p (k j) -> p k j", k=DT) for _ in range(2)]
        outs = [cut(late, D) for _ in range(2)]
        scale_t = sb("scale_t", [P, 1])

        ps = ctx.enter_context(nc.psum_tensor("ps", [P, 8, 512], F32))

        def bank(n):
            return ps[:, n, :]

        filled = [sem(f"bank{n}_filled") for n in range(8)]
        drained = [sem(f"bank{n}_drained") for n in range(8)]
        fills, drains = [0] * 8, [0] * 8
        place = {}

        def filled_at(key):
            n, c, _ = place[key]
            return filled[n], c

        def drained_at(key):
            n, _, c = place[key]
            return drained[n], c

        ld = {n: sem(f"loaded_{n}") for n in
              ("wq", "wk", "wv", "wo", "bias", "wg", "b1", "rows",
               "at1w", "at1rows", "ffnw", "mask", "ffnb1", "scale")}
        ld_ctx = [sem(f"loaded_ctx{b}") for b in range(NB)]
        ld_wv_at1 = sem("loaded_at1_wv")
        ld_ring = [sem(f"loaded_expert{n}") for n in range(RING)]
        ld_kstack = [sem(f"loaded_kstack{n}") for n in range(3)]
        ld_x = [sem(f"loaded_x{n}") for n in range(2)]
        ld_qstack = [sem(f"loaded_qstack{c}") for c in range(QCHUNKS)]
        ld_ones = sem("ones_of_other_stacks_placed")
        ld_b2 = [sem(f"loaded_b2row{n}") for n in range(2)]
        k_written = [sem(f"k_pieces_written{n}") for n in range(2)]
        q_written = [sem(f"q_pieces_written{n}") for n in range(2)]
        max_placed = sem("max_rows_placed")
        consts = sem("constants_ready")
        ones_ready = sem("ones_and_zeros_ready")
        var_ready = sem("variance_ready")
        rstd_ready = sem("rstd_ready")
        xn_ready = sem("normalised_ready")
        xbo_ready = sem("x_plus_bo_ready")
        k_high = sem("k_high_piece_ready")
        k_rest = sem("k_less_high_piece_ready")
        k_middle = sem("k_middle_piece_ready")
        k_split = sem("k_pieces_ready")
        q_high = sem("q_high_piece_ready")
        q_split = sem("q_pieces_ready")
        pv_units = sem("pv_units_done")
        max_ready = sem("max_pieces_ready")
        lg_ready = sem("logit_max_ready")
        esum_ready = sem("gate_sum_ready")
        onehot_ready = sem("onehot_ready")
        slots_ready = sem("slots_ready")
        zeroed = sem("expert_in_zeroed")
        put = sem("rows_put")
        xe_loaded = [sem(f"expert_rows_loaded{n}") for n in range(2)]
        eo_stored = [sem(f"expert_out_stored{n}") for n in range(2)]
        got_rows = [sem(f"rows_got{b}") for b in range(NB)]
        bq_ready = sem("bq_wide_ready")
        mask_ready = sem("mask_terms_ready")
        at_ready = sem("second_scores_ready")
        exp_ready = sem("second_probs_ready")
        xbv_ready = sem("x_plus_bv_ready")
        xb2_ready = sem("x_plus_b2_ready")
        even_written = [sem(f"even_rows_written{n}") for n in range(2)]
        ld_even1 = [sem(f"even_rows_for_w1_loaded{n}") for n in range(2)]
        ld_even2 = [sem(f"even_rows_for_w2_loaded{n}") for n in range(2)]
        w1_ready = sem("w1_of_batch_ready")
        w2_ready = sem("w2_of_batch_ready")
        w2_pool_ready = sem("w2_of_batch_ready_by_gpsimd")
        gelu_ready = sem("gelu_ready")
        stored = [sem(f"out_stored{n}") for n in range(2)]
        dve = sem("dve_step")
        acts = sem("act_step")
        pools = sem("pool_step")

        block = ctx.enter_context(nc.Block())

        @block.tensor
        def _(pe):
            def open_bank(key, n, fill=1):
                if drains[n]:
                    pe.wait_ge(drained[n], drains[n])
                fills[n] += fill
                drains[n] += 1
                place[key] = (n, fills[n], drains[n])
                return bank(n)

            def read(key):
                pe.wait_ge(*drained_at(key))

            ring_bank = [0]

            def next_bank(banks):
                ring_bank[0] += 1
                return banks[ring_bank[0] % len(banks)]

            def transpose_x(key, b, n):
                o = open_bank((key, b), n)[:, 0:DT * S].rearrange("p (k s) -> p k s", k=DT)
                for k in range(DT):
                    mm = pe.transpose(o[:, k, :], xn[:, b, k * P:(k + 1) * P], ident[0:S, 0:S])
                mm.then_inc(filled[n], 1)

            def project_k(b, ms, banks):
                pe.wait_ge(ld_ctx[b], 16)
                for m in ms:
                    n = next_bank(banks)
                    o = open_bank(("K", b, m), n)
                    for k in range(DT):
                        mm = pe.matmul(o[:, 0:S2], w_in[:, 1, k, m * P:(m + 1) * P],
                                       ctxT[:, k, b * S2:(b + 1) * S2], start=k == 0, stop=k == DT - 1)
                    mm.then_inc(filled[n], 1)

            def turn_x(c, banks):
                pe.wait_ge(xn_ready, 2 * (c + 1))
                for b in (2 * c, 2 * c + 1):
                    transpose_x("XT1", b, next_bank(banks))

            def project_q(c, banks):
                for b in (2 * c, 2 * c + 1):
                    read(("XT1", b))
                for m in range(DT):
                    n = next_bank(banks)
                    o = open_bank(("Q", c, m), n)
                    for k in range(DT):
                        mm = pe.matmul(o[:, 0:QW], w_in[:, 0, k, m * P:(m + 1) * P],
                                       xT[:, k, c * QW:(c + 1) * QW], start=k == 0, stop=k == DT - 1)
                    mm.then_inc(filled[n], 1)

            def values(b, c):
                n = next_bank((6, 7))
                o = open_bank(("V", b, c), n)
                for k in range(DT):
                    mm = pe.matmul(o[0:KC, 0:D], ctxT[:, k, b * S2 + c * KC:b * S2 + (c + 1) * KC],
                                   w_in[:, 2, k, :], start=k == 0, stop=k == DT - 1)
                mm.then_inc(filled[n], 1)

            pe.wait_ge(consts, 1)
            for c in range(FIRST_Q):
                if c == 0:
                    pe.wait_ge(ld["wk"], 16)
                project_k(c, [0], range(4))
                turn_x(c, (6, 7))
                project_k(c, [1], range(4))
                if c == 0:
                    pe.wait_ge(ld["wq"], 16)
                project_q(c, range(4))
            project_k(FIRST_K - 1, range(DT), range(4))
            pe.wait_ge(ld["wv"], 16)
            for c in range(NKC):
                values(0, c)

            def row_max(b, h):
                n = 2 + h % 2
                o = open_bank(("MX", b, h), n)
                pe.matmul(o[0:S, 0:S2], qstack[0:ROWS, h, b * S:(b + 1) * S], kstack[b % 3][0:ROWS, h, :],
                          start=True, stop=True).then_inc(filled[n], 1)

            def scores(b, u):
                c, g = divmod(u, H // HG)
                n = (UNITS * b + u) % 2
                o = open_bank(("ST", b, u), n)
                if u == 0:
                    pe.wait_ge(max_placed, 32 * (b + 1))
                    if b == 0:
                        pe.wait_ge(consts, 2)
                    if b == 1:
                        pe.wait_ge(ld_ones, 32)
                for j in range(HG):
                    h = HG * g + j
                    mm = pe.matmul(o[0:KC, j * S:(j + 1) * S], kstack[b % 3][0:ROWS + 2, h, c * KC:(c + 1) * KC],
                                   qstack[0:ROWS + 2, h, b * S:(b + 1) * S], start=True, stop=True)
                mm.then_inc(filled[n], 1)

            def weighted(b, u):
                c, g = divmod(u, H // HG)
                if u == 0:
                    open_bank(("PV", b), 4 + b % 2, fill=0)
                    if b == 0:
                        pe.wait_ge(ones_ready, 7)
                    for chunk in range(NKC):
                        read(("V", b, chunk))
                read(("ST", b, u))
                for j in range(HG):
                    h = HG * g + j
                    mm = pe.matmul(bank(4 + b % 2)[32 * j:32 * j + VW, g * S:(g + 1) * S],
                                   vones[b % 2][0:KC, c, h, :], pT[(UNITS * b + u) % 3][0:KC, j * S:(j + 1) * S],
                                   start=u == 0, stop=c == NKC - 1, skip_group_check=True)
                mm.then_inc(pv_units, 1)

            chunks_done = [0]

            def project_context(n):
                for _ in range(n):
                    t = chunks_done[0]
                    chunks_done[0] += 1
                    b, c = divmod(t, NKC)
                    if t == 0:
                        pe.wait_ge(ld_wv_at1, 16)
                    bk = next_bank(range(4))
                    o = open_bank(("CV", t), bk)
                    for k in range(DT):
                        mm = pe.matmul(o[0:KC, 0:D], ctxT[:, k, b * S2 + c * KC:b * S2 + (c + 1) * KC],
                                       wv_at1[:, k, :], start=k == 0, stop=k == DT - 1)
                    mm.then_inc(filled[bk], 1)

            def post(stage, b):
                if b == NB - 1 and stage in CTX_FILL:
                    project_context(CTX_FILL[stage])
                if stage in ("V0", "V1", "V2"):
                    values(b, int(stage[1]))
                elif stage == "QX":
                    turn_x(b, (6, 7))
                elif stage == "QP":
                    project_q(b, (6, 7))
                elif stage in ("K0", "K1"):
                    project_k(b, [int(stage[1])], (6, 7))
                elif stage == "NM":
                    pe.wait_ge(max_ready, b + 1)
                    n = next_bank((6, 7))
                    o = open_bank(("NM", b), n).bitcast(BF16)
                    pe.transpose(o[0:2 * H, 0:S], mpieces[:, :], identb[0:S, 0:S]).then_inc(filled[n], 1)
                elif stage == "C1":
                    read(("PV", b))
                    n = next_bank((6, 7))
                    o = open_bank(("C1", b), n)
                    for g in range(4):
                        mm = pe.transpose(o[0:S, g * P:(g + 1) * P], ctxU[:, g * S:(g + 1) * S], ident[:, :])
                    mm.then_inc(filled[n], 1)
                elif stage == "C2":
                    read(("C1", b))
                    n = next_bank((6, 7))
                    o = open_bank(("C2", b), n)[:, 0:DT * S].rearrange("p (k s) -> p k s", k=DT)
                    for k in range(DT):
                        mm = pe.transpose(o[:, k, :], cc[:, k * P:(k + 1) * P], ident[0:S, 0:S])
                    mm.then_inc(filled[n], 1)
                elif stage == "C3":
                    read(("C2", b))
                    n = next_bank((6, 7))
                    o = open_bank(("C3", b), n)
                    for k in range(DT):
                        mm = pe.matmul(o[0:S, 0:D], ccT[:, k, :], w_in[:, 3, k, :], start=k == 0, stop=k == DT - 1)
                    mm.then_inc(filled[n], 1)
                elif stage == "C4":
                    pe.wait_ge(xn_ready, NB + b + 1)
                    transpose_x("XT2", b, next_bank((6, 7)))
                elif stage == "C5":
                    read(("XT2", b))
                    n = next_bank((6, 7))
                    o = open_bank(("LG", b), n)
                    for k in range(DT):
                        mm = pe.matmul(o[0:S, 0:E], xT[:, k, b * S:(b + 1) * S], wg[:, k, :],
                                       start=k == 0, stop=k == DT - 1)
                    mm.then_inc(filled[n], 1)
                elif stage == "C6":
                    if b == 0:
                        pe.wait_ge(consts, 3)
                    pe.wait_ge(onehot_ready, b + 1)
                    n = next_bank((6, 7))
                    o = open_bank(("CUM", b), n)
                    pe.matmul(o[0:S, 0:E], tri[:, :], onehot[:, :], start=True, stop=False)
                    pe.matmul(o[0:S, 0:E], onesb[:, :], seen[:, b % 2, :], start=False, stop=True)\
                      .then_inc(filled[n], 1)

            pe.wait_ge(ld["wo"], 16)
            pe.wait_ge(ld["wg"], 16)
            for i, u in steps():
                if i < NB and i >= 0:
                    scores(i, u)
                before = UNITS * i + u - 2
                if 0 <= before < UNITS * NB:
                    weighted(*divmod(before, UNITS))
                for b, h in max_heads(i, u):
                    if h == 0:
                        pe.wait_ge(ld_kstack[b % 3], 96 * (b // 3 + 1))
                        if b % 2 == 0:
                            pe.wait_ge(ld_qstack[b // 2], 96)
                    row_max(b, h)
                for stage, b in extras(i, u):
                    if stage not in ("U", "L2", "ND", "SK0", "SK1", "SK2", "QS", "D5", "D6"):
                        post(stage, b)

            def expert_rows(e):
                n = 6 + e % 2
                pe.wait_ge(xe_loaded[e // 4], 16)
                transpose_x("XE", e, n)

            def expert_up(e):
                read(("XE", e))
                pe.wait_ge(ld_ring[e % RING], 32 * (e // RING + 1))
                for half in range(2):
                    n = 2 * (e % 2) + half
                    o = open_bank(("UP", e, half), n)
                    for f in range(4):
                        ft = 4 * half + f
                        for k in range(DT):
                            mm = pe.matmul(o[:, f * S:(f + 1) * S], w1e[e % RING][:, k, ft * P:(ft + 1) * P],
                                           xT[:, k, e * S:(e + 1) * S], start=k == 0, stop=k == DT - 1)
                    mm.then_inc(filled[n], 1)

            def expert_down(e):
                n = 4 + e % 2
                read(("UP", e, 0))
                read(("UP", e, 1))
                o = open_bank(("DN", e), n)
                for ft in range(FT):
                    mm = pe.matmul(o[0:S, 0:D], hid[e % 2][:, ft, :], w2e[e % RING][:, ft, :],
                                   start=ft == 0, stop=ft == FT - 1)
                mm.then_inc(filled[n], 1)

            for e in range(E + 1):
                if e == 0:
                    project_context(CTX_BEFORE_EXPERTS)
                    expert_rows(0)
                if e + 1 < E:
                    expert_rows(e + 1)
                if e < E:
                    expert_up(e)
                if e >= 1:
                    expert_down(e - 1)

            pe.wait_ge(ld["at1w"], 32)
            o = open_bank("WQK", 0)
            for m in range(DT):
                for k in range(DT):
                    mm = pe.matmul(o[:, m * D:(m + 1) * D], w_at1[:, 0, k, m * P:(m + 1) * P], w_at1[:, 1, k, :],
                                   start=k == 0, stop=k == DT - 1)
            mm.then_inc(filled[0], 1)
            pe.wait_ge(bq_ready, 1)
            o = open_bank("WQKB", 1)
            for side in range(2):
                for m in range(DT):
                    for k in range(DT):
                        pe.matmul(o[:, DT * side + m:DT * side + m + 1], w_at1[:, 1 - side, k, m * P:(m + 1) * P],
                                  bcol[:, 2 + side, k:k + 1], start=k == 0, stop=k == DT - 1)
            for k in range(DT):
                mm = pe.matmul(o[0:S, 2 * DT:2 * DT + 1], bq_wide[:, k, :], bcol[:, 3, k:k + 1],
                               start=k == 0, stop=k == DT - 1)
            mm.then_inc(filled[1], 1)

            project_context(NB * NKC - chunks_done[0])

            def attend(stage, b):
                s = b % 2
                if stage == 0:
                    pe.wait_ge(xn_ready, ROWS_DONE[3, b])
                    transpose_x("XT3", b, 0)
                elif stage == 1:
                    if b == 0:
                        read("WQK")
                        read("WQKB")
                    read(("XT3", b))
                    o = open_bank(("QK", b), 1)
                    for m in range(DT):
                        for k in range(DT):
                            pe.matmul(o[:, m * S:(m + 1) * S], wqk[:, k, m * P:(m + 1) * P],
                                      xT[:, k, b * S:(b + 1) * S], start=k == 0, stop=k == DT - 1)
                    for k in range(DT):
                        mm = pe.matmul(o[0:S, 2 * S:2 * S + 1], xT[:, k, b * S:(b + 1) * S],
                                       qk_bias[:, DT + k:DT + k + 1], start=k == 0, stop=k == DT - 1)
                    mm.then_inc(filled[1], 1)
                elif stage == 2:
                    read(("QK", b))
                    o = open_bank(("S1", b), 2 + s)
                    for k in range(DT):
                        mm = pe.matmul(o[0:S, 0:S2], qkT[s][:, k, :], ctxT[:, k, b * S2:(b + 1) * S2],
                                       start=k == 0, stop=k == DT - 1)
                    mm.then_inc(filled[2 + s], 1)
                elif stage == 3:
                    pe.wait_ge(exp_ready, b + 1)
                    o = open_bank(("PT", b), 4)
                    for c in range(NKC):
                        mm = pe.transpose(o[0:KC, c * S:(c + 1) * S], pr[s][0:S, c * KC:(c + 1) * KC],
                                          ident[0:S, 0:S])
                    mm.then_inc(filled[4], 1)
                elif stage == 4:
                    read(("PT", b))
                    for c in range(NKC):
                        read(("CV", NKC * b + c))
                    o = open_bank(("O1", b), 6)
                    for c in range(NKC):
                        mm = pe.matmul(o[0:S, 0:D], pT1[s][0:KC, c, :], ctxV[0:KC, NKC * b + c, :],
                                       start=c == 0, stop=c == NKC - 1)
                    mm.then_inc(filled[6], 1)
                elif stage == 5:
                    pe.wait_ge(xn_ready, ROWS_DONE[4, b])
                    transpose_x("XT4", b, 7)

            def ffn(stage, b):
                s = b % 2
                if stage == 1:
                    read(("XT4", b))
                    pe.wait_ge(w1_ready, b + 1)
                    for half in range(2):
                        n = 2 * s + half
                        o = open_bank(("F1", b, half), n)
                        for f in range(4):
                            ft = 4 * half + f
                            for k in range(DT):
                                mm = pe.matmul(o[:, f * S:(f + 1) * S], w1b[s][:, k, ft * P:(ft + 1) * P],
                                               xT[:, k, b * S:(b + 1) * S], start=k == 0, stop=k == DT - 1)
                        mm.then_inc(filled[n], 1)
                elif stage == 2:
                    pe.wait_ge(gelu_ready, FT * (b + 1))
                    pe.wait_ge(w2_ready, b + 1)
                    pe.wait_ge(w2_pool_ready, b + 1)
                    n = 4 + s
                    o = open_bank(("F2", b), n)
                    for ft in range(FT):
                        mm = pe.matmul(o[0:S, 0:D], gT[s][:, ft, :], w2b[s][:, ft, :],
                                       start=ft == 0, stop=ft == FT - 1)
                    mm.then_inc(filled[n], 1)

            for i in range(FFN_AT + NB + 2):
                for stage in (4, 2, 3, 1, 0):
                    if 0 <= i - stage < NB:
                        attend(stage, i - stage)
                for stage in (1, 2):
                    if 0 <= i - FFN_AT - stage < NB:
                        ffn(stage, i - FFN_AT - stage)
                if 0 <= i - 5 < NB:
                    attend(5, i - 5)

        @block.scalar
        def _(act):
            n_act = [0]

            def step(ins):
                n_act[0] += 1
                ins.then_inc(acts, 1)
                act.wait_ge(acts, n_act[0])

            def full(key):
                act.wait_ge(*filled_at(key))
                return bank(place[key][0]), drained[place[key][0]]

            act.dma_start(w_in[:, 1, :, :], A["L0_xattn_Wk"].rearrange("(k p) n -> p k n", p=P)).then_inc(ld["wk"], 16)
            act.dma_start(w_in[:, 0, :, :], A["L0_xattn_Wq"].rearrange("(k p) n -> p k n", p=P)).then_inc(ld["wq"], 16)
            act.dma_start(bcol[:, :, :], A["bias_columns"]).then_inc(ld["bias"], 16)
            act.dma_start(w_in[:, 2, :, :], A["L0_xattn_Wv"].rearrange("(k p) n -> p k n", p=P)).then_inc(ld["wv"], 16)
            act.dma_start(w_in[:, 3, :, :], A["L0_xattn_Wo"].rearrange("(k p) n -> p k n", p=P)).then_inc(ld["wo"], 16)
            act.dma_start(wg[:, :, :], A["L0_ffn_Wg"].rearrange("(k p) n -> p k n", p=P)).then_inc(ld["wg"], 16)
            act.dma_start(browL0[:, :], A["L0_xattn_bo"].partition_broadcast(S)).then_inc(ld["rows"], 16)
            act.dma_start(b1col[:, :, :], A["L0_ffn_b1"]).then_inc(ld["b1"], 16)
            act.dma_start(fb1col[:, :], A["L1_ffn_b1"]).then_inc(ld["ffnb1"], 16)

            def copy_xT(key, b):
                o, free = full((key, b))
                act.activation(xT[:, :, b * S:(b + 1) * S], o[:, 0:DT * S].rearrange("p (k s) -> p k s", k=DT),
                               ACT.Copy).then_inc(free, 1)

            def split_k(b, ms):
                if b >= 2:
                    act.wait_ge(k_split, b - 1)
                for m in ms:
                    o, free = full(("K", b, m))
                    act.activation(kt[b % 2][:, m, :], o[:, 0:S2], ACT.Identity, bias=bcol[:, 1, m:m + 1])\
                       .then_inc(free, 1)
                if DT - 1 not in ms:
                    return
                if b >= 2:
                    act.wait_ge(k_written[b % 2], 16 * (b // 2))
                for m in range(DT):
                    act.wait_ge(*drained_at(("K", b, m)))
                act.activation(kp[b % 2][:, 0, :, :], kt[b % 2][:, :, :], ACT.Copy).then_inc(k_high, 1)

            def split_q(c):
                if c >= 2:
                    act.wait_ge(q_split, c - 1)
                for m in range(DT):
                    o, free = full(("Q", c, m))
                    act.activation(qt[c % 2][:, m, :], o[:, 0:QW], ACT.Identity, bias=bcol[:, 0, m:m + 1])\
                       .then_inc(free, 1)
                if c >= 2:
                    act.wait_ge(q_written[c % 2], 16 * (c // 2))
                for m in range(DT):
                    act.wait_ge(*drained_at(("Q", c, m)))
                act.activation(qp[c % 2][:, 0, :, :], qt[c % 2][:, :, :], ACT.Copy).then_inc(q_high, 1)

            def copy_chunk(c):
                for b in (2 * c, 2 * c + 1):
                    copy_xT("XT1", b)

            def copy_v(b, c):
                if c == 0 and b >= 2:
                    act.wait_ge(pv_units, UNITS * (b - 1))
                o, free = full(("V", b, c))
                act.activation(vones[b % 2][0:KC, c, :, 0:DK],
                               o[0:KC, 0:D].rearrange("p (h w) -> p h w", h=H), ACT.Copy).then_inc(free, 1)

            act.wait_ge(ld["bias"], 16)
            for c in range(FIRST_Q):
                split_k(c, [0])
                copy_chunk(c)
                split_k(c, [1])
                split_q(c)
            split_k(FIRST_K - 1, range(DT))
            for c in range(NKC):
                copy_v(0, c)

            def exps(b, u):
                w = UNITS * b + u
                o, free = full(("ST", b, u))
                if w >= 3:
                    act.wait_ge(pv_units, w - 2)
                act.activation(pT[w % 3][0:KC, :], o[0:KC, 0:HG * S], ACT.Exp, scale=DK ** -0.5).then_inc(free, 1)

            def post(stage, b):
                if stage == "U":
                    act.wait_ge(pv_units, UNITS * (b + 1))
                    if b:
                        act.wait_ge(*filled_at(("C1", b - 1)))
                    act.activation(ctxU[:, :], bank(4 + b % 2)[:, 0:4 * S], ACT.Copy)\
                       .then_inc(drained[4 + b % 2], 1)
                elif stage in ("V0", "V1", "V2"):
                    copy_v(b, int(stage[1]))
                elif stage in ("K0", "K1"):
                    split_k(b, [int(stage[1])])
                elif stage == "QX":
                    copy_chunk(b)
                elif stage == "QP":
                    split_q(b)
                elif stage == "SK1":
                    act.wait_ge(k_rest, b - POOL_K + 1)
                    act.activation(kp[b % 2][:, 1, :, :], kr[:, :, :], ACT.Copy).then_inc(k_middle, 1)
                elif stage == "C2":
                    o, free = full(("C2", b))
                    for k in range(DT):
                        ins = act.activation(ccT[:, k, :], o[:, k * S:(k + 1) * S], ACT.Identity,
                                             bias=bcol[:, 4, k:k + 1])
                    ins.then_inc(free, 1)
                elif stage == "NM":
                    o, free = full(("NM", b))
                    if b:
                        act.wait_ge(max_placed, 32 * b)
                    act.activation(mT[:, :], o.bitcast(BF16)[0:2 * H, 0:S], ACT.Copy).then_inc(free, 1)
                elif stage == "C4":
                    copy_xT("XT2", b)
                elif stage == "C5":
                    act.wait_ge(lg_ready, b + 1)
                    act.activation(ex[:, :], lg[:, :], ACT.Exp, bias=small[:, 0:1], accum_out=small[:, 1:2])\
                       .then_inc(esum_ready, 1)

            chunks_done = [0]

            def copy_context_values(n):
                for _ in range(n):
                    t = chunks_done[0]
                    chunks_done[0] += 1
                    o, free = full(("CV", t))
                    act.activation(ctxV[0:KC, t, :], o[0:KC, 0:D], ACT.Copy).then_inc(free, 1)

            for i, u in steps():
                if 0 <= i < NB:
                    exps(i, u)
                for stage, b in extras(i, u):
                    if b == NB - 1 and stage in CTX_FILL:
                        copy_context_values(CTX_FILL[stage])
                    if stage in ("V0", "V1", "V2", "K0", "K1", "SK1", "QX", "QP", "U", "C2", "NM", "C4", "C5"):
                        post(stage, b)

            def hidden(e):
                if e >= 2:
                    act.wait_ge(*filled_at(("DN", e - 2)))
                o, free = full(("UP", e, 0))
                for f in range(4):
                    ins = act.activation(hid[e % 2][:, f, :], o[:, f * S:(f + 1) * S], ACT.Relu,
                                         bias=b1col[:, e, f:f + 1])
                ins.then_inc(free, 1)

            act.wait_ge(ld["b1"], 16)
            for e in range(E):
                if e == 0:
                    copy_context_values(CTX_BEFORE_EXPERTS)
                    copy_xT("XE", 0)
                if e + 1 < E:
                    copy_xT("XE", e + 1)
                hidden(e)

            def attend(stage, b):
                s = b % 2
                if stage == 0:
                    copy_xT("XT3", b)
                elif stage == 1:
                    if b == 0:
                        act.wait_ge(*drained_at("WQKB"))
                    if b >= 2:
                        act.wait_ge(*drained_at(("S1", b - 2)))
                    o, free = full(("QK", b))
                    act.activation(tq[s][0:S, :], o[0:S, 2 * S:2 * S + 1], ACT.Identity, bias=bqbk[0:S, :])
                    for m in range(DT):
                        ins = act.activation(qkT[s][:, m, :], o[:, m * S:(m + 1) * S], ACT.Identity,
                                             bias=qk_bias[:, m:m + 1])
                    ins.then_inc(free, 1)
                elif stage == 2:
                    act.wait_ge(at_ready, b + 1)
                    if b >= 2:
                        act.wait_ge(*filled_at(("PT", b - 2)))
                    act.activation(pr[s][0:S, :], sc[s][0:S, :], ACT.Exp, bias=sm1[0:S, b, 1:2],
                                   scale=DK ** -0.5, accum_out=sm1[0:S, b, 2:3]).then_inc(exp_ready, 1)
                elif stage == 3:
                    o, free = full(("PT", b))
                    if b >= 2:
                        act.wait_ge(*filled_at(("O1", b - 2)))
                    act.activation(pT1[s][0:KC, :, :], o[0:KC, 0:NKC * S].rearrange("p (c s) -> p c s", c=NKC),
                                   ACT.Copy).then_inc(free, 1)
                elif stage == 5:
                    copy_xT("XT4", b)

            def gelu(b):
                if b == 0:
                    act.wait_ge(ld["ffnb1"], 16)
                if b >= 2:
                    act.wait_ge(*filled_at(("F2", b - 2)))
                for half in range(2):
                    o, free = full(("F1", b, half))
                    for f in range(4):
                        ft = 4 * half + f
                        act.activation(gT[b % 2][:, ft, :], o[:, f * S:(f + 1) * S], ACT.Gelu,
                                       bias=fb1col[:, ft:ft + 1]).then_inc(gelu_ready, 1)
                    act.wait_ge(gelu_ready, FT * b + 4 * half + 4)
                    act.sem_inc(free, 1)

            o, free = full("WQK")
            act.activation(wqk[:, :, :], o[:, 0:DT * D].rearrange("p (k e) -> p k e", k=DT), ACT.Copy)\
               .then_inc(free, 1)
            o, free = full("WQKB")
            act.activation(qk_bias[:, :], o[:, 0:2 * DT], ACT.Copy)
            act.activation(bqbk[0:S, :], o[0:S, 2 * DT:2 * DT + 1], ACT.Copy).then_inc(free, 1)
            copy_context_values(NB * NKC - chunks_done[0])
            for i in range(FFN_AT + NB + 1):
                for stage in (3, 1, 2, 0):
                    if 0 <= i - stage < NB:
                        attend(stage, i - stage)
                if 0 <= i - FFN_AT - 1 < NB:
                    gelu(i - FFN_AT - 1)
                if 0 <= i - 5 < NB:
                    attend(5, i - 5)

        @block.vector
        def _(v):
            n_dve = [0]

            def step(ins):
                n_dve[0] += 1
                ins.then_inc(dve, 1)
                v.wait_ge(dve, n_dve[0])

            def full(key):
                v.wait_ge(*filled_at(key))
                return bank(place[key][0]), drained[place[key][0]]

            def drained_by_me(key):
                v.wait_ge(*drained_at(key))

            def moments(b):
                step(v.bn_stats(stats[:, b, :], xres[:, b, :]))
                step(v.bn_aggr(mv[:, b, :], stats[:, b, :]))
                v.tensor_scalar(veps[:, b:b + 1], mv[:, b, 1:2], EPS, None, ALU.add).then_inc(var_ready, 1)

            def normalise(norm, b):
                v.wait_ge(rstd_ready, MOMENTS[norm, b])
                v.tensor_scalar(xn[:, b, :], xres[:, b, :], mv[:, b, 0:1], rstd[:, b:b + 1],
                                ALU.subtract, ALU.mult).then_inc(xn_ready, 1)

            def split_k(b):
                v.wait_ge(k_high, b + 1)
                step(v.tensor_tensor(kr[:, :, :], kt[b % 2][:, :, :], kp[b % 2][:, 0, :, :], ALU.subtract))
                step(v.tensor_copy(kp[b % 2][:, 1, :, :], kr[:, :, :]))
                v.tensor_tensor(kp[b % 2][:, 2, :, :], kr[:, :, :], kp[b % 2][:, 1, :, :], ALU.subtract)\
                 .then_inc(k_split, 1)
                v.wait_ge(k_split, b + 1)

            def split_q(c):
                v.wait_ge(q_high, c + 1)
                step(v.tensor_tensor(qr[:, :, :], qt[c % 2][:, :, :], qp[c % 2][:, 0, :, :], ALU.subtract))
                step(v.tensor_copy(qp[c % 2][:, 1, :, :], qr[:, :, :]))
                v.tensor_tensor(qp[c % 2][:, 2, :, :], qr[:, :, :], qp[c % 2][:, 1, :, :], ALU.subtract)\
                 .then_inc(q_split, 1)
                v.wait_ge(q_split, c + 1)

            v.memset(neghalf[:, :], -0.5).then_inc(ones_ready, 1)
            v.memset(eo[0][:, :], 0.0).then_inc(ones_ready, 1)
            v.memset(vones[0][:, :, :, DK:VW], 1.0).then_inc(ones_ready, 1)
            v.memset(vones[1][:, :, :, DK:VW], 1.0).then_inc(ones_ready, 1)
            for n in (4, 5):
                v.memset(bank(n)[:, :], 0.0).then_inc(ones_ready, 1)
            v.memset(seen[:, :, :], 0.0).then_inc(ones_ready, 1)
            for n, group in enumerate((range(0, 2), range(2, 4))):
                v.wait_ge(ld_x[n], 16)
                for b in group:
                    moments(b)
                for b in group:
                    normalise(1, b)
            split_k(0)
            split_q(0)
            for b in range(4, NB):
                moments(b)
            for b in range(4, NB):
                normalise(1, b)
            split_k(1)
            split_q(1)
            v.wait_ge(ones_ready, 7)

            def row_max(b, h):
                o, free = full(("MX", b, h))
                v.tensor_reduce(mneg[:, b % 2, h:h + 1], o[0:S, 0:S2], AX.X, ALU.max, negate=True).then_inc(free, 1)

            def post(stage, b):
                if stage == "QS":
                    split_q(b)
                elif stage == "ND":
                    for h in (H - 2, H - 1):
                        drained_by_me(("MX", b, h))
                    if b:
                        v.wait_ge(*filled_at(("NM", b - 1)))
                    step(v.tensor_copy(mpieces[:, 0:H], mneg[:, b % 2, :]))
                    v.tensor_tensor(mpieces[:, H:2 * H], mneg[:, b % 2, :], mpieces[:, 0:H], ALU.subtract)\
                     .then_inc(max_ready, 1)
                    v.wait_ge(max_ready, b + 1)
                elif stage == "C1":
                    o, free = full(("C1", b))
                    o = o[0:S, :].rearrange("p (h w) -> p h w", h=H)
                    step(v.reciprocal(rden[:, :], o[:, :, DK]))
                    if b:
                        v.wait_ge(*filled_at(("C2", b - 1)))
                    v.tensor_tensor(cc[:, :].rearrange("p (h w) -> p h w", h=H), o[:, :, 0:DK],
                                    rden[:, :].unsqueeze(2).broadcast_to([S, H, DK]), ALU.mult)\
                     .then_inc(free, 1)
                elif stage == "C3":
                    o, free = full(("C3", b))
                    v.wait_ge(xbo_ready, NB)
                    v.tensor_tensor(xres[:, b, :], o[0:S, 0:D], xres[:, b, :], ALU.add).then_inc(free, 1)
                    drained_by_me(("C3", b))
                    moments(b)
                elif stage == "L2":
                    normalise(2, b)
                elif stage == "C5":
                    o, free = full(("LG", b))
                    if b:
                        v.wait_ge(esum_ready, b)
                    else:
                        v.wait_ge(consts, 3)
                    v.tensor_copy(lg[:, :], o[0:S, 0:E]).then_inc(free, 1)
                    drained_by_me(("LG", b))
                    v.tensor_reduce(small[:, 0:1], lg[:, :], AX.X, ALU.max, negate=True).then_inc(lg_ready, 1)
                elif stage == "D5":
                    v.wait_ge(lg_ready, b + 1)
                    step(v.tensor_scalar(tmp8[:, 0, :], lg[:, :], small[:, 0:1], 0.0, ALU.add, ALU.is_equal))
                    step(v.tensor_tensor(tmp8[:, 1, :], tmp8[:, 0, :], em8[:, :], ALU.mult))
                    step(v.tensor_reduce(small[:, 2:3], tmp8[:, 1, :], AX.X, ALU.min))
                    v.tensor_scalar(onehot[:, :], tmp8[:, 1, :], small[:, 2:3], None, ALU.is_equal)\
                     .then_inc(onehot_ready, 1)
                    v.wait_ge(onehot_ready, b + 1)
                    step(v.tensor_tensor(seen[:, (b + 1) % 2, :], seen[:, b % 2, :], onehot[:, :], ALU.add))
                elif stage == "C6":
                    o, free = full(("CUM", b))
                    v.tensor_copy(tmp8[:, 2, :], o[0:S, 0:E]).then_inc(free, 1)
                    drained_by_me(("CUM", b))
                    step(v.scalar_tensor_tensor(tmp8[:, 0, :], tmp8[:, 2, :], float(CAP), onehot[:, :],
                                                ALU.is_le, ALU.mult))
                    step(v.tensor_tensor(tmp8[:, 3, :], tmp8[:, 2, :], slot0[:, :], ALU.add))
                elif stage == "D6":
                    step(v.tensor_tensor(tmp8[:, 1, :], tmp8[:, 3, :], onehot[:, :], ALU.mult))
                    step(v.tensor_reduce(small[:, 3:5], tmp8[:, 0:2, :], AX.X, ALU.add))
                    v.tensor_scalar(idx_get[:, b:b + 1], small[:, 4:5], small[:, 3:4], None, ALU.mult)
                    step(v.tensor_scalar(small[:, 5:6], small[:, 4:5], spill[:, b:b + 1], small[:, 3:4],
                                         ALU.subtract, ALU.mult))
                    v.tensor_scalar(idx_put[:, b:b + 1], small[:, 5:6], spill[:, b:b + 1], None, ALU.add)\
                     .then_inc(slots_ready, 1)
                    v.wait_ge(esum_ready, b + 1)
                    step(v.reciprocal(small[:, 6:7], small[:, 1:2]))
                    step(v.tensor_scalar(gate[:, b:b + 1], small[:, 6:7], small[:, 3:4], None, ALU.mult))

            for i, u in steps():
                for b, h in max_heads(i, u):
                    row_max(b, h)
                for stage, b in extras(i, u):
                    if stage in ("QS", "ND", "C1", "C3", "L2", "C5", "D5", "C6", "D6"):
                        post(stage, b)

            v.wait_ge(ld["b1"], 16)
            v.wait_ge(*filled_at(("ST", NB - 1, UNITS - 1)))
            v.tensor_copy(bq_wide[:, :, :], bcol[:, 2, :].unsqueeze(2).broadcast_to([P, DT, S]))\
             .then_inc(bq_ready, 1)

            def finish(e):
                o, free = full(("DN", e))
                v.wait_ge(ld_b2[e % 2], 16 * (e // 2 + 1))
                if e >= 2:
                    v.wait_ge(eo_stored[e % 2], 16 * (e // 2))
                v.tensor_tensor(eo[e % 2][:, :], o[0:S, 0:D], b2row[e % 2][:, :], ALU.add).then_inc(free, 1)

            for e in range(E):
                if e >= 2:
                    v.wait_ge(*filled_at(("DN", e - 2)))
                o, free = full(("UP", e, 1))
                for f in range(4):
                    ins = v.tensor_scalar(hid[e % 2][:, 4 + f, :], o[:, f * S:(f + 1) * S],
                                          b1col[:, e, 4 + f:5 + f], 0.0, ALU.add, ALU.max)
                ins.then_inc(free, 1)
                if e:
                    finish(e - 1)
            finish(E - 1)

            def combine(b):
                v.wait_ge(got_rows[b], 16)
                step(v.scalar_tensor_tensor(xres[:, b, :], xn[:, b, :], gate[:, b:b + 1], xres[:, b, :],
                                            ALU.mult, ALU.add))
                moments(b)

            def attend(stage, b):
                s = b % 2
                if stage == 2:
                    o, free = full(("S1", b))
                    v.wait_ge(mask_ready, b + 1)
                    if b >= 2:
                        v.wait_ge(exp_ready, b - 1)
                    v.scalar_tensor_tensor(sc[s][0:S, :], o[0:S, 0:S2], tq[s][0:S, :], maskr[0:S, b, :],
                                           ALU.add, ALU.add).then_inc(free, 1)
                    drained_by_me(("S1", b))
                    step(v.tensor_reduce(sm1[0:S, b, 0:1], sc[s][0:S, :], AX.X, ALU.max, negate=True))
                    v.tensor_scalar(sm1[0:S, b, 1:2], sm1[0:S, b, 0:1], DK ** -0.5, None, ALU.mult)\
                     .then_inc(at_ready, 1)
                elif stage == 4:
                    v.wait_ge(exp_ready, b + 1)
                    step(v.reciprocal(sm1[0:S, b, 3:4], sm1[0:S, b, 2:3]))
                    o, free = full(("O1", b))
                    v.wait_ge(xbv_ready, b + 1)
                    v.scalar_tensor_tensor(xres[:, b, :], o[0:S, 0:D], sm1[0:S, b, 3:4], xres[:, b, :],
                                           ALU.mult, ALU.add).then_inc(free, 1)
                    drained_by_me(("O1", b))
                    moments(b)

            def add_rank_one(which, b):
                s = b % 2
                if which == 1:
                    if b == 0:
                        v.wait_ge(ld["scale"], 16)
                        v.wait_ge(ld["ffnw"], 32)
                    if b >= 2:
                        v.wait_ge(w2_ready, b - 1)
                        v.wait_ge(w2_pool_ready, b - 1)
                        for half in range(2):
                            v.wait_ge(*filled_at(("F1", b - 2, half)))
                    drained_by_me(("XT4", b))
                    step(v.tensor_scalar(odd[s][:, :, :], xT[:, :, b * S + 2:b * S + 18:2], scale_t[:, :], None,
                                         ALU.mult))
                    v.wait_ge(ld_even1[s], 16 * (b // 2 + 1))
                    for k in range(DT):
                        for j in range(4):
                            ins = v.scalar_tensor_tensor(w1b[s][:, k, j * D:(j + 1) * D], even1[s][:, j, :],
                                                         odd[s][:, k, j:j + 1], w1f[:, k, j * D:(j + 1) * D],
                                                         ALU.mult, ALU.add)
                    ins.then_inc(w1_ready, 1)
                else:
                    if b >= 2:
                        v.wait_ge(*filled_at(("F2", b - 2)))
                    v.wait_ge(ld_even2[s], 16 * (b // 2 + 1))
                    for m in range(DT):
                        for j in range(4 - POOL_J):
                            ins = v.scalar_tensor_tensor(w2_part(w2b[s], m, j),
                                                         even2[s][:, j, :].rearrange("p (o r) -> p r o", r=4),
                                                         odd[s][:, m, 4 + j:5 + j], w2_part(w2f, m, j),
                                                         ALU.mult, ALU.add)
                    ins.then_inc(w2_ready, 1)

            def finish_ffn(b):
                o, free = full(("F2", b))
                v.wait_ge(xb2_ready, b + 1)
                if b >= 2:
                    v.wait_ge(stored[b % 2], 16 * (b // 2))
                v.tensor_tensor(outs[b % 2][0:S, :], o[0:S, 0:D], xres[:, b, :], ALU.add).then_inc(free, 1)

            combine(0)
            for i in range(FFN_AT + NB + 2):
                if 0 <= i - 5 < NB:
                    normalise(4, i - 5)
                if i < NB:
                    normalise(3, i)
                for b in combined_in(i):
                    combine(b)
                for stage in (4, 2):
                    if 0 <= i - stage < NB:
                        attend(stage, i - stage)
                j = i - FFN_AT
                if 0 <= j < NB:
                    add_rank_one(1, j)
                if 0 <= j - 1 < NB:
                    add_rank_one(2, j - 1)
                if 0 <= j - 2 < NB:
                    finish_ffn(j - 2)

        @block.gpsimd
        def _(g):
            n_pool = [0]

            def step(ins):
                n_pool[0] += 1
                ins.then_inc(pools, 1)
                g.wait_ge(pools, n_pool[0])

            def root(norm, b):
                g.wait_ge(var_ready, MOMENTS[norm, b])
                g.tensor_tensor(rstd[:, b:b + 1], veps[:, b:b + 1], neghalf[:, b:b + 1], ALU.pow)\
                 .then_inc(rstd_ready, 1)

            def diagonal(ap, base, pattern, cm):
                step(g.affine_select(out=ap, in_=ap, compare_op=ALU.not_equal, fill=1.0, base=base,
                                     pattern=pattern, channel_multiplier=cm))

            step(g.memset(ident[:, :], 0.0))
            diagonal(ident[:, :], 0, [[-1, P]], 1)
            g.tensor_copy(identb[:, :], ident[:, :]).then_inc(consts, 1)
            g.wait_ge(ones_ready, 1)
            for b in range(NB):
                root(1, b)
            g.wait_ge(rstd_ready, NB)
            g.memset(kstack[0][96:98, :, :], 1.0).then_inc(consts, 1)
            g.wait_ge(consts, 2)
            for n in range(1, 3):
                g.dma_start(kstack[n][96:98, :, :], kstack[0][96:98, :, :]).then_inc(ld_ones, 16)
            step(g.memset(onesb[:, :], 1.0))
            step(g.affine_select(out=tri[:, :], in_=onesb[:, :], compare_op=ALU.is_ge, fill=0.0, base=0,
                                 pattern=[[1, S]], channel_multiplier=-1))
            step(g.iota(em8[:, :], pattern=[[1, E]], base=-E, channel_multiplier=0,
                        allow_small_or_imprecise_dtypes=True))
            step(g.iota(slot0[:, :], pattern=[[CAP, E]], base=-1, channel_multiplier=0,
                        allow_small_or_imprecise_dtypes=True))
            g.iota(spill[:, :], pattern=[[S, NB]], base=T, channel_multiplier=1,
                   allow_small_or_imprecise_dtypes=True).then_inc(consts, 1)
            g.wait_ge(xn_ready, NB)
            g.wait_ge(ld["rows"], 16)
            for b in range(NB):
                g.tensor_tensor(xres[:, b, :], xres[:, b, :], browL0[:, :], ALU.add).then_inc(xbo_ready, 1)
            g.wait_ge(xbo_ready, NB)
            for i, u in steps():
                for stage, b in extras(i, u):
                    if stage == "C3":
                        root(2, b)
                    elif stage == "SK0":
                        g.wait_ge(k_high, b + 1)
                        g.wait_ge(k_split, b)
                        g.tensor_tensor(kr[:, :, :], kt[b % 2][:, :, :], kp[b % 2][:, 0, :, :], ALU.subtract)\
                         .then_inc(k_rest, 1)
                    elif stage == "SK2":
                        g.wait_ge(k_middle, b - POOL_K + 1)
                        g.tensor_tensor(kp[b % 2][:, 2, :, :], kr[:, :, :], kp[b % 2][:, 1, :, :], ALU.subtract)\
                         .then_inc(k_split, 1)
                    elif stage == "D6":
                        if b == 0:
                            g.wait_ge(zeroed, 16)
                        g.wait_ge(slots_ready, b + 1)
                        g.indirect_dma_start(out=xg_dram, out_offset=bass.IndirectOffsetOnAxis(
                            ap=idx_put[:, b:b + 1], axis=0), in_=xn[:, b, :], in_offset=None).then_inc(put, 16)

            g.wait_ge(ld["mask"], 16)
            for b in range(NB):
                g.tensor_scalar(maskr[0:S, b, :], maskr[0:S, b, :], 40000.0, -40000.0, ALU.mult, ALU.add)\
                 .then_inc(mask_ready, 1)
            for n in range(2):
                g.wait_ge(eo_stored[n], 16 * E // 2)
            def plus(b, r, s):
                g.tensor_tensor(xres[:, b, :], xres[:, b, :], browL1[:, r, :], ALU.add).then_inc(s, 1)

            for i in range(NB + GATHER_AHEAD):
                if i < NB:
                    g.indirect_dma_start(out=xn[:, i, :], out_offset=None, in_=eo_dram,
                                         in_offset=bass.IndirectOffsetOnAxis(ap=idx_get[:, i:i + 1], axis=0))\
                     .then_inc(got_rows[i], 16)
                if i >= GATHER_AHEAD:
                    root(3, i - GATHER_AHEAD)
                if i == GATHER_AHEAD:
                    g.wait_ge(ld["at1rows"], 32)
                if GATHER_AHEAD + 2 <= i < GATHER_AHEAD + 7:
                    g.wait_ge(xn_ready, ROWS_DONE[3, i - GATHER_AHEAD - 2])
                    plus(i - GATHER_AHEAD - 2, 0, xbv_ready)

            def add_rank_one(b):
                s = b % 2
                g.wait_ge(w1_ready, b + 1)
                if b >= 2:
                    g.wait_ge(*filled_at(("F2", b - 2)))
                g.wait_ge(ld_even2[s], 16 * (b // 2 + 1))
                parts = [(m, j) for m in range(DT) for j in range(4 - POOL_J, 4)]
                for m, j in parts:
                    ins = g.tensor_scalar(w2_part(w2b[s], m, j), even2[s][:, j, :].rearrange("p (o r) -> p r o", r=4),
                                          odd[s][:, m, 4 + j:5 + j], None, ALU.mult)
                step(ins)
                for m, j in parts:
                    ins = g.tensor_tensor(w2_part(w2b[s], m, j), w2_part(w2b[s], m, j), w2_part(w2f, m, j), ALU.add)
                ins.then_inc(w2_pool_ready, 1)

            for i in range(FFN_AT + NB + 1):
                if 5 <= i < NB:
                    g.wait_ge(xn_ready, ROWS_DONE[3, i])
                    plus(i, 0, xbv_ready)
                if 0 <= i - 4 < NB:
                    root(4, i - 4)
                if 0 <= i - 5 < NB:
                    g.wait_ge(xn_ready, ROWS_DONE[4, i - 5])
                    plus(i - 5, 1, xb2_ready)
                if 0 <= i - FFN_AT - 1 < NB:
                    add_rank_one(i - FFN_AT - 1)

        @block.sync
        def _(sp):
            def wait_filled(key):
                sp.wait_ge(*filled_at(key))

            def kp_of(name, **kw):
                return A[name].rearrange("(k p) n -> p k n", p=P)

            def load_ctx(b):
                sp.dma_start(ctxT[:, :, b * S2:(b + 1) * S2],
                             A["ctxT"].rearrange("(k p) t -> p k t", p=P)[:, :, b * S2:(b + 1) * S2])\
                  .then_inc(ld_ctx[b], 16)

            def load_expert(e, parts=(0, 1)):
                n = e % RING
                if 0 in parts:
                    sp.dma_start(w1e[n], A["L0_ffn_W1"][e].rearrange("(k p) f -> p k f", p=P))\
                      .then_inc(ld_ring[n], 16)
                if 1 in parts:
                    sp.dma_start(w2e[n], A["L0_ffn_W2"][e].rearrange("(f p) o -> p f o", p=P))\
                      .then_inc(ld_ring[n], 16)

            def load_b2(e):
                sp.dma_start(b2row[e % 2][:, :], A["L0_ffn_b2"][e].partition_broadcast(S)).then_inc(ld_b2[e % 2], 16)

            for n, (b0, b1) in enumerate(((0, 2), (2, NB))):
                sp.dma_start(xres[:, b0:b1, :], A["x"].rearrange("b s d -> s b d")[:, b0:b1, :]).then_inc(ld_x[n], 16)
                if n == 0:
                    load_ctx(0)
            for b in range(1, 4):
                load_ctx(b)

            def write_k(b):
                sp.wait_ge(k_split, b + 1)
                sp.dma_start(k_dram[b].rearrange("c (m p) k -> p c m k", p=P), kp[b % 2][:, :, :, :])\
                  .then_inc(k_written[b % 2], 16)

            def write_q(c):
                sp.wait_ge(q_split, c + 1)
                sp.dma_start(q_dram.rearrange("c (m p) t -> p c m t", p=P)[:, :, :, c * QW:(c + 1) * QW],
                             qp[c % 2][:, :, :, :]).then_inc(q_written[c % 2], 16)

            def stack_k(b):
                sp.wait_ge(k_written[b % 2], 16 * (b // 2 + 1))
                if b >= 3:
                    wait_filled(("ST", b - 3, UNITS - 1))
                for j, piece in enumerate(K_PIECES):
                    sp.dma_start(kstack[b % 3][j * DK:(j + 1) * DK, :, :],
                                 k_dram[b, piece].rearrange("(h d) k -> d h k", d=DK)).then_inc(ld_kstack[b % 3], 16)

            def stack_q(c):
                sp.wait_ge(q_written[c % 2], 16 * (c // 2 + 1))
                for j, piece in enumerate(Q_PIECES):
                    sp.dma_start(qstack[j * DK:(j + 1) * DK, :, c * QW:(c + 1) * QW],
                                 q_dram[piece].rearrange("(h d) t -> d h t", d=DK)[:, :, c * QW:(c + 1) * QW])\
                      .then_inc(ld_qstack[c], 16)

            write_k(0)
            write_q(0)
            stack_k(0)
            stack_q(0)
            write_k(1)
            write_q(1)
            stack_k(1)
            stack_q(1)
            sp.dma_start(scale_t[:, :], A["L1_ffn_scale"].partition_broadcast(P)).then_inc(ld["scale"], 16)
            for i in range(-1, NB):
                if 3 <= i + 2 < NB:
                    stack_k(i + 2)
                if FIRST_Q <= i + 2 < QCHUNKS:
                    stack_q(i + 2)
                if i == 1:
                    sp.wait_ge(ones_ready, 2)
                    sp.dma_start(xg_dram[0:T].rearrange("(e c) d -> c e d", e=E),
                                 eo[0][:, :].unsqueeze(1).broadcast_to([S, E, D])).then_inc(zeroed, 16)
                elif i == 3:
                    sp.wait_ge(*filled_at(("Q", QCHUNKS - 1, DT - 1)))
                    sp.dma_start(wv_at1, kp_of("L1_xattn_Wv")).then_inc(ld_wv_at1, 16)
                    for b in range(2):
                        load_b2(b)
                    for r, name in enumerate(("L1_xattn_bv", "L1_ffn_b2")):
                        sp.dma_start(browL1[:, r, :], A[name].partition_broadcast(S)).then_inc(ld["at1rows"], 16)
                if 2 <= i < 6:
                    load_expert((i - 2) // 2, [(i - 2) % 2])
                elif i == 6:
                    for n in range(2):
                        sp.wait_ge(k_written[n], 16 * NB // 2)
                    load_expert(2)
                elif i == 7:
                    load_expert(3)
                if i + 1 < NB:
                    sp.wait_ge(*drained_at(("NM", i + 1)))
                    for piece in range(2):
                        sp.dma_start(qstack[96 + piece:97 + piece, :, (i + 1) * S:(i + 2) * S],
                                     mT[piece * H:(piece + 1) * H, :]).then_inc(max_placed, 16)
                if POOL_K <= i + 3 < NB:
                    write_k(i + 3)
                if i == -1:
                    stack_k(2)
                if FIRST_Q <= i + 3 < QCHUNKS:
                    write_q(i + 3)
                if i == -1:
                    for b in range(4, NB):
                        load_ctx(b)

            wait_filled(("ST", NB - 1, UNITS - 1))
            for r, name in enumerate(("L1_xattn_Wq", "L1_xattn_Wk")):
                sp.dma_start(w_at1[:, r, :, :], kp_of(name)).then_inc(ld["at1w"], 16)

            sp.wait_ge(put, 16 * NB)
            for half in range(2):
                sp.dma_start(xn[:, 4 * half:4 * half + 4, :],
                             xg_dram[0:T].rearrange("(e c) d -> c e d", e=E)[:, 4 * half:4 * half + 4, :])\
                  .then_inc(xe_loaded[half], 16)
            sp.dma_start(w1f, A["L1_ffn_W1"].rearrange("(k p) f -> p k f", p=P)).then_inc(ld["ffnw"], 16)
            sp.dma_start(w2f, A["L1_ffn_W2"].rearrange("(f p) o -> p f o", p=P)).then_inc(ld["ffnw"], 16)
            for e in range(E):
                wait_filled(("DN", e))
                if e + RING < E:
                    load_expert(e + RING)
                if e == E - RING:
                    sp.dma_start(maskr[0:S, :, :].rearrange("p b k -> p (b k)"),
                                 A["mask"].partition_broadcast(S)).then_inc(ld["mask"], 16)
                sp.wait_ge(*drained_at(("DN", e)))
                if e + 2 < E:
                    load_b2(e + 2)
                sp.dma_start(eo_dram[e * CAP:(e + 1) * CAP, :], eo[e % 2][:, :]).then_inc(eo_stored[e % 2], 16)

            def spread_even_rows(b):
                s = b % 2
                sp.wait_ge(xn_ready, ROWS_DONE[4, b])
                sp.dma_start(even_dram[b].rearrange("w j d -> (w j) d"), xn[1:17:2, b, :]).then_inc(even_written[s], 16)
                sp.wait_ge(even_written[s], 16 * (b // 2 + 1))
                if b >= 2:
                    sp.wait_ge(w1_ready, b - 1)
                sp.dma_start(even1[s].rearrange("p j d -> p (j d)"),
                             even_dram[b, 0].rearrange("j d -> (j d)").partition_broadcast(P)).then_inc(ld_even1[s], 16)
                if b >= 2:
                    sp.wait_ge(w2_ready, b - 1)
                    sp.wait_ge(w2_pool_ready, b - 1)
                sp.dma_start(even2[s].rearrange("p j d -> p (j d)"),
                             even_dram[b, 1].rearrange("j d -> (j d)").partition_broadcast(P)).then_inc(ld_even2[s], 16)

            for b in range(NB + 4):
                if b < NB:
                    spread_even_rows(b)
                if b >= 4:
                    sp.wait_ge(*drained_at(("F2", b - 4)))
                    sp.dma_start(out[b - 4], outs[b % 2][0:S, :]).then_inc(stored[b % 2], 16)
            for n in range(2):
                sp.wait_ge(stored[n], 16 * NB // 2)


BIAS_COLUMNS = ("L0_xattn_bq", "L0_xattn_bk", "L1_xattn_bq", "L1_xattn_bk", "L0_xattn_bv")

_INS = {
    "x": lambda v: v["x"],
    "ctxT": lambda v: v["ctx_1024"].reshape(NB * S2, D).T,
    "mask": lambda v: v["mask_BxS2_ff1"].reshape(-1),
    "L0_xattn_Wq": lambda v: v["L0_xattn_Wq"].T,
    "L0_xattn_Wk": lambda v: v["L0_xattn_Wk"].T,
    "L0_xattn_Wv": lambda v: v["L0_xattn_Wv"].T,
    "L0_xattn_Wo": lambda v: v["L0_xattn_Wo"].T,
    "bias_columns": lambda v: np.stack([v[n].reshape(DT, P) for n in BIAS_COLUMNS]).transpose(2, 0, 1),
    "L0_xattn_bo": lambda v: v["L0_xattn_bo"],
    "L0_ffn_Wg": lambda v: v["L0_ffn_Wg"],
    "L0_ffn_W1": lambda v: v["L0_ffn_W1"],
    "L0_ffn_b1": lambda v: v["L0_ffn_b1"].reshape(E, FT, P).transpose(2, 0, 1),
    "L0_ffn_W2": lambda v: v["L0_ffn_W2"],
    "L0_ffn_b2": lambda v: v["L0_ffn_b2"],
    "L1_xattn_Wq": lambda v: v["L1_xattn_Wq"].T,
    "L1_xattn_Wk": lambda v: v["L1_xattn_Wk"].T,
    "L1_xattn_Wv": lambda v: v["L1_xattn_Wv"],
    "L1_xattn_bv": lambda v: v["L1_xattn_bv"],
    "L1_ffn_W1": lambda v: v["L1_ffn_W1"].T,
    "L1_ffn_b1": lambda v: v["L1_ffn_b1"].reshape(FT, P).T,
    "L1_ffn_W2": lambda v: v["L1_ffn_W2"].T,
    "L1_ffn_b2": lambda v: v["L1_ffn_b2"],
    "L1_ffn_scale": lambda v: v["L1_ffn_scale"].reshape(1),
}


def kernel(**inputs):
    import numpy as _np
    import concourse.bacc as _bacc
    from concourse import mybir as _mybir
    from concourse.bass_utils import run_bass_kernel_spmd as _run

    given = {n: _np.asarray(a) for n, a in inputs.items()}
    nc = _bacc.Bacc("TRN2", target_bir_lowering=False, num_devices=1)
    arrays, aps = {}, {}
    for name, lay in _INS.items():
        a = _np.ascontiguousarray(lay(given))
        arrays[f"in_{name}"] = a
        aps[name] = nc.dram_tensor(f"in_{name}", a.shape, _mybir.dt.from_np(a.dtype), kind="ExternalInput").ap()
    aps["out"] = nc.dram_tensor("out_dram", (NB, S, D), _mybir.dt.float32, kind="ExternalOutput").ap()
    build(nc, aps)
    r = _run(nc, [arrays], core_ids=[0])
    return r.results[0]["out_dram"]
```
